# Optimizing a Trainium2 kernel written in Bass

```python
import numpy as np
import jax
import jax.numpy as jnp

def _softmax(x, axis=-1):
    return jax.nn.softmax(x, axis=axis)

def _gelu(x):
    return jax.nn.gelu(x, approximate=True)

def _silu(x):
    return jax.nn.silu(x)

def _sigmoid(x):
    return jax.nn.sigmoid(x)

def _layernorm(x, axis=-1, eps=1e-05):
    m = jnp.mean(x, axis=axis, keepdims=True)
    v = jnp.var(x, axis=axis, keepdims=True)
    return (x - m) / jnp.sqrt(v + eps)

def _scatter_add(tgt, idx, src, axis=0):
    return tgt.at[idx].add(src)

def _segment_sum(src, seg, n):
    return jax.ops.segment_sum(src, seg, n)
kernel_name = 'mk_xattn_ffn_d2_seqx_r4_3b4068'

def setup_inputs(seed: int=0):
    np.random.seed(seed)
    _w = jnp.asarray

    def _rec_inputs():
        import jax
        import jax.numpy as jnp
        _rk = jax.random.key(seed)
        x = 4.136e-05 + 0.9999 * jax.random.normal(jax.random.fold_in(_rk, 1), (4, 512, 512), jnp.float32)
        _lenS = 512 - jax.random.randint(jax.random.fold_in(_rk, 7), (4,), 0, max(1, 512 // 4) + 1, jnp.int32)
        _lenS2 = 512 - jax.random.randint(jax.random.fold_in(_rk, 8), (4,), 0, max(1, 512 // 4) + 1, jnp.int32)
        _ctx_1024P = jax.random.normal(jax.random.fold_in(_rk, 11), (4, 16, 256), jnp.float32)
        _ctx_1024c = jax.random.dirichlet(jax.random.fold_in(_rk, 511), 0.3 * jnp.ones((16,), jnp.float32), (4, 512))
        _ctx_1024t = jnp.einsum('bsk,bkd->bsd', _ctx_1024c, _ctx_1024P)
        _ctx_1024t = _ctx_1024t * jax.lax.rsqrt(jnp.mean(jnp.square(_ctx_1024t)) + 1e-12) * 0.953939
        ctx_1024 = -0.000292821 + 1.00034 * (_ctx_1024t + 0.3 * jax.random.normal(jax.random.fold_in(_rk, 611), (4, 512, 256), jnp.float32))
        fside_BxSx2_0 = jax.random.uniform(jax.random.fold_in(_rk, 12), (4, 512, 2), jnp.float32, 0.0, 0.999707)
        return (x, ctx_1024, fside_BxSx2_0)
    x, ctx_1024, fside_BxSx2_0 = _rec_inputs()

    def _L0_xattn_setup():
        import jax, jax.numpy as jnp
        import numpy as np
        import math
        B, L, DM = (2, 512, 256)
        DS, DC, EXP = (16, 4, 2)
        DI = EXP * DM
        DR = math.ceil(DM / 16)
        DT_MIN, DT_MAX, DT_FLOOR = (0.001, 0.1, 0.0001)

        def _ssm_forward(hidden_states, z, in_proj_w, conv_w, conv_b, x_proj_w, dt_proj_w, dt_proj_b, A_log, D):
            b = hidden_states.shape[0]
            x = jnp.einsum('ed,bld->bel', in_proj_w, hidden_states)
            xp = jnp.pad(x, ((0, 0), (0, 0), (DC - 1, 0)))
            xc = jax.lax.conv_general_dilated(xp, conv_w[:, None, :], window_strides=(1,), padding='VALID', dimension_numbers=('NCH', 'OIH', 'NCH'), feature_group_count=DI)
            u = jax.nn.silu(xc + conv_b[None, :, None])
            x_dbl = jnp.einsum('ke,bel->bkl', x_proj_w, u)
            dt_lo = x_dbl[:, :DR]
            Bm = x_dbl[:, DR:DR + DS]
            Cm = x_dbl[:, DR + DS:]
            delta = jax.nn.softplus(jnp.einsum('er,brl->bel', dt_proj_w, dt_lo) + dt_proj_b[None, :, None])
            A = -jnp.exp(A_log)

            def step(state, xs):
                d_t, B_t, C_t, u_t = xs
                dA = jnp.exp(d_t[..., None] * A)
                state = state * dA + (d_t * u_t)[..., None] * B_t[:, None, :]
                y_t = jnp.einsum('ben,bn->be', state, C_t)
                return (state, y_t)
            xs = (jnp.moveaxis(delta, -1, 0), jnp.moveaxis(Bm, -1, 0), jnp.moveaxis(Cm, -1, 0), jnp.moveaxis(u, -1, 0))
            state0 = jnp.zeros((b, DI, DS), delta.dtype)
            _, ys = jax.lax.scan(step, state0, xs)
            y = jnp.moveaxis(ys, 0, -1)
            y = y + D[None, :, None] * u
            y = y * jax.nn.silu(z)
            return jnp.swapaxes(y, 1, 2)
        key = jax.random.key(seed)
        ks = jax.random.split(key, 8)
        hidden_states = jax.random.normal(ks[0], (B, L, DM), jnp.float32)
        z = jax.random.normal(ks[1], (B, DI, L), jnp.float32)
        in_proj_w = jax.random.normal(ks[2], (DI, DM), jnp.float32) * DM ** (-0.5)
        conv_w = jax.random.normal(ks[3], (DI, DC), jnp.float32) * DC ** (-0.5)
        conv_b = jnp.zeros((DI,), jnp.float32)
        x_proj_w = jax.random.normal(ks[4], (DR + 2 * DS, DI), jnp.float32) * DI ** (-0.5)
        dt_std = DR ** (-0.5)
        dt_proj_w = jax.random.uniform(ks[5], (DI, DR), jnp.float32, -dt_std, dt_std)
        dt = jnp.exp(jax.random.uniform(ks[6], (DI,), jnp.float32) * (math.log(DT_MAX) - math.log(DT_MIN)) + math.log(DT_MIN))
        dt = jnp.clip(dt, DT_FLOOR)
        dt_proj_b = dt + jnp.log(-jnp.expm1(-dt))
        A_log = jnp.log(jnp.broadcast_to(jnp.arange(1, DS + 1, dtype=jnp.float32), (DI, DS)))
        D = jnp.ones((DI,), jnp.float32)
        return dict(hidden_states=hidden_states, z=z, in_proj_w=in_proj_w, conv_w=conv_w, conv_b=conv_b, x_proj_w=x_proj_w, dt_proj_w=dt_proj_w, dt_proj_b=dt_proj_b, A_log=A_log, D=D)
    _L0_xattn_all = _L0_xattn_setup()
    _L0_xattn_in = {k: v for k, v in _L0_xattn_all.items() if k in ('in_proj_w', 'conv_w', 'conv_b', 'x_proj_w', 'dt_proj_w', 'dt_proj_b', 'A_log', 'D')}
    del _L0_xattn_all

    def _L0_ffn_setup():
        import jax, jax.numpy as jnp
        import numpy as np
        B, S, D_IN, D_OUT, E = (4, 256, 512, 512, 32)
        MASK_DENSITY = 0.3
        THRESH = 0.5
        key = jax.random.key(seed)
        k_x, k_w, k_m, k_r = jax.random.split(key, 4)
        x = jax.random.normal(k_x, (B, S, D_IN), dtype=jnp.float32)
        bound = np.sqrt(1.0 / D_IN) * np.sqrt(3.0)
        weight = jax.random.uniform(k_w, (D_OUT, D_IN), minval=-bound, maxval=bound, dtype=jnp.float32)
        scale = jnp.ones((D_OUT,), dtype=jnp.float32)
        expert_masks = (jax.random.uniform(k_m, (E, D_OUT, D_IN)) < MASK_DENSITY).astype(jnp.float32)
        router_w = 0.01 * jax.random.normal(k_r, (E, D_IN), dtype=jnp.float32)
        return {'x': x, 'weight': weight, 'scale': scale, 'expert_masks': expert_masks, 'router_w': router_w}
    _L0_ffn_all = _L0_ffn_setup()
    _L0_ffn_in = {k: v for k, v in _L0_ffn_all.items() if k in ('weight', 'scale', 'expert_masks', 'router_w')}
    del _L0_ffn_all

    def _L1_xattn_setup():
        import jax, jax.numpy as jnp
        import numpy as np
        DIM = 512
        CTX_DIM = 256
        N_HEADS = 32
        HEAD_DIM = DIM // N_HEADS
        POS_DIM = 2
        B, N, CTXN = (2, 512, 512)
        ROPE_BASE = 10000.0

        def apply_axial_rope(x, pos):
            b, n, h, d = x.shape
            p = pos.shape[-1]
            dpa = d // p
            half = dpa // 2
            freqs = ROPE_BASE ** (-jnp.arange(half, dtype=x.dtype) / half)
            ang = pos[..., :, None] * freqs
            cos = jnp.cos(ang)[:, :, None, :, :]
            sin = jnp.sin(ang)[:, :, None, :, :]
            xr = x.reshape(b, n, h, p, half, 2)
            x1, x2 = (xr[..., 0], xr[..., 1])
            out = jnp.stack([x1 * cos - x2 * sin, x1 * sin + x2 * cos], axis=-1)
            return out.reshape(b, n, h, d)
        key = jax.random.key(seed)
        ks = jax.random.split(key, 8)
        x = jax.random.normal(ks[0], (B, N, DIM), jnp.float32)
        ctx = jax.random.normal(ks[1], (B, CTXN, CTX_DIM), jnp.float32)
        pos_map = jax.random.uniform(ks[2], (B, N, POS_DIM), jnp.float32)
        ctx_pos_map = jax.random.uniform(ks[3], (B, CTXN, POS_DIM), jnp.float32)
        Wq = jax.random.normal(ks[4], (DIM, DIM), jnp.float32) / np.sqrt(DIM)
        Wkv = jax.random.normal(ks[5], (CTX_DIM, 2 * DIM), jnp.float32) / np.sqrt(CTX_DIM)
        Wout = jax.random.normal(ks[6], (DIM, DIM), jnp.float32) / np.sqrt(DIM)
        bout = jnp.zeros((DIM,), jnp.float32)
        return {'x': x, 'ctx': ctx, 'pos_map': pos_map, 'ctx_pos_map': ctx_pos_map, 'Wq': Wq, 'Wkv': Wkv, 'Wout': Wout, 'bout': bout}
    _L1_xattn_all = _L1_xattn_setup()
    _L1_xattn_in = {k: v for k, v in _L1_xattn_all.items() if k in ('Wq', 'Wkv', 'Wout', 'bout')}
    del _L1_xattn_all

    def _L1_ffn_setup():
        import jax, jax.numpy as jnp
        import numpy as np
        _FP4_LUT = jnp.array([0.0, 0.5, 1.0, 1.5, 2.0, 3.0, 4.0, 6.0, -0.0, -0.5, -1.0, -1.5, -2.0, -3.0, -4.0, -6.0], dtype=jnp.float32)
        GROUP_SIZE = 128
        EPS = 1e-06

        def _dequant_fp4(packed_i32, scales_f16, group_size):
            out_f, in_p = packed_i32.shape
            w = packed_i32.astype(jnp.uint32)
            shifts = jnp.arange(8, dtype=jnp.uint32) * 4
            nib = w[:, :, None] >> shifts & jnp.uint32(15)
            vals = _FP4_LUT[nib.astype(jnp.int32)].reshape(out_f, in_p * 8)
            s = scales_f16.astype(jnp.float32).T
            s_full = jnp.repeat(s, group_size, axis=1)
            return vals * s_full
        key = jax.random.key(seed)
        k1, k2, k3, k4, k5 = jax.random.split(key, 5)
        B, S, H, I = (4, 512, 512, 1408)
        x = jax.random.normal(k1, (B, S, H), dtype=jnp.float32)
        gate_up_packed = jax.random.randint(k2, (2 * I, H // 8), 0, 2147483647, dtype=jnp.int32)
        gate_up_scales = jax.random.uniform(k3, (H // GROUP_SIZE, 2 * I), dtype=jnp.float32).astype(jnp.float16)
        down_packed = jax.random.randint(k4, (H, I // 8), 0, 2147483647, dtype=jnp.int32)
        down_scales = jax.random.uniform(k5, (I // GROUP_SIZE, H), dtype=jnp.float32).astype(jnp.float16)
        return {'x': x, 'gate_up_packed': gate_up_packed, 'gate_up_scales': gate_up_scales, 'down_packed': down_packed, 'down_scales': down_scales}
    _L1_ffn_all = _L1_ffn_setup()
    _L1_ffn_in = {k: v for k, v in _L1_ffn_all.items() if k in ('gate_up_packed', 'gate_up_scales', 'down_packed', 'down_scales')}
    del _L1_ffn_all
    return {'x': x, 'ctx_1024': ctx_1024, 'fside_BxSx2_0': fside_BxSx2_0, 'L0_xattn_in_proj_w': _L0_xattn_in['in_proj_w'], 'L0_xattn_conv_w': _L0_xattn_in['conv_w'], 'L0_xattn_conv_b': _L0_xattn_in['conv_b'], 'L0_xattn_x_proj_w': _L0_xattn_in['x_proj_w'], 'L0_xattn_dt_proj_w': _L0_xattn_in['dt_proj_w'], 'L0_xattn_dt_proj_b': _L0_xattn_in['dt_proj_b'], 'L0_xattn_A_log': _L0_xattn_in['A_log'], 'L0_xattn_D': _L0_xattn_in['D'], 'L0_ffn_weight': _L0_ffn_in['weight'], 'L0_ffn_scale': _L0_ffn_in['scale'], 'L0_ffn_expert_masks': _L0_ffn_in['expert_masks'], 'L0_ffn_router_w': _L0_ffn_in['router_w'], 'L1_xattn_Wq': _L1_xattn_in['Wq'], 'L1_xattn_Wkv': _L1_xattn_in['Wkv'], 'L1_xattn_Wout': _L1_xattn_in['Wout'], 'L1_xattn_bout': _L1_xattn_in['bout'], 'L1_ffn_gate_up_packed': _L1_ffn_in['gate_up_packed'], 'L1_ffn_gate_up_scales': _L1_ffn_in['gate_up_scales'], 'L1_ffn_down_packed': _L1_ffn_in['down_packed'], 'L1_ffn_down_scales': _L1_ffn_in['down_scales']}

def reference(x, ctx_1024, fside_BxSx2_0, L0_xattn_in_proj_w, L0_xattn_conv_w, L0_xattn_conv_b, L0_xattn_x_proj_w, L0_xattn_dt_proj_w, L0_xattn_dt_proj_b, L0_xattn_A_log, L0_xattn_D, L0_ffn_weight, L0_ffn_scale, L0_ffn_expert_masks, L0_ffn_router_w, L1_xattn_Wq, L1_xattn_Wkv, L1_xattn_Wout, L1_xattn_bout, L1_ffn_gate_up_packed, L1_ffn_gate_up_scales, L1_ffn_down_packed, L1_ffn_down_scales):
    import jax
    import jax.numpy as jnp

    def _L0_xattn_ref(hidden_states, z, in_proj_w, conv_w, conv_b, x_proj_w, dt_proj_w, dt_proj_b, A_log, D):
        import jax, jax.numpy as jnp
        import numpy as np
        import math
        B, L, DM = (2, 512, 256)
        DS, DC, EXP = (16, 4, 2)
        DI = EXP * DM
        DR = math.ceil(DM / 16)
        DT_MIN, DT_MAX, DT_FLOOR = (0.001, 0.1, 0.0001)

        def _ssm_forward(hidden_states, z, in_proj_w, conv_w, conv_b, x_proj_w, dt_proj_w, dt_proj_b, A_log, D):
            b = hidden_states.shape[0]
            x = jnp.einsum('ed,bld->bel', in_proj_w, hidden_states)
            xp = jnp.pad(x, ((0, 0), (0, 0), (DC - 1, 0)))
            xc = jax.lax.conv_general_dilated(xp, conv_w[:, None, :], window_strides=(1,), padding='VALID', dimension_numbers=('NCH', 'OIH', 'NCH'), feature_group_count=DI)
            u = jax.nn.silu(xc + conv_b[None, :, None])
            x_dbl = jnp.einsum('ke,bel->bkl', x_proj_w, u)
            dt_lo = x_dbl[:, :DR]
            Bm = x_dbl[:, DR:DR + DS]
            Cm = x_dbl[:, DR + DS:]
            delta = jax.nn.softplus(jnp.einsum('er,brl->bel', dt_proj_w, dt_lo) + dt_proj_b[None, :, None])
            A = -jnp.exp(A_log)

            def step(state, xs):
                d_t, B_t, C_t, u_t = xs
                dA = jnp.exp(d_t[..., None] * A)
                state = state * dA + (d_t * u_t)[..., None] * B_t[:, None, :]
                y_t = jnp.einsum('ben,bn->be', state, C_t)
                return (state, y_t)
            xs = (jnp.moveaxis(delta, -1, 0), jnp.moveaxis(Bm, -1, 0), jnp.moveaxis(Cm, -1, 0), jnp.moveaxis(u, -1, 0))
            state0 = jnp.zeros((b, DI, DS), delta.dtype)
            _, ys = jax.lax.scan(step, state0, xs)
            y = jnp.moveaxis(ys, 0, -1)
            y = y + D[None, :, None] * u
            y = y * jax.nn.silu(z)
            return jnp.swapaxes(y, 1, 2)
        return _ssm_forward(hidden_states, z, in_proj_w, conv_w, conv_b, x_proj_w, dt_proj_w, dt_proj_b, A_log, D)

    def _L0_ffn_ref(x, weight, scale, expert_masks, router_w):
        import jax, jax.numpy as jnp
        import numpy as np
        B, S, D_IN, D_OUT, E = (4, 256, 512, 512, 32)
        MASK_DENSITY = 0.3
        THRESH = 0.5
        logits = jnp.einsum('bsd,ed->bse', x, router_w)
        probs = jax.nn.softmax(logits, axis=-1)
        top1_w = jnp.max(probs, axis=-1)
        top1_idx = jnp.argmax(probs, axis=-1)
        w_q = jnp.clip(jnp.round(weight / THRESH), -1.0, 1.0)
        w_scaled = w_q * scale[:, None]
        out0 = jnp.zeros((x.shape[0], x.shape[1], weight.shape[0]), dtype=x.dtype)

        def body(out, inputs):
            e_idx, mask_e = inputs
            y = jnp.einsum('bsi,oi->bso', x, w_scaled * mask_e)
            sel = (top1_idx == e_idx)[..., None]
            out = jnp.where(sel, y * top1_w[..., None], out)
            return (out, None)
        out, _ = jax.lax.scan(body, out0, (jnp.arange(E), expert_masks))
        return out

    def _L1_xattn_ref(x, ctx, pos_map, ctx_pos_map, Wq, Wkv, Wout, bout):
        import jax, jax.numpy as jnp
        import numpy as np
        DIM = 512
        CTX_DIM = 256
        N_HEADS = 32
        HEAD_DIM = DIM // N_HEADS
        POS_DIM = 2
        B, N, CTXN = (2, 512, 512)
        ROPE_BASE = 10000.0

        def apply_axial_rope(x, pos):
            b, n, h, d = x.shape
            p = pos.shape[-1]
            dpa = d // p
            half = dpa // 2
            freqs = ROPE_BASE ** (-jnp.arange(half, dtype=x.dtype) / half)
            ang = pos[..., :, None] * freqs
            cos = jnp.cos(ang)[:, :, None, :, :]
            sin = jnp.sin(ang)[:, :, None, :, :]
            xr = x.reshape(b, n, h, p, half, 2)
            x1, x2 = (xr[..., 0], xr[..., 1])
            out = jnp.stack([x1 * cos - x2 * sin, x1 * sin + x2 * cos], axis=-1)
            return out.reshape(b, n, h, d)
        b, n, _ = x.shape
        ctx_n = ctx.shape[1]
        q = (x @ Wq).reshape(b, n, N_HEADS, HEAD_DIM)
        k, v = jnp.split(ctx @ Wkv, 2, axis=-1)
        k = k.reshape(b, ctx_n, N_HEADS, HEAD_DIM)
        v = v.reshape(b, ctx_n, N_HEADS, HEAD_DIM)
        q = apply_axial_rope(q, pos_map)
        k = apply_axial_rope(k, ctx_pos_map)
        scale = 1.0 / np.sqrt(HEAD_DIM).astype(np.float32)
        logits = jnp.einsum('bqhd,bkhd->bhqk', q, k) * scale
        w = jax.nn.softmax(logits, axis=-1)
        attn = jnp.einsum('bhqk,bkhd->bqhd', w, v)
        attn = attn.reshape(b, n, N_HEADS * HEAD_DIM)
        return attn @ Wout + bout

    def _L1_ffn_ref(x, gate_up_packed, gate_up_scales, down_packed, down_scales):
        import jax, jax.numpy as jnp
        import numpy as np
        _FP4_LUT = jnp.array([0.0, 0.5, 1.0, 1.5, 2.0, 3.0, 4.0, 6.0, -0.0, -0.5, -1.0, -1.5, -2.0, -3.0, -4.0, -6.0], dtype=jnp.float32)
        GROUP_SIZE = 128
        EPS = 1e-06

        def _dequant_fp4(packed_i32, scales_f16, group_size):
            out_f, in_p = packed_i32.shape
            w = packed_i32.astype(jnp.uint32)
            shifts = jnp.arange(8, dtype=jnp.uint32) * 4
            nib = w[:, :, None] >> shifts & jnp.uint32(15)
            vals = _FP4_LUT[nib.astype(jnp.int32)].reshape(out_f, in_p * 8)
            s = scales_f16.astype(jnp.float32).T
            s_full = jnp.repeat(s, group_size, axis=1)
            return vals * s_full
        I = gate_up_packed.shape[0] // 2
        w_gu = _dequant_fp4(gate_up_packed, gate_up_scales, GROUP_SIZE)
        w_down = _dequant_fp4(down_packed, down_scales, GROUP_SIZE)
        gate_up = jnp.einsum('bsh,oh->bso', x, w_gu)
        gate, up = (gate_up[..., :I], gate_up[..., I:])
        h = jax.nn.silu(gate) * up
        y = jnp.einsum('bsi,hi->bsh', h, w_down)
        rms = jnp.sqrt(jnp.mean(y * y, axis=-1, keepdims=True) + EPS)
        return y / rms
    x = x + _L0_xattn_ref(ctx_1024, _layernorm(x, axis=-1), L0_xattn_in_proj_w, L0_xattn_conv_w, L0_xattn_conv_b, L0_xattn_x_proj_w, L0_xattn_dt_proj_w, L0_xattn_dt_proj_b, L0_xattn_A_log, L0_xattn_D)
    x = x + _L0_ffn_ref(_layernorm(x, axis=-1), L0_ffn_weight, L0_ffn_scale, L0_ffn_expert_masks, L0_ffn_router_w)
    x = x + _L1_xattn_ref(_layernorm(x, axis=-1), ctx_1024, fside_BxSx2_0, fside_BxSx2_0, L1_xattn_Wq, L1_xattn_Wkv, L1_xattn_Wout, L1_xattn_bout)
    x = x + _L1_ffn_ref(_layernorm(x, axis=-1), L1_ffn_gate_up_packed, L1_ffn_gate_up_scales, L1_ffn_down_packed, L1_ffn_down_scales)
    return x

_drawn_inputs = setup_inputs


def setup_inputs(seed=0):
    import zlib

    import numpy as np

    out = dict(_drawn_inputs(seed))
    spreads = {'L0_xattn_conv_b': (0.0, 0.1),
     'L0_xattn_D': (1.0, 0.2),
     'L0_ffn_scale': (1.0, 0.2),
     'L1_xattn_bout': (0.0, 0.1)}
    factors = {'L0_xattn_dt_proj_w': 4.856}
    for name, (base, spread) in spreads.items():
        noise = np.random.default_rng([zlib.crc32(name.encode()), seed]).standard_normal(out[name].shape)
        drawn = base * np.exp(spread * noise) if base else spread * noise
        out[name] = jnp.asarray(drawn.astype(out[name].dtype))
    for name, factor in factors.items():
        out[name] = (out[name] * factor).astype(out[name].dtype)
    return out
```

```python
import math
from contextlib import ExitStack

import concourse.bass as bass
from concourse import mybir

F32 = mybir.dt.float32
F16 = mybir.dt.float16
I32 = mybir.dt.int32
U32 = mybir.dt.uint32
ALU = mybir.AluOpType
ACT = mybir.ActivationFunctionType
AX = mybir.AxisListType

P = 128
B, S, D = 4, 512, 512
NT = S // P
TILES = B * NT
DT = D // P
LN_EPS = 1e-5


class Tally:

    def __init__(self, eng, sem):
        self.eng, self.sem, self.n = eng, sem, 0

    def mark(self, ins):
        ins.then_inc(self.sem, 1)
        self.n += 1
        return self.n

    def wait(self, n=None):
        self.eng.wait_ge(self.sem, self.n if n is None else n)

    def link(self, ins):
        self.mark(ins)
        self.wait()


class Space:

    def __init__(self, nc, ctx, tag):
        self.nc, self.ctx, self.tag, self.sems = nc, ctx, tag, []

    def sb(self, name, shape, dt=F32):
        return self.ctx.enter_context(self.nc.sbuf_tensor(f"{self.tag}_{name}", shape, dt))

    def ps(self, name, shape, dt=F32):
        return self.ctx.enter_context(self.nc.psum_tensor(f"{self.tag}_{name}", shape, dt))

    def sem(self, name):
        s = self.ctx.enter_context(self.nc.semaphore(f"{self.tag}_{name}"))
        self.sems.append(s)
        return s

    def clear(self):
        for s in self.sems:
            self.nc.sync.sem_clear(s)
        self.nc.all_engine_barrier()


def layernorm_stats(nc, dve, chain, x_tiles, stats, mv):
    for t, x in enumerate(x_tiles):
        chain.mark(nc.vector.bn_stats(stats[:, t, :], x))
    chain.wait()
    for t in range(len(x_tiles)):
        chain.mark(nc.vector.bn_aggr(mv[:, t, :], stats[:, t, :]))
    chain.wait()


def stage_ssm(nc, X, ident, scratch, ins):
    DC, CK = 4, 2
    DR, DS = 16, 16
    RING = 4
    with ExitStack() as ctx:
        sp_ = Space(nc, ctx, "ssm")
        sb, ps, sem = sp_.sb, sp_.ps, sp_.sem
        ctxT = sb("ctxT", [P, B, CK, S])
        w_in = sb("w_in", [P, CK, D])
        w_xp = sb("w_xp", [P, DT, DR + 2 * DS])
        w_dt = sb("w_dt", [DR, D])
        par = sb("par", [P, DT, DC + 3])
        negA = sb("negA", [P, DT, DS])
        acc = sb("acc", [P, DT, S])
        u = sb("u", [P, DT, S])
        tpre = sb("tpre", [P, DT, S])
        delta = sb("delta", [P, DT, S])
        zs = sb("zs", [P, NT, S])
        xdbl = sb("xdbl", [DR + 2 * DS, S])
        BC = sb("BC", [P, RING, 2, S])
        dBu = sb("dBu", [P, 3, S])
        hC = sb("hC", [P, 3, S])
        yo = sb("yo", [P, 2, S])
        stats = sb("stats", [P, NT, 6])
        mv = sb("mv", [P, NT, 2])
        rstd = sb("rstd", [P, NT, 1])
        psY = ps("psY", [P, DT, S])
        psA = ps("psA", [P, 2, S])
        psH = ps("psH", [P, 2, S])

        loaded = sem("loaded")
        prep = sem("prep")
        with nc.Block() as block:
            @block.sync
            def _(sp):
                sp.dma_start(X[:], ins["x"].rearrange("b (t p) d -> p (b t) d", p=P)).then_inc(loaded, 16)
                for b in range(B):
                    sp.dma_start(ctxT[:, b], ins["ctxT"][b].rearrange("(c p) s -> p c s", p=P)).then_inc(loaded, 16)

            @block.scalar
            def _(act):
                act.dma_start(w_in[:], ins["in_proj_wT"].rearrange("(c p) e -> p c e", p=P)).then_inc(loaded, 16)
                act.dma_start(w_xp[:], ins["x_proj_wT"].rearrange("(c p) k -> p c k", p=P)).then_inc(loaded, 16)
                act.dma_start(w_dt[:], ins["dt_proj_wT"]).then_inc(loaded, 16)
                act.dma_start(par[:], ins["channels"].rearrange("(c p) k -> p c k", p=P)).then_inc(loaded, 16)
                act.dma_start(negA[:], ins["A_log"].rearrange("(c p) n -> p c n", p=P)).then_inc(loaded, 16)
                act.wait_ge(loaded, 16 * 10)
                nc.scalar.activation(negA[:], negA[:], ACT.Exp).then_inc(prep, 1)

            @block.vector
            def _(dve):
                dve.wait_ge(prep, 1)
                nc.vector.tensor_scalar(negA[:], negA[:], -1.0, None, ALU.mult).then_inc(prep, 1)
                dve.wait_ge(loaded, 16 * 10)

        sp_.clear()
        inproj, u_done, xdbl_ps, xdbl_sb, dtp = (sem(n) for n in ("inproj", "u_done", "xdbl_ps", "xdbl_sb", "dtp"))
        conv_done, t_done, e_done, l_done, r_done, z_done = (sem(n) for n in ("conv_done", "t_done", "e_done", "l_done", "r_done", "z_done"))
        mv_done, du_done, bc_out, dA_done, dBu_done, hC_done = (sem(n) for n in ("mv_done", "du_done", "bc_out", "dA_done", "dBu_done", "hC_done"))
        bc_in = [sem(f"bc_in{i}") for i in range(RING)]
        h_done, summed, y_done, turned, own, own_act = (sem(n) for n in ("h_done", "summed", "y_done", "turned", "own", "own_act"))
        zcol = sem("zcol")
        UNITS = DS * DT
        X4 = X[:].rearrange("p (b t) d -> p b t d", t=NT)
        with nc.Fori(0, B) as b:
            with nc.Block() as block:
                @block.sync
                def _(sp):
                    sp.wait_ge(xdbl_sb, 1)
                    sp.dma_start(scratch[b], xdbl[DR:, :]).then_inc(bc_out, 16)
                    sp.wait_ge(bc_out, 16)
                    for n in range(DS):
                        if n >= RING:
                            sp.wait_ge(hC_done, DT * (n - RING + 1))
                        sp.dma_start(BC[:, n % RING], bcast_rows(scratch[b], n)).then_inc(bc_in[n % RING], 16)

                @block.tensor
                def _(pe):
                    for e in range(DT):
                        for c in range(CK):
                            mm = nc.tensor.matmul(psY[:, e, :], w_in[:, c, e * P:(e + 1) * P], ctxT[:, b, c, :],
                                                  start=(c == 0), stop=(c == CK - 1))
                        mm.then_inc(inproj, 1)
                    for e in range(DT):
                        pe.wait_ge(u_done, e + 1)
                        mm = nc.tensor.matmul(psA[0:DR + 2 * DS, 0, :], w_xp[:, e, :], u[:, e, :],
                                              start=(e == 0), stop=(e == DT - 1))
                    mm.then_inc(xdbl_ps, 1)
                    pe.wait_ge(xdbl_sb, 1)
                    for e in range(DT):
                        nc.tensor.matmul(psY[:, e, :], w_dt[:, e * P:(e + 1) * P], xdbl[0:DR, :],
                                         start=True, stop=True).then_inc(dtp, 1)
                    pe.wait_ge(t_done, DT)
                    for i in range(UNITS):
                        n, e = divmod(i, DT)
                        pe.wait_ge(hC_done, i + 1)
                        nc.tensor.matmul(psY[:, e, :], ident[:], hC[:, i % 3, :],
                                         start=(n == 0), stop=(n == DS - 1)).then_inc(summed, 1)
                    for e in range(DT):
                        pe.wait_ge(y_done, e + 1)
                        if e >= 2:
                            pe.wait_ge(r_done, 1 + e - 1)
                        for t in range(NT):
                            mm = nc.tensor.transpose(psA[:, e % 2, t * P:(t + 1) * P], yo[:, e % 2, t * P:(t + 1) * P], ident[:])
                        mm.then_inc(turned, 1)

                @block.scalar
                def _(act):
                    for e in range(DT):
                        act.wait_ge(conv_done, e + 1)
                        nc.scalar.activation(u[:, e, :], acc[:, e, :], ACT.Silu, bias=par[:, e, DC:DC + 1]).then_inc(u_done, 1)
                    act.wait_ge(mv_done, 1)
                    nc.scalar.activation(rstd[:], mv[:, :, 1:2], ACT.Sqrt).then_inc(own_act, 1)
                    act.wait_ge(xdbl_ps, 1)
                    nc.scalar.activation(xdbl[:], psA[0:DR + 2 * DS, 0, :], ACT.Copy).then_inc(xdbl_sb, 1)
                    act.wait_ge(z_done, 1)
                    nc.scalar.activation(zs[:], zs[:], ACT.Silu).then_inc(z_done, 1)
                    act.wait_ge(t_done, DT + 1)
                    nc.scalar.activation(acc[:], acc[:], ACT.Exp, scale=-1.0).then_inc(e_done, 1)
                    act.wait_ge(e_done, 1)
                    nc.scalar.activation(acc[:], acc[:], ACT.Ln, bias=1.0).then_inc(l_done, 1)
                    act.wait_ge(zcol, 1)
                    act.wait_ge(r_done, 1)
                    for i in range(UNITS):
                        n, e = divmod(i, DT)
                        if i >= 2:
                            act.wait_ge(h_done, i - 1)
                        nc.scalar.activation(psA[:, i % 2, 1:S], delta[:, e, 1:S], ACT.Exp,
                                             scale=negA[:, e, n:n + 1]).then_inc(dA_done, 1)

                @block.gpsimd
                def _(pool):
                    pool.wait_ge(du_done, 1)
                    for i in range(UNITS):
                        n, e = divmod(i, DT)
                        if e == 0:
                            pool.wait_ge(bc_in[n % RING], 16 * (n // RING + 1))
                        if i >= 3:
                            pool.wait_ge(h_done, i - 2)
                        nc.gpsimd.tensor_tensor(dBu[:, i % 3, :], tpre[:, e, :], BC[:, n % RING, 0, :], ALU.mult).then_inc(dBu_done, 1)

                @block.vector
                def _(dve):
                    chain = Tally(dve, own)
                    layernorm_stats(nc, dve, chain, [X4[:, b, t, :] for t in range(NT)], stats, mv)
                    nc.vector.tensor_scalar(mv[:, :, 1:2], mv[:, :, 1:2], LN_EPS, None, ALU.add).then_inc(mv_done, 1)
                    for e in range(DT):
                        dve.wait_ge(inproj, e + 1)
                        chain.link(nc.vector.tensor_scalar(acc[:, e, :], psY[:, e, :], par[:, e, DC - 1:DC], None, ALU.mult))
                        for k in range(1, DC):
                            ins_ = nc.vector.scalar_tensor_tensor(out=acc[:, e, k:], in0=psY[:, e, :S - k], scalar=par[:, e, DC - 1 - k:DC - k],
                                                                  in1=acc[:, e, k:], op0=ALU.mult, op1=ALU.add)
                            if k < DC - 1:
                                chain.link(ins_)
                        ins_.then_inc(conv_done, 1)
                    dve.wait_ge(own_act, 1)
                    chain.link(nc.vector.reciprocal(rstd[:], rstd[:]))
                    for t in range(NT):
                        ins_ = nc.vector.tensor_scalar(zs[:, t, :], X4[:, b, t, :], mv[:, t, 0:1], rstd[:, t, :], ALU.subtract, ALU.mult)
                        if t < NT - 1:
                            chain.mark(ins_)
                    ins_.then_inc(z_done, 1)
                    chain.wait()
                    for e in range(DT):
                        dve.wait_ge(dtp, e + 1)
                        nc.vector.tensor_scalar(tpre[:, e, :], psY[:, e, :], par[:, e, DC + 1:DC + 2], None, ALU.add).then_inc(t_done, 1)
                    dve.wait_ge(t_done, DT)
                    dve.wait_ge(u_done, DT)
                    nc.vector.scalar_tensor_tensor(out=acc[:], in0=tpre[:], scalar=-1.0, in1=tpre[:], op0=ALU.mult, op1=ALU.max).then_inc(t_done, 1)
                    dve.wait_ge(xdbl_sb, 1)
                    nc.vector.memset(psA[:, :, 0:1], 0.0).then_inc(zcol, 1)
                    dve.wait_ge(l_done, 1)
                    nc.vector.scalar_tensor_tensor(out=delta[:], in0=tpre[:], scalar=0.0, in1=acc[:], op0=ALU.max, op1=ALU.add).then_inc(r_done, 1)
                    dve.wait_ge(r_done, 1)
                    nc.vector.tensor_tensor(tpre[:], delta[:], u[:], ALU.mult).then_inc(du_done, 1)
                    dve.wait_ge(zcol, 1)

                    def project_states(i):
                        n, e = divmod(i, DT)
                        dve.wait_ge(h_done, i + 1)
                        if i >= 3:
                            dve.wait_ge(summed, i - 2)
                        nc.vector.tensor_tensor(hC[:, i % 3, :], psH[:, i % 2, :], BC[:, n % RING, 1, :], ALU.mult).then_inc(hC_done, 1)

                    for i in range(UNITS):
                        n, e = divmod(i, DT)
                        dve.wait_ge(dA_done, i + 1)
                        dve.wait_ge(dBu_done, i + 1)
                        if e == 0:
                            dve.wait_ge(bc_in[n % RING], 16 * (n // RING + 1))
                        if i >= 2:
                            dve.wait_ge(hC_done, i - 1)
                        nc.vector.tensor_tensor_scan(psH[:, i % 2, :], psA[:, i % 2, :], dBu[:, i % 3, :], 0.0, ALU.mult, ALU.add).then_inc(h_done, 1)
                        if i >= 1:
                            project_states(i - 1)
                    project_states(UNITS - 1)
                    dve.wait_ge(z_done, 2)
                    for e in range(DT):
                        dve.wait_ge(summed, UNITS - DT + e + 1)
                        if e >= 2:
                            dve.wait_ge(turned, e - 1)
                        chain.link(nc.vector.scalar_tensor_tensor(out=yo[:, e % 2, :], in0=u[:, e, :], scalar=par[:, e, DC + 2:DC + 3],
                                                                  in1=psY[:, e, :], op0=ALU.mult, op1=ALU.add))
                        nc.vector.tensor_tensor(yo[:, e % 2, :], yo[:, e % 2, :], zs[:, e, :], ALU.mult).then_inc(y_done, 1)
                        dve.wait_ge(turned, e + 1)
                        xe = X4[:, b, :, e * P:(e + 1) * P]
                        nc.vector.tensor_tensor(xe, xe, psA[:, e % 2, :].rearrange("p (t e) -> p t e", e=P), ALU.add).then_inc(r_done, 1)
            sp_.clear()


def bcast_rows(rows, n):
    return rows.rearrange("(w n) s -> n w s", w=2)[n].partition_broadcast(P)


def make_identity(nc, tiles, sems):
    with nc.Block() as block:
        @block.gpsimd
        def _(pool):
            for tile, s in zip(tiles, sems):
                nc.gpsimd.memset(tile[:], 0.0).then_inc(s, 1)
                pool.wait_ge(s, 1)
                nc.gpsimd.affine_select(out=tile[:], in_=tile[:], compare_op=ALU.not_equal, fill=1.0, base=0,
                                        pattern=[[-1, P]], channel_multiplier=1).then_inc(s, 1)
                pool.wait_ge(s, 2)


def stage_experts(nc, X, ident, ident16, scratch, ins):
    E = 32
    STEPS = TILES + E - 1
    ROW = D + 2
    rows, results = scratch
    with ExitStack() as ctx:
        sp_ = Space(nc, ctx, "moe")
        sb, ps, sem = sp_.sb, sp_.ps, sp_.sem
        XN = sb("XN", [P, TILES, ROW])
        router = sb("router", [P, DT, E])
        tern32 = sb("tern32", [P, DT * D])
        tern = sb("tern", [P, DT * D], F16)
        negs = sb("negs", [P, DT * D], F16)
        scale = sb("scale", [P, D])
        iota_i = sb("iota_i", [P, 64], I32)
        iota = sb("iota", [P, 64])
        tile_end = sb("tile_end", [P, TILES])
        before = sb("before", [P, P], F16)
        ones = sb("ones", [P, P], F16)
        ones32 = sb("ones32", [P, E])
        OH = sb("OH", [P, TILES, E], F16)
        CUM = sb("CUM", [P, TILES + 1, E], F16)
        POS = sb("POS", [P, TILES], U32)
        Ef = sb("Ef", [P, STEPS])
        EI = sb("EI", [P, STEPS], I32)
        TI = sb("TI", [P, STEPS], I32)

        with ExitStack() as ctx2:
            r_ = Space(nc, ctx2, "route")
            xb = r_.sb("xb", [P, NT, D])
            xT = r_.sb("xT", [P, 2, DT * P])
            lg = r_.sb("lg", [P, NT, E])
            ex = r_.sb("ex", [P, NT, E])
            m8 = r_.sb("m8", [P, NT, 8])
            negm = r_.sb("negm", [P, NT])
            i8 = r_.sb("i8", [P, NT, 8], U32)
            idx = r_.sb("idx", [P, NT, 1])
            den = r_.sb("den", [P, NT, 1])
            stats = r_.sb("stats", [P, NT, 6])
            mv = r_.sb("mv", [P, NT, 2])
            rstd = r_.sb("rstd", [P, NT, 1])
            psT = r_.ps("psT", [P, 2, DT * P])
            psL = r_.ps("psL", [P, NT, E])
            loaded, consts, tern_own = r_.sem("loaded"), r_.sem("consts"), r_.sem("tern_own")
            with nc.Block() as block:
                @block.sync
                def _(sp):
                    sp.dma_start(router[:], ins["routerT"].rearrange("(c p) e -> p c e", p=P)).then_inc(loaded, 16)
                    sp.dma_start(scale[:], ins["out_scale"].partition_broadcast(P)).then_inc(loaded, 16)
                    sp.dma_start(tern32[:].rearrange("p (c o) -> p c o", c=DT),
                                 ins["ternaryT"].rearrange("(c p) o -> p c o", p=P)).then_inc(loaded, 16)

                @block.gpsimd
                def _(pool):
                    nc.gpsimd.iota(iota_i[:], [[1, 64]], base=0, channel_multiplier=0).then_inc(consts, 1)
                    nc.gpsimd.memset(ones[:], 1.0).then_inc(consts, 1)
                    nc.gpsimd.memset(ones32[:], 1.0).then_inc(consts, 1)
                    pool.wait_ge(consts, 3)
                    nc.gpsimd.tensor_copy(iota[:], iota_i[:]).then_inc(consts, 1)
                    nc.gpsimd.affine_select(out=before[:], in_=ones[:], compare_op=ALU.is_ge, fill=0.0, base=-1,
                                            pattern=[[1, P]], channel_multiplier=-1).then_inc(consts, 1)

                @block.vector
                def _(dve):
                    dve.wait_ge(consts, 5)
                    nc.vector.tensor_scalar(tile_end[:], iota[:, 0:TILES], 1.0, float(P), ALU.add, ALU.mult).then_inc(tern_own, 1)
                    dve.wait_ge(loaded, 48)
                    nc.vector.tensor_scalar(tern[:], tern32[:], 0.25, None, ALU.is_gt).then_inc(tern_own, 1)
                    nc.vector.tensor_scalar(negs[:], tern32[:], -0.25, None, ALU.is_lt).then_inc(tern_own, 1)
                    dve.wait_ge(tern_own, 3)
                    nc.vector.tensor_tensor(tern[:], tern[:], negs[:], ALU.subtract).then_inc(tern_own, 1)
            r_.clear()
            mv_done, rooted, xn_done, kept, turned, xT_done, logits = (r_.sem(n) for n in ("mv_done", "rooted", "xn_done", "kept", "turned", "xT_done", "logits"))
            top_done, summed, own = r_.sem("top_done"), r_.sem("summed"), r_.sem("own")
            X4 = X[:].rearrange("p (b t) d -> p b t d", t=NT)
            XN4 = XN[:].rearrange("p (b t) d -> p b t d", t=NT)
            OH4 = OH[:].rearrange("p (b t) e -> p b t e", t=NT)
            with nc.Fori(0, B) as b:
                with nc.Block() as block:
                    @block.vector
                    def _(dve):
                        chain = Tally(dve, own)
                        layernorm_stats(nc, dve, chain, [X4[:, b, t, :] for t in range(NT)], stats, mv)
                        nc.vector.tensor_scalar(mv[:, :, 1:2], mv[:, :, 1:2], LN_EPS, None, ALU.add).then_inc(mv_done, 1)
                        dve.wait_ge(rooted, 1)
                        chain.link(nc.vector.reciprocal(rstd[:], rstd[:]))
                        for t in range(NT):
                            nc.vector.tensor_scalar(xb[:, t, :], X4[:, b, t, :], mv[:, t, 0:1], rstd[:, t, :], ALU.subtract, ALU.mult).then_inc(xn_done, 1)
                        dve.wait_ge(logits, NT)
                        chain.link(nc.vector.tensor_copy(lg[:], psL[:]))
                        for t in range(NT):
                            chain.mark(nc.vector.max(m8[:, t, :], lg[:, t, :]))
                        chain.wait()
                        nc.vector.tensor_scalar(negm[:], m8[:, :, 0], -1.0, None, ALU.mult).then_inc(top_done, 1)
                        for t in range(NT):
                            chain.mark(nc.vector.max_index(i8[:, t, :], m8[:, t, :], lg[:, t, :]))
                        chain.wait()
                        chain.link(nc.vector.tensor_copy(idx[:], i8[:, :, 0:1]))
                        chain.mark(nc.vector.tensor_copy(XN4[:, b, :, D:D + 1], idx[:]))
                        for t in range(NT):
                            chain.mark(nc.vector.tensor_scalar(OH4[:, b, t, :], iota[:, 0:E], idx[:, t, :], None, ALU.is_equal))
                        dve.wait_ge(summed, NT)
                        chain.mark(nc.vector.reciprocal(XN4[:, b, :, D + 1:D + 2], den[:]))

                    @block.scalar
                    def _(act):
                        act.wait_ge(mv_done, 1)
                        nc.scalar.activation(rstd[:], mv[:, :, 1:2], ACT.Sqrt).then_inc(rooted, 1)
                        for t in range(NT):
                            act.wait_ge(turned, t + 1)
                            if t >= 2:
                                act.wait_ge(logits, t - 1)
                            nc.scalar.activation(xT[:, t % 2, :], psT[:, t % 2, :], ACT.Copy).then_inc(xT_done, 1)
                        act.wait_ge(top_done, 1)
                        for t in range(NT):
                            nc.scalar.activation(ex[:, t, :], lg[:, t, :], ACT.Exp, bias=negm[:, t:t + 1],
                                                 accum_out=den[:, t, :]).then_inc(summed, 1)

                    @block.gpsimd
                    def _(pool):
                        for t in range(NT):
                            pool.wait_ge(xn_done, t + 1)
                            nc.gpsimd.tensor_copy(XN4[:, b, t, 0:D], xb[:, t, :]).then_inc(kept, 1)

                    @block.tensor
                    def _(pe):
                        for t in range(NT + 1):
                            if t < NT:
                                pe.wait_ge(xn_done, t + 1)
                                if t >= 2:
                                    pe.wait_ge(xT_done, t - 1)
                                for c in range(DT):
                                    mm = nc.tensor.transpose(psT[:, t % 2, c * P:(c + 1) * P], xb[:, t, c * P:(c + 1) * P], ident[:])
                                mm.then_inc(turned, 1)
                            if t >= 1:
                                pe.wait_ge(xT_done, t)
                                for c in range(DT):
                                    mm = nc.tensor.matmul(psL[:, t - 1, :], xT[:, (t - 1) % 2, c * P:(c + 1) * P], router[:, c, :],
                                                          start=(c == 0), stop=(c == DT - 1))
                                mm.then_inc(logits, 1)
                r_.clear()

        XH = sb("XH", [P, 2, 2, D], F16)
        XST = sb("XST", [P, TILES, 2 * DT, P], F16)
        CMP = sb("CMP", [P, STEPS, E])
        incl = sb("incl", [P, E])
        excl = sb("excl", [P, E])
        rk = sb("rk", [P, E])
        place = sb("place", [P, TILES, E])
        posf = sb("posf", [P, TILES])
        GO = sb("GO", [P, TILES * E])
        oh2 = sb("oh2", [P, TILES, E])
        with ExitStack() as ctx2:
            s_ = Space(nc, ctx2, "sort")
            psR = s_.ps("psR", [P, TILES, E])
            psC = s_.ps("psC", [P, E])
            psX = s_.ps("psX", [P, 2, 2 * DT, P], F16)
            cum, ranked, own, pos_done, sent, back, hi_done, lo_done, turned, evac = (
                s_.sem(n) for n in ("cum", "ranked", "own", "pos_done", "sent", "back", "hi_done", "lo_done", "turned", "evac"))
            rowsT = rows.rearrange("(t p) d -> p t d", p=P)
            with nc.Block() as block:
                @block.vector
                def _(dve):
                    chain = Tally(dve, own)
                    nc.vector.memset(CUM[:, 0, :], 0.0).then_inc(cum, 1)
                    for t in range(TILES):
                        dve.wait_ge(cum, t + 1)
                        nc.vector.tensor_tensor(CUM[:, t + 1, :], CUM[:, t, :], OH[:, t, :], ALU.add).then_inc(cum, 1)
                    dve.wait_ge(ranked, 1)
                    chain.link(nc.vector.tensor_tensor_scan(incl[:], ones32[:], psC[:], 0.0, ALU.mult, ALU.add))
                    chain.link(nc.vector.tensor_tensor(excl[:], incl[:], psC[:], ALU.subtract))
                    chain.link(nc.vector.tensor_tensor(place[:], psR[:], excl[:].unsqueeze(1).broadcast_to([P, TILES, E]), ALU.add))
                    chain.link(nc.vector.tensor_tensor(place[:], place[:], OH[:], ALU.mult))
                    chain.link(nc.vector.tensor_reduce(posf[:], place[:], AX.X, ALU.add))
                    nc.vector.tensor_copy(POS[:], posf[:]).then_inc(pos_done, 1)
                    ends = CMP[:].rearrange("p k e -> p (k e)")[:, 0:E * TILES].rearrange("p (e t) -> p e t", t=TILES)
                    chain.link(nc.vector.tensor_tensor(ends, incl[:].unsqueeze(2).broadcast_to([P, E, TILES]),
                                                       tile_end[:].unsqueeze(1).broadcast_to([P, E, TILES]), ALU.is_gt))
                    chain.link(nc.vector.tensor_reduce(rk[:], ends, AX.X, ALU.add))
                    chain.link(nc.vector.tensor_tensor(rk[:], rk[:], iota[:, 0:E], ALU.add))
                    chain.link(nc.vector.tensor_tensor(CMP[:], rk[:].unsqueeze(1).broadcast_to([P, STEPS, E]),
                                                       iota[:, 0:STEPS].unsqueeze(2).broadcast_to([P, STEPS, E]), ALU.is_lt))
                    chain.link(nc.vector.tensor_reduce(Ef[:], CMP[:], AX.X, ALU.add))
                    chain.mark(nc.vector.tensor_copy(EI[:], Ef[:]))
                    chain.mark(nc.vector.tensor_tensor(TI[:], iota[:, 0:STEPS], Ef[:], ALU.subtract))
                    for t in range(TILES):
                        dve.wait_ge(hi_done, t + 1)
                        nc.vector.tensor_tensor(XH[:, t % 2, 1, :], XN[:, t, 0:D], XH[:, t % 2, 0, :], ALU.subtract).then_inc(lo_done, 1)
                    chain.link(nc.vector.tensor_tensor(oh2[:], iota[:, 0:E].unsqueeze(1).broadcast_to([P, TILES, E]),
                                                       XN[:, :, D:D + 1].broadcast_to([P, TILES, E]), ALU.is_equal))
                    chain.mark(nc.vector.tensor_tensor(GO[:].rearrange("p (t e) -> p t e", e=E), oh2[:],
                                                       XN[:, :, D + 1:D + 2].broadcast_to([P, TILES, E]), ALU.mult))

                @block.tensor
                def _(pe):
                    pe.wait_ge(cum, TILES + 1)
                    for t in range(TILES):
                        nc.tensor.matmul(psR[:, t, :], before[:], OH[:, t, :], start=True, stop=False)
                        nc.tensor.matmul(psR[:, t, :], ones[:], CUM[:, t, :], start=False, stop=True)
                    nc.tensor.matmul(psC[:], ones[:], CUM[:, TILES, :], start=True, stop=True).then_inc(ranked, 1)
                    for t in range(TILES):
                        pe.wait_ge(lo_done, t + 1)
                        if t >= 2:
                            pe.wait_ge(evac, t - 1)
                        for h in range(2):
                            for c in range(DT):
                                mm = nc.tensor.transpose(psX[:, t % 2, h * DT + c, :], XH[:, t % 2, h, c * P:(c + 1) * P], ident16[:])
                        mm.then_inc(turned, 1)

                @block.gpsimd
                def _(pool):
                    pool.wait_ge(pos_done, 1)
                    for t in range(TILES):
                        pool.indirect_dma_start(out=rows, out_offset=bass.IndirectOffsetOnAxis(ap=POS[:, t:t + 1], axis=0),
                                                in_=XN[:, t, :], in_offset=None).then_inc(sent, 16)

                @block.sync
                def _(sp):
                    sp.wait_ge(sent, 16 * TILES)
                    for g in range(4):
                        sp.dma_start(XN[:, 4 * g:4 * g + 4, :], rowsT[:, 4 * g:4 * g + 4, :]).then_inc(back, 16)

                @block.scalar
                def _(act):
                    for t in range(TILES + 1):
                        if t < TILES:
                            if t == 0:
                                act.wait_ge(back, 16 * 4)
                            if t >= 2:
                                act.wait_ge(turned, t - 1)
                            nc.scalar.activation(XH[:, t % 2, 0, :], XN[:, t, 0:D], ACT.Copy).then_inc(hi_done, 1)
                        if t >= 1:
                            act.wait_ge(turned, t)
                            nc.scalar.activation(XST[:, t - 1], psX[:, (t - 1) % 2], ACT.Copy).then_inc(evac, 1)
            s_.clear()

        YS = sb("YS", [P, TILES, D])
        with ExitStack() as ctx2:
            w_ = Space(nc, ctx2, "walk")
            mask = [w_.sb(f"mask{i}", [P, DT * D]) for i in range(2)]
            W = [w_.sb(f"W{i}", [P, DT, D], F16) for i in range(2)]
            g = w_.sb("g", [P, 1])
            psO = w_.ps("psO", [P, 2, D])
            mask_in = [w_.sem(f"mask_in{i}") for i in range(2)]
            zeroed, W_done, mm_done, g_done, acc_done = (w_.sem(n) for n in ("zeroed", "W_done", "mm_done", "g_done", "acc_done"))
            masks = ins["masksT"].rearrange("e (c p) o -> e p c o", p=P)
            PAIRS = (STEPS - 3) // 2
            with nc.Block() as block:
                @block.sync
                def _(sp):
                    def load_mask(k, j, first=False):
                        e = sp.value_load(EI[0:1, bass.ds(k, 1)], min_val=0, max_val=E - 1)
                        if not first:
                            sp.wait_ge(W_done, k - 1)
                        sp.dma_start(mask[j][:].rearrange("p (c o) -> p c o", c=DT), masks[e]).then_inc(mask_in[j], 16)

                    load_mask(0, 0, True)
                    load_mask(1, 1, True)
                    with sp.Fori(0, PAIRS) as i:
                        for j in range(2):
                            load_mask(i * 2 + (2 + j), j)
                    load_mask(STEPS - 1, 0)

                @block.vector
                def _(dve):
                    def build(n, j):
                        dve.wait_ge(mask_in[j], n * 16)
                        nc.vector.tensor_tensor(W[j][:].rearrange("p c o -> p (c o)"), mask[j][:], tern[:], ALU.mult).then_inc(W_done, 1)

                    def accumulate(k, j):
                        e = dve.value_load(EI[0:1, bass.ds(k, 1)], min_val=0, max_val=E - 1)
                        t = dve.value_load(TI[0:1, bass.ds(k, 1)], min_val=0, max_val=TILES - 1)
                        at = dve.snap(t * E + e, max_val=TILES * E - 1)
                        nc.vector.tensor_copy(g[:], GO[:, bass.ds(at, 1)]).then_inc(g_done, 1)
                        dve.wait_ge(g_done, k + 1)
                        dve.wait_ge(mm_done, k + 1)
                        y = YS[:, t, :]
                        nc.vector.scalar_tensor_tensor(out=y, in0=psO[:, j, :], scalar=g[:], in1=y, op0=ALU.mult, op1=ALU.add).then_inc(acc_done, 1)

                    nc.vector.memset(YS[:], 0.0).then_inc(zeroed, 1)
                    dve.wait_ge(zeroed, 1)
                    build(1, 0)
                    build(1, 1)
                    accumulate(0, 0)
                    with dve.Fori(0, PAIRS) as i:
                        for j in range(2):
                            dve.wait_ge(acc_done, i * 2 + (1 + j))
                            build(i + 2, j)
                            accumulate(i * 2 + (1 + j), 1 - j)
                    dve.wait_ge(acc_done, STEPS - 2)
                    build(STEPS // 2 + 1, 0)
                    accumulate(STEPS - 2, 1)
                    dve.wait_ge(acc_done, STEPS - 1)
                    accumulate(STEPS - 1, 0)

                @block.tensor
                def _(pe):
                    def product(k, j, first=False):
                        t = pe.value_load(TI[0:1, bass.ds(k, 1)], min_val=0, max_val=TILES - 1)
                        pe.wait_ge(W_done, k + 1)
                        if not first:
                            pe.wait_ge(acc_done, k - 1)
                        for q in range(2 * DT):
                            mm = nc.tensor.matmul(psO[:, j, :], XST[:, t, q, :], W[j][:, q % DT, :], start=(q == 0), stop=(q == 2 * DT - 1))
                        mm.then_inc(mm_done, 1)

                    product(0, 0, True)
                    product(1, 1, True)
                    with pe.Fori(0, PAIRS) as i:
                        for j in range(2):
                            product(i * 2 + (2 + j), j)
                    product(STEPS - 1, 0)
            w_.clear()

        with ExitStack() as ctx2:
            u_ = Space(nc, ctx2, "unsort")
            scaled, sent, got, added = (u_.sem(n) for n in ("scaled", "sent", "got", "added"))
            GR = 4
            resT = results.rearrange("(t p) d -> p t d", p=P)
            with nc.Block() as block:
                @block.vector
                def _(dve):
                    for q in range(TILES // GR):
                        y = YS[:, GR * q:GR * q + GR, :]
                        nc.vector.tensor_tensor(y, y, scale[:].unsqueeze(1).broadcast_to([P, GR, D]), ALU.mult).then_inc(scaled, 1)
                    for t in range(TILES):
                        dve.wait_ge(got, 16 * TILES)
                        nc.vector.tensor_tensor(X[:, t, :], X[:, t, :], XN[:, t, 0:D], ALU.add).then_inc(added, 1)

                @block.sync
                def _(sp):
                    for q in range(TILES // GR):
                        sp.wait_ge(scaled, q + 1)
                        sp.dma_start(resT[:, GR * q:GR * q + GR, :], YS[:, GR * q:GR * q + GR, :]).then_inc(sent, 16)

                @block.gpsimd
                def _(pool):
                    pool.wait_ge(sent, 16 * (TILES // GR))
                    for t in range(TILES):
                        pool.indirect_dma_start(out=XN[:, t, 0:D], out_offset=None, in_=results,
                                                in_offset=bass.IndirectOffsetOnAxis(ap=POS[:, t:t + 1], axis=0)).then_inc(got, 16)
            u_.clear()


def stage_attention(nc, X, ident, ident16, ins):
    H, HD = 32, 16
    CK = 2
    AXES, HALF = 2, HD // 4
    FQ = AXES * HALF
    HW = 4 * HD
    G, NG = 4, H // 4
    SCALE = HD ** -0.5
    PI = math.pi
    with ExitStack() as ctx:
        a_ = Space(nc, ctx, "att")
        sb = a_.sb
        Wq = sb("Wq", [P, DT, D])
        Wkv = sb("Wkv", [P, CK, 2 * D])
        Wout = sb("Wout", [P, DT, D])
        bout = sb("bout", [P, D])
        freq = sb("freq", [P, FQ])
        ctxT = sb("ctxT", [P, CK, S])
        xb = sb("xb", [P, NT, D])
        xT = sb("xT", [P, DT, S])
        pos = sb("pos", [P, NT, AXES])
        QS = [sb("QS", [P, H, P], F16), sb("KS", [P, H, P], F16)]
        rot = sb("rot", [P, D])
        t_cos = sb("t_cos", [P, D])
        t_sin = sb("t_sin", [P, D])
        V = sb("V", [P, NT, H, 32])
        QT = sb("QT", [P, H, S], F16)
        KT = sb("KT", [P, H, S], F16)
        with ExitStack() as ctx2:
            c_ = Space(nc, ctx2, "attc")
            loaded, consts, own = c_.sem("loaded"), c_.sem("consts"), c_.sem("own")
            with nc.Block() as block:
                @block.sync
                def _(sp):
                    sp.dma_start(Wq[:], ins["Wq"].rearrange("(c p) n -> p c n", p=P)).then_inc(loaded, 16)
                    sp.dma_start(Wkv[:], ins["Wkv"].rearrange("(c p) n -> p c n", p=P)).then_inc(loaded, 16)
                    sp.dma_start(Wout[:], ins["Wout"].rearrange("(c p) n -> p c n", p=P)).then_inc(loaded, 16)
                    sp.dma_start(bout[:], ins["bout"].partition_broadcast(P)).then_inc(loaded, 16)
                    sp.wait_ge(loaded, 64)

                @block.gpsimd
                def _(pool):
                    nc.gpsimd.memset(V[:], 0.0).then_inc(consts, 1)
                    pool.wait_ge(consts, 1)
                    nc.gpsimd.memset(V[:, :, :, HD:HD + 1], 1.0).then_inc(consts, 1)

                @block.vector
                def _(dve):
                    chain = Tally(dve, own)
                    for j in range(HALF):
                        chain.mark(nc.vector.memset(freq[:].rearrange("p (a f) -> p a f", f=HALF)[:, :, j:j + 1], 10000.0 ** (-j / HALF)))
                    chain.mark(nc.vector.memset(QS[0][:, :, HW:], 0.0))
                    chain.link(nc.vector.memset(QS[1][:, :, HW:], 0.0))
                    chain.mark(nc.vector.memset(QS[1][:, :, HW:HW + 2], 1.0))
            c_.clear()
        X4 = X[:].rearrange("p (b t) d -> p b t d", t=NT)
        posT = ins["pos"].rearrange("b (t p) a -> b p t a", p=P)

        with nc.Fori(0, B) as b:
            with ExitStack() as ctx2:
                p_ = Space(nc, ctx2, "qkv")
                stats = p_.sb("stats", [P, NT, 6])
                mv = p_.sb("mv", [P, NT, 2])
                rstd = p_.sb("rstd", [P, NT, 1])
                ang = p_.sb("ang", [P, 2, NT, FQ])
                turns = p_.sb("turns", [P, 2, NT, FQ], I32)
                turns_f = p_.sb("turns_f", [P, 2, NT, FQ])
                table = p_.sb("table", [P, 2, 2, NT, FQ])
                psX = p_.ps("psX", [P, 2, DT * P])
                psQ = p_.ps("psQ", [P, 3, D])
                psP = p_.ps("psP", [P, 3, 8, P], F16)
                ctx_in, pos_in, mv_done, rooted, xn_done, turned, xT_done = (
                    p_.sem(n) for n in ("ctx_in", "pos_in", "mv_done", "rooted", "xn_done", "turned", "xT_done"))
                proj, ang_done, sin_done, rot_done, hi_done, lo_done, v_done, parts, evac_a, evac_v, own = (
                    p_.sem(n) for n in ("proj", "ang_done", "sin_done", "rot_done", "hi_done", "lo_done", "v_done", "parts", "evac_a", "evac_v", "own"))
                dst = (QT, KT)
                hi_of = (lambda s: s[:, :, 0:2 * HD].rearrange("p h (r d) -> p h r d", r=2),
                         lambda s: s[:, :, 0:HW].rearrange("p h (r w d) -> p h r w d", r=2, w=2)[:, :, :, 0, :])
                lo_of = (lambda s: s[:, :, 2 * HD:HW].rearrange("p h (r d) -> p h r d", r=2),
                         lambda s: s[:, :, 0:HW].rearrange("p h (r w d) -> p h r w d", r=2, w=2)[:, :, :, 1, :])
                with nc.Block() as block:
                    @block.sync
                    def _(sp):
                        sp.dma_start(ctxT[:], ins["ctxT"][b].rearrange("(c p) s -> p c s", p=P)).then_inc(ctx_in, 16)
                        sp.dma_start(pos[:], posT[b]).then_inc(pos_in, 16)

                    @block.tensor
                    def _(pe):
                        def project(t):
                            rows = slice(t * P, (t + 1) * P)
                            if t >= 1:
                                pe.wait_ge(rot_done, 2 * t - 1)
                            for c in range(DT):
                                mm = nc.tensor.matmul(psQ[:, 0, :], xT[:, c, rows], Wq[:, c, :], start=(c == 0), stop=(c == DT - 1))
                            mm.then_inc(proj, 1)
                            if t >= 1:
                                pe.wait_ge(rot_done, 2 * t)
                            for c in range(CK):
                                mm = nc.tensor.matmul(psQ[:, 1, :], ctxT[:, c, rows], Wkv[:, c, 0:D], start=(c == 0), stop=(c == CK - 1))
                            mm.then_inc(proj, 1)
                            if t >= 1:
                                pe.wait_ge(v_done, t)
                            for c in range(CK):
                                mm = nc.tensor.matmul(psQ[:, 2, :], ctxT[:, c, rows], Wkv[:, c, D:], start=(c == 0), stop=(c == CK - 1))
                            mm.then_inc(proj, 1)

                        def turn_parts(t):
                            for s in range(2):
                                pe.wait_ge(hi_done, 2 * t + s + 1)
                                pe.wait_ge(lo_done, 2 * t + s + 1)
                                for q in range(4):
                                    i = (2 * t + s) * 4 + q
                                    if i >= 3:
                                        j = i - 3
                                        pe.wait_ge(evac_v if j % 2 else evac_a, j // 2 + 1)
                                    for h in range(8):
                                        mm = nc.tensor.transpose(psP[:, i % 3, h, :], QS[s][:, 8 * q + h, :], ident16[:])
                                    mm.then_inc(parts, 1)

                        for t in range(NT):
                            pe.wait_ge(xn_done, t + 1)
                            if t >= 2:
                                pe.wait_ge(xT_done, t - 1)
                            for c in range(DT):
                                mm = nc.tensor.transpose(psX[:, t % 2, c * P:(c + 1) * P], xb[:, t, c * P:(c + 1) * P], ident[:])
                            mm.then_inc(turned, 1)
                        pe.wait_ge(ctx_in, 16)
                        for t in range(NT + 1):
                            if t < NT:
                                pe.wait_ge(xT_done, t + 1)
                                project(t)
                            if t >= 1:
                                turn_parts(t - 1)

                    @block.scalar
                    def _(act):
                        act.wait_ge(mv_done, 1)
                        nc.scalar.activation(rstd[:], mv[:, :, 1:2], ACT.Sqrt).then_inc(rooted, 1)
                        act.wait_ge(ang_done, 1)
                        nc.scalar.activation(table[:, 1], ang[:], ACT.Sin).then_inc(sin_done, 1)
                        for t in range(NT):
                            act.wait_ge(turned, t + 1)
                            nc.scalar.activation(xT[:, :, t * P:(t + 1) * P], psX[:, t % 2, :].rearrange("p (c k) -> p c k", c=DT),
                                                 ACT.Copy).then_inc(xT_done, 1)
                        for t in range(NT + 1):
                            for s in range(2):
                                if t >= 1:
                                    for q in (0, 2):
                                        i = (2 * (t - 1) + s) * 4 + q
                                        act.wait_ge(parts, i + 1)
                                        nc.scalar.activation(dst[s][:, 8 * q:8 * q + 8, (t - 1) * P:t * P], psP[:, i % 3], ACT.Copy).then_inc(evac_a, 1)
                                if t < NT:
                                    act.wait_ge(rot_done, 2 * t + s + 1)
                                    if t >= 1:
                                        act.wait_ge(parts, (2 * (t - 1) + s + 1) * 4)
                                    nc.scalar.activation(hi_of[s](QS[s]), rot[:].rearrange("p (h d) -> p h d", h=H).unsqueeze(2).broadcast_to([P, H, 2, HD]),
                                                         ACT.Copy).then_inc(hi_done, 1)
                            if t < NT:
                                act.wait_ge(proj, 3 * t + 3)
                                nc.scalar.activation(V[:, t, :, 0:HD], psQ[:, 2, :].rearrange("p (h d) -> p h d", h=H), ACT.Copy).then_inc(v_done, 1)

                    @block.gpsimd
                    def _(pool):
                        for t in range(NT):
                            for s in range(2):
                                pool.wait_ge(hi_done, 2 * t + s + 1)
                                nc.gpsimd.tensor_tensor(lo_of[s](QS[s]), rot[:].rearrange("p (h d) -> p h d", h=H).unsqueeze(2).broadcast_to([P, H, 2, HD]),
                                                        hi_of[s](QS[s]), ALU.subtract).then_inc(lo_done, 1)

                    @block.vector
                    def _(dve):
                        chain = Tally(dve, own)
                        layernorm_stats(nc, dve, chain, [X4[:, b, t, :] for t in range(NT)], stats, mv)
                        nc.vector.tensor_scalar(mv[:, :, 1:2], mv[:, :, 1:2], LN_EPS, None, ALU.add).then_inc(mv_done, 1)
                        dve.wait_ge(pos_in, 16)
                        chain.link(nc.vector.tensor_tensor(ang[:, 1].rearrange("p t (a f) -> p t a f", f=HALF),
                                                           pos[:].unsqueeze(3).broadcast_to([P, NT, AXES, HALF]),
                                                           freq[:].rearrange("p (a f) -> p a f", f=HALF).unsqueeze(1).broadcast_to([P, NT, AXES, HALF]), ALU.mult))
                        chain.link(nc.vector.tensor_scalar(ang[:, 0], ang[:, 1], PI / 2, None, ALU.add))
                        chain.link(nc.vector.tensor_scalar(turns[:], ang[:], 1 / (2 * PI), None, ALU.mult))
                        chain.link(nc.vector.tensor_copy(turns_f[:], turns[:]))
                        nc.vector.scalar_tensor_tensor(out=ang[:], in0=turns_f[:], scalar=-2 * PI, in1=ang[:], op0=ALU.mult, op1=ALU.add).then_inc(ang_done, 1)
                        dve.wait_ge(rooted, 1)
                        chain.link(nc.vector.reciprocal(rstd[:], rstd[:]))
                        for t in range(NT):
                            nc.vector.tensor_scalar(xb[:, t, :], X4[:, b, t, :], mv[:, t, 0:1], rstd[:, t, :], ALU.subtract, ALU.mult).then_inc(xn_done, 1)
                        dve.wait_ge(sin_done, 1)
                        chain.link(nc.vector.tensor_scalar(table[:, 0], table[:, 1], SCALE, None, ALU.mult))
                        for t in range(NT + 1):
                            for s in range(2):
                                if t < NT:
                                    dve.wait_ge(proj, 3 * t + s + 1)
                                    src = psQ[:, s, :].rearrange("p (h a w) -> p h a w", h=H, w=2)
                                    cos, sin = (table[:, s, w, t, :].unsqueeze(1).unsqueeze(3).broadcast_to([P, H, FQ, 2]) for w in range(2))
                                    chain.mark(nc.vector.tensor_tensor(t_cos[:].rearrange("p (h a w) -> p h a w", h=H, w=2), src, cos, ALU.mult))
                                    chain.link(nc.vector.tensor_tensor(t_sin[:].rearrange("p (h a w) -> p h a w", h=H, w=2), src, sin, ALU.mult))
                                    if 2 * t + s >= 1:
                                        dve.wait_ge(lo_done, 2 * t + s)
                                    c2, s2, r2 = (x[:].rearrange("p (a w) -> p a w", w=2) for x in (t_cos, t_sin, rot))
                                    chain.link(nc.vector.tensor_tensor(r2[:, :, 0], c2[:, :, 0], s2[:, :, 1], ALU.subtract))
                                    nc.vector.tensor_tensor(r2[:, :, 1], s2[:, :, 0], c2[:, :, 1], ALU.add).then_inc(rot_done, 1)
                                    dve.wait_ge(rot_done, 2 * t + s + 1)
                                if t >= 1:
                                    for q in (1, 3):
                                        i = (2 * (t - 1) + s) * 4 + q
                                        dve.wait_ge(parts, i + 1)
                                        nc.vector.tensor_copy(dst[s][:, 8 * q:8 * q + 8, (t - 1) * P:t * P], psP[:, i % 3]).then_inc(evac_v, 1)
                p_.clear()

            with ExitStack() as ctx2:
                s_ = Space(nc, ctx2, "soft")
                NP_ = 4
                Pr = s_.sb("Pr", [P, NP_, 2, S])
                mx = s_.sb("mx", [P, 3, NT, G])
                nm = s_.sb("nm", [P, 3, NT, 2 * G], F16)
                nmT = s_.sb("nmT", [2 * G, 3, S], F16)
                OT = s_.sb("OT", [P, S])
                rec = s_.sb("rec", [P, NT, G])
                psT = s_.ps("psT", [P, 2, 2, S])
                psS = s_.ps("psS", [P, 2, S])
                psO = s_.ps("psO", [P, S])
                psM = s_.ps("psM", [P, S])
                scored, maxed, nm_done, nm_turned, nmT_done, st_done, exp_done, av_done, ot_done, o_turned, o_done, own = (
                    s_.sem(n) for n in ("scored", "maxed", "nm_done", "nm_turned", "nmT_done", "st_done", "exp_done", "av_done", "ot_done", "o_turned", "o_done", "own"))
                rows_in = [s_.sem(f"rows_in{i}") for i in range(3)]
                LAG = 2
                with nc.Block() as block:
                    @block.tensor
                    def _(pe):
                        def scores(g, j):
                            for qt in range(NT):
                                i = (g * G + j) * NT + qt
                                if i >= 2:
                                    pe.wait_ge(maxed, i - 1)
                                nc.tensor.matmul(psS[:, i % 2, :], QT[:, g * G + j, qt * P:(qt + 1) * P], KT[:, g * G + j, :],
                                                 start=True, stop=True).then_inc(scored, 1)

                        def turn_maxima(g):
                            pe.wait_ge(nm_done, g + 1)
                            if g >= LAG + 1:
                                pe.wait_ge(o_done, g - LAG)
                            elif g >= 1:
                                pe.wait_ge(nmT_done, g)
                            v = psM[:, 0:S // 2].bitcast(F16)
                            for qt in range(NT):
                                mm = nc.tensor.transpose(v[0:2 * G, qt * P:(qt + 1) * P], nm[:, g % 3, qt, :], ident16[:])
                            mm.then_inc(nm_turned, 1)

                        def key_scores(g, kt, pair):
                            i = (g * NT + kt) * 2 + pair
                            if kt == 0 and pair == 0:
                                pe.wait_ge(rows_in[g % 3], 32 * (g // 3 + 1))
                            if i >= 2:
                                pe.wait_ge(exp_done, i - 1)
                            for w in range(2):
                                h = g * G + 2 * pair + w
                                mm = nc.tensor.matmul(psT[:, i % 2, w, :], KT[:, h, kt * P:(kt + 1) * P], QT[:, h, :], start=True, stop=True)
                            mm.then_inc(st_done, 1)

                        def values(g, kt):
                            i = (g * NT + kt) * 2
                            pe.wait_ge(exp_done, i + 2)
                            if kt == 0 and g >= 1:
                                pe.wait_ge(ot_done, g)
                            for j in range(G):
                                mm = nc.tensor.matmul(psO[32 * j:32 * j + 32, :], V[:, kt, g * G + j, :], Pr[:, (i + j // 2) % NP_, j % 2, :],
                                                      start=(kt == 0), stop=(kt == NT - 1))
                            mm.then_inc(av_done, 1)

                        def turn_results(g):
                            pe.wait_ge(ot_done, g + 1)
                            if g + LAG < NG:
                                pe.wait_ge(nmT_done, g + LAG + 1)
                            elif g >= 1:
                                pe.wait_ge(o_done, g)
                            for qt in range(NT):
                                mm = nc.tensor.transpose(psM[:, qt * P:(qt + 1) * P], OT[:, qt * P:(qt + 1) * P], ident[:])
                            mm.then_inc(o_turned, 1)

                        for g in range(-LAG, NG):
                            for kt in range(NT):
                                if g >= 0:
                                    key_scores(g, kt, 0)
                                    key_scores(g, kt, 1)
                                if g + LAG < NG:
                                    scores(g + LAG, kt)
                                if g >= 0 and kt >= 1:
                                    values(g, kt - 1)
                            if g >= 0:
                                values(g, NT - 1)
                            if g + LAG < NG:
                                turn_maxima(g + LAG)
                            if g >= 0:
                                turn_results(g)

                    @block.vector
                    def _(dve):
                        chain = Tally(dve, own)
                        for g in range(-LAG, NG):
                            if g + LAG < NG:
                                m = g + LAG
                                for i in range(m * G * NT, (m + 1) * G * NT):
                                    j, qt = i // NT % G, i % NT
                                    dve.wait_ge(scored, i + 1)
                                    nc.vector.tensor_reduce(mx[:, m % 3, qt, j:j + 1], psS[:, i % 2, :], AX.X, ALU.max).then_inc(maxed, 1)
                                dve.wait_ge(maxed, (m + 1) * G * NT)
                                if m >= 3:
                                    dve.wait_ge(nm_turned, m - 2)
                                chain.link(nc.vector.tensor_scalar(nm[:, m % 3, :, 0:G], mx[:, m % 3], -1.0, None, ALU.mult))
                                nc.vector.scalar_tensor_tensor(out=nm[:, m % 3, :, G:], in0=mx[:, m % 3], scalar=-1.0, in1=nm[:, m % 3, :, 0:G],
                                                               op0=ALU.mult, op1=ALU.subtract).then_inc(nm_done, 1)
                            if g >= 0:
                                dve.wait_ge(av_done, NT * (g + 1))
                                if g >= 1:
                                    dve.wait_ge(o_turned, g)
                                nc.vector.tensor_copy(OT[:], psO[:]).then_inc(ot_done, 1)
                                dve.wait_ge(o_turned, g + 1)
                                o = psM[:].rearrange("p (q h d) -> p q h d", q=NT, h=G)
                                chain.link(nc.vector.reciprocal(rec[:], o[:, :, :, HD]))
                                nc.vector.tensor_tensor(xb[:].rearrange("p q (h d) -> p q h d", d=HD)[:, :, G * g:G * g + G, :], o[:, :, :, 0:HD],
                                                        rec[:].unsqueeze(3).broadcast_to([P, NT, G, HD]), ALU.mult).then_inc(o_done, 1)

                    @block.scalar
                    def _(act):
                        def send_maxima(g):
                            act.wait_ge(nm_turned, g + 1)
                            if g >= 3:
                                act.wait_ge(rows_in[g % 3], 32 * (g // 3))
                            nc.scalar.activation(nmT[:, g % 3, :], psM[:, 0:S // 2].bitcast(F16)[0:2 * G, :], ACT.Copy).then_inc(nmT_done, 1)

                        for g in range(-LAG, NG):
                            if g >= 0:
                                for i in range(g * NT * 2, (g + 1) * NT * 2):
                                    act.wait_ge(st_done, i + 1)
                                    if i >= NP_:
                                        act.wait_ge(av_done, (i - NP_) // 2 + 1)
                                    nc.scalar.activation(Pr[:, i % NP_], psT[:, i % 2], ACT.Exp).then_inc(exp_done, 1)
                            if g + LAG < NG:
                                send_maxima(g + LAG)

                    @block.sync
                    def _(sp):
                        for g in range(NG):
                            sp.wait_ge(nmT_done, g + 1)
                            for w in range(2):
                                sp.dma_start(QT[HW + w:HW + w + 1, G * g:G * g + G, :], nmT[G * w:G * w + G, g % 3, :]).then_inc(rows_in[g % 3], 16)
                s_.clear()

            with ExitStack() as ctx2:
                o_ = Space(nc, ctx2, "wout")
                psX = o_.ps("psX", [P, 2, DT * P])
                psY = o_.ps("psY", [P, 2, D])
                turned, xT_done, proj, biased, added = (o_.sem(n) for n in ("turned", "xT_done", "proj", "biased", "added"))
                with nc.Block() as block:
                    @block.tensor
                    def _(pe):
                        for t in range(NT + 1):
                            if t < NT:
                                if t >= 2:
                                    pe.wait_ge(xT_done, t - 1)
                                for c in range(DT):
                                    mm = nc.tensor.transpose(psX[:, t % 2, c * P:(c + 1) * P], xb[:, t, c * P:(c + 1) * P], ident[:])
                                mm.then_inc(turned, 1)
                            if t >= 1:
                                pe.wait_ge(xT_done, t)
                                if t >= 3:
                                    pe.wait_ge(added, t - 2)
                                for c in range(DT):
                                    mm = nc.tensor.matmul(psY[:, (t - 1) % 2, :], xT[:, c, (t - 1) * P:t * P], Wout[:, c, :], start=(c == 0), stop=(c == DT - 1))
                                mm.then_inc(proj, 1)

                    @block.scalar
                    def _(act):
                        for t in range(NT):
                            act.wait_ge(turned, t + 1)
                            nc.scalar.activation(xT[:, :, t * P:(t + 1) * P], psX[:, t % 2, :].rearrange("p (c k) -> p c k", c=DT),
                                                 ACT.Copy).then_inc(xT_done, 1)

                    @block.gpsimd
                    def _(pool):
                        for t in range(NT):
                            nc.gpsimd.tensor_tensor(X4[:, b, t, :], X4[:, b, t, :], bout[:], ALU.add).then_inc(biased, 1)

                    @block.vector
                    def _(dve):
                        for t in range(NT):
                            dve.wait_ge(biased, t + 1)
                            dve.wait_ge(proj, t + 1)
                            nc.vector.tensor_tensor(X4[:, b, t, :], X4[:, b, t, :], psY[:, t % 2, :], ALU.add).then_inc(added, 1)
                o_.clear()


def stage_mlp(nc, X, ident, ins):
    INNER = 11 * P
    JT = INNER // P
    GU = 2 * INNER
    PER = 8
    EPS = 1e-6
    with ExitStack() as ctx:
        m_ = Space(nc, ctx, "mlp")
        sb = m_.sb
        Wgu = sb("Wgu", [P, DT, GU])
        Wd = sb("Wd", [P, JT, D])
        with ExitStack() as ctx2:
            d_ = Space(nc, ctx2, "deq")
            shift = d_.sb("shift", [P, 1], I32)
            t1 = d_.sb("t1", [P, GU], I32)
            t2 = d_.sb("t2", [P, GU], I32)
            s_gu = d_.sb("s_gu", [P, DT * GU], F16)
            s_d = d_.sb("s_d", [P, JT * D], F16)
            loaded, consts, own = d_.sem("loaded"), d_.sem("consts"), d_.sem("own")
            with nc.Block() as block:
                @block.sync
                def _(sp):
                    for k in range(PER):
                        sp.dma_start(Wgu[k:P:PER].bitcast(I32), ins["gate_upT"].rearrange("(g j) o -> j g o", j=P // PER)).then_inc(loaded, 16)
                        sp.dma_start(Wd[k:P:PER].bitcast(I32), ins["downT"].rearrange("(g j) o -> j g o", j=P // PER)).then_inc(loaded, 16)

                @block.scalar
                def _(act):
                    act.dma_start(s_gu[:], ins["gate_up_scales"].rearrange("g o -> (g o)").partition_broadcast(P)).then_inc(loaded, 16)
                    act.dma_start(s_d[:], ins["down_scales"].rearrange("g o -> (g o)").partition_broadcast(P)).then_inc(loaded, 16)

                @block.gpsimd
                def _(pool):
                    nc.gpsimd.iota(shift[:], [[0, 1]], base=0, channel_multiplier=4).then_inc(consts, 1)

                @block.vector
                def _(dve):
                    chain = Tally(dve, own)
                    dve.wait_ge(consts, 1)
                    chain.link(nc.vector.tensor_scalar(shift[:], shift[:], 4 * PER - 1, None, ALU.bitwise_and))
                    dve.wait_ge(loaded, 16 * (2 * PER + 2))
                    flat_d = Wd[:].rearrange("p j o -> p (j o)")
                    parts = [(Wgu[:, g, :], s_gu[:, g * GU:(g + 1) * GU]) for g in range(DT)]
                    parts += [(flat_d[:, g * GU:(g + 1) * GU], s_d[:, g * GU:(g + 1) * GU]) for g in range(JT * D // GU)]
                    for w, s in parts:
                        words = w.bitcast(I32)
                        chain.mark(nc.vector.tensor_scalar(t1[:], words, shift[:], 7, ALU.logical_shift_right, ALU.bitwise_and))
                        chain.link(nc.vector.tensor_scalar(t2[:], words, shift[:], 8, ALU.logical_shift_right, ALU.bitwise_and))
                        chain.link(nc.vector.scalar_tensor_tensor(out=t1[:], in0=t2[:], scalar=3, in1=t1[:], op0=ALU.logical_shift_left, op1=ALU.bitwise_or))
                        chain.link(nc.vector.tensor_scalar(t1[:], t1[:], 9, None, ALU.logical_shift_left))
                        half = t1[:].bitcast(F16).rearrange("p (o w) -> p o w", w=2)[:, :, 0]
                        chain.link(nc.vector.scalar_tensor_tensor(out=w, in0=half, scalar=2.0 ** 14, in1=s, op0=ALU.mult, op1=ALU.mult))
            d_.clear()

        xb = sb("xb", [P, NT, D])
        xT = sb("xT", [P, DT, S])
        hT = sb("hT", [P, JT, S])
        sg = sb("sg", [P, 2, S])
        sq = sb("sq", [P, D])
        ss = sb("ss", [P, NT])
        stats = sb("stats", [P, NT, 6])
        mv = sb("mv", [P, NT, 2])
        rstd = sb("rstd", [P, NT, 1])
        ps = m_.ps
        psX = ps("psX", [P, 2, DT * P])
        psG = ps("psG", [P, 2, S])
        psU = ps("psU", [P, 2, S])
        psD = ps("psD", [P, 2, D])
        X4 = X[:].rearrange("p (b t) d -> p b t d", t=NT)
        mv_done, rooted, xn_done, turned, xT_done, gated, upped, silu_done, h_done, down, squared, ms_done, root2, added, own = (
            m_.sem(n) for n in ("mv_done", "rooted", "xn_done", "turned", "xT_done", "gated", "upped", "silu_done", "h_done", "down", "squared",
                                "ms_done", "root2", "added", "own"))
        with nc.Fori(0, B) as b:
            with nc.Block() as block:
                @block.vector
                def _(dve):
                    chain = Tally(dve, own)
                    layernorm_stats(nc, dve, chain, [X4[:, b, t, :] for t in range(NT)], stats, mv)
                    nc.vector.tensor_scalar(mv[:, :, 1:2], mv[:, :, 1:2], LN_EPS, None, ALU.add).then_inc(mv_done, 1)
                    dve.wait_ge(rooted, 1)
                    chain.link(nc.vector.reciprocal(rstd[:], rstd[:]))
                    for t in range(NT):
                        nc.vector.tensor_scalar(xb[:, t, :], X4[:, b, t, :], mv[:, t, 0:1], rstd[:, t, :], ALU.subtract, ALU.mult).then_inc(xn_done, 1)
                    for j in range(JT):
                        dve.wait_ge(silu_done, j + 1)
                        dve.wait_ge(upped, j + 1)
                        nc.vector.tensor_tensor(hT[:, j, :], sg[:, j % 2, :], psU[:, j % 2, :], ALU.mult).then_inc(h_done, 1)
                    for t in range(NT):
                        dve.wait_ge(squared, t + 1)
                        nc.vector.tensor_scalar(ss[:, t:t + 1], ss[:, t:t + 1], 1.0 / D, EPS, ALU.mult, ALU.add).then_inc(ms_done, 1)
                        dve.wait_ge(root2, t + 1)
                        chain.link(nc.vector.reciprocal(ss[:, t:t + 1], ss[:, t:t + 1]))
                        nc.vector.scalar_tensor_tensor(out=X4[:, b, t, :], in0=psD[:, t % 2, :], scalar=ss[:, t:t + 1], in1=X4[:, b, t, :],
                                                       op0=ALU.mult, op1=ALU.add).then_inc(added, 1)

                @block.scalar
                def _(act):
                    act.wait_ge(mv_done, 1)
                    nc.scalar.activation(rstd[:], mv[:, :, 1:2], ACT.Sqrt).then_inc(rooted, 1)
                    for t in range(NT):
                        act.wait_ge(turned, t + 1)
                        nc.scalar.activation(xT[:, :, t * P:(t + 1) * P], psX[:, t % 2, :].rearrange("p (c k) -> p c k", c=DT), ACT.Copy).then_inc(xT_done, 1)
                    for j in range(JT):
                        act.wait_ge(gated, j + 1)
                        if j >= 2:
                            act.wait_ge(h_done, j - 1)
                        nc.scalar.activation(sg[:, j % 2, :], psG[:, j % 2, :], ACT.Silu).then_inc(silu_done, 1)
                    for t in range(NT):
                        act.wait_ge(down, t + 1)
                        if t >= 1:
                            act.wait_ge(squared, t)
                        nc.scalar.activation(sq[:], psD[:, t % 2, :], ACT.Square, accum_out=ss[:, t:t + 1]).then_inc(squared, 1)
                        act.wait_ge(ms_done, t + 1)
                        nc.scalar.activation(ss[:, t:t + 1], ss[:, t:t + 1], ACT.Sqrt).then_inc(root2, 1)

                @block.tensor
                def _(pe):
                    for t in range(NT):
                        pe.wait_ge(xn_done, t + 1)
                        if t >= 2:
                            pe.wait_ge(xT_done, t - 1)
                        for c in range(DT):
                            mm = nc.tensor.transpose(psX[:, t % 2, c * P:(c + 1) * P], xb[:, t, c * P:(c + 1) * P], ident[:])
                        mm.then_inc(turned, 1)
                    pe.wait_ge(xT_done, NT)
                    for j in range(JT):
                        if j >= 2:
                            pe.wait_ge(silu_done, j - 1)
                        for c in range(DT):
                            mm = nc.tensor.matmul(psG[:, j % 2, :], Wgu[:, c, j * P:(j + 1) * P], xT[:, c, :], start=(c == 0), stop=(c == DT - 1))
                        mm.then_inc(gated, 1)
                        if j >= 2:
                            pe.wait_ge(h_done, j - 1)
                        for c in range(DT):
                            mm = nc.tensor.matmul(psU[:, j % 2, :], Wgu[:, c, INNER + j * P:INNER + (j + 1) * P], xT[:, c, :], start=(c == 0), stop=(c == DT - 1))
                        mm.then_inc(upped, 1)
                    pe.wait_ge(h_done, JT)
                    for t in range(NT):
                        if t >= 2:
                            pe.wait_ge(added, t - 1)
                        for j in range(JT):
                            mm = nc.tensor.matmul(psD[:, t % 2, :], hT[:, j, t * P:(t + 1) * P], Wd[:, j, :], start=(j == 0), stop=(j == JT - 1))
                        mm.then_inc(down, 1)
            m_.clear()


LAYOUT = {
    "x": ("x", None),
    "ctxT": ("ctx_1024", (0, 2, 1)),
    "pos": ("fside_BxSx2_0", None),
    "in_proj_wT": ("L0_xattn_in_proj_w", (1, 0)),
    "x_proj_wT": ("L0_xattn_x_proj_w", (1, 0)),
    "dt_proj_wT": ("L0_xattn_dt_proj_w", (1, 0)),
    "A_log": ("L0_xattn_A_log", None),
    "ternaryT": ("L0_ffn_weight", (1, 0)),
    "out_scale": ("L0_ffn_scale", None),
    "masksT": ("L0_ffn_expert_masks", (0, 2, 1)),
    "routerT": ("L0_ffn_router_w", (1, 0)),
    "Wq": ("L1_xattn_Wq", None),
    "Wkv": ("L1_xattn_Wkv", None),
    "Wout": ("L1_xattn_Wout", None),
    "bout": ("L1_xattn_bout", None),
    "gate_upT": ("L1_ffn_gate_up_packed", (1, 0)),
    "gate_up_scales": ("L1_ffn_gate_up_scales", None),
    "downT": ("L1_ffn_down_packed", (1, 0)),
    "down_scales": ("L1_ffn_down_scales", None),
}


CHANNELS = ("L0_xattn_conv_w", "L0_xattn_conv_b", "L0_xattn_dt_proj_b", "L0_xattn_D")


def layouts(inputs):
    import numpy as np

    arrays = {}
    for name, (source, axes) in LAYOUT.items():
        a = np.asarray(inputs[source])
        arrays[name] = np.ascontiguousarray(a if axes is None else a.transpose(axes))
    columns = [np.asarray(inputs[c]) for c in CHANNELS]
    arrays["channels"] = np.concatenate([c if c.ndim == 2 else c[:, None] for c in columns], axis=1)
    return arrays


def program(nc, ins, out):
    with ExitStack() as ctx:
        X = ctx.enter_context(nc.sbuf_tensor("X", [P, TILES, D], F32))
        ident = ctx.enter_context(nc.sbuf_tensor("ident", [P, P], F32))
        ident16 = ctx.enter_context(nc.sbuf_tensor("ident16", [P, P], F16))
        id_done = [ctx.enter_context(nc.semaphore(f"id_done{i}")) for i in range(2)]
        stored = ctx.enter_context(nc.semaphore("stored"))
        bc_rows = nc.dram_tensor("bc_rows", (B, 32, S), F32).ap()
        sorted_rows = nc.dram_tensor("sorted_rows", (B * S, D + 2), F32).ap()
        sorted_results = nc.dram_tensor("sorted_results", (B * S, D), F32).ap()
        make_identity(nc, (ident, ident16), id_done)
        stage_ssm(nc, X, ident, bc_rows, ins)
        stage_experts(nc, X, ident, ident16, (sorted_rows, sorted_results), ins)
        stage_attention(nc, X, ident, ident16, ins)
        stage_mlp(nc, X, ident, ins)
        with nc.Block() as block:
            @block.sync
            def _(sp):
                sp.dma_start(out.rearrange("b (t p) d -> p (b t) d", p=P), X[:]).then_inc(stored, 16)
                sp.wait_ge(stored, 16)


def kernel(**inputs):
    import numpy as np
    import concourse.bacc as bacc
    from concourse.bass_utils import run_bass_kernel_spmd

    nc = bacc.Bacc("TRN2", target_bir_lowering=False, num_devices=1)
    arrays = {f"in_{name}": a for name, a in layouts(inputs).items()}
    ins = {name[3:]: nc.dram_tensor(name, a.shape, mybir.dt.from_np(a.dtype), kind="ExternalInput").ap() for name, a in arrays.items()}
    out = nc.dram_tensor("out_x", (B, S, D), F32, kind="ExternalOutput").ap()
    program(nc, ins, out)
    return run_bass_kernel_spmd(nc, [arrays], core_ids=[0]).results[0]["out_x"]
```

```python
import math
from contextlib import ExitStack

import concourse.bass as bass
from concourse import mybir

F32 = mybir.dt.float32
F16 = mybir.dt.float16
I32 = mybir.dt.int32
U32 = mybir.dt.uint32
ALU = mybir.AluOpType
ACT = mybir.ActivationFunctionType
AX = mybir.AxisListType

P = 128
B, S, D = 4, 512, 512
NT = S // P
TILES = B * NT
DT = D // P
LN_EPS = 1e-5


class Tally:

    def __init__(self, eng, sem):
        self.eng, self.sem, self.n = eng, sem, 0

    def mark(self, ins):
        ins.then_inc(self.sem, 1)
        self.n += 1
        return self.n

    def wait(self, n=None):
        self.eng.wait_ge(self.sem, self.n if n is None else n)

    def link(self, ins):
        self.mark(ins)
        self.wait()


class Space:

    def __init__(self, nc, ctx, tag):
        self.nc, self.ctx, self.tag, self.sems = nc, ctx, tag, []

    def sb(self, name, shape, dt=F32):
        return self.ctx.enter_context(self.nc.sbuf_tensor(f"{self.tag}_{name}", shape, dt))

    def ps(self, name, shape, dt=F32):
        return self.ctx.enter_context(self.nc.psum_tensor(f"{self.tag}_{name}", shape, dt))

    def sem(self, name):
        s = self.ctx.enter_context(self.nc.semaphore(f"{self.tag}_{name}"))
        self.sems.append(s)
        return s

    def clear(self):
        for s in self.sems:
            self.nc.sync.sem_clear(s)
        self.nc.all_engine_barrier()


def layernorm_stats(nc, dve, chain, x_tiles, stats, mv):
    for t, x in enumerate(x_tiles):
        chain.mark(nc.vector.bn_stats(stats[:, t, :], x))
    chain.wait()
    for t in range(len(x_tiles)):
        chain.mark(nc.vector.bn_aggr(mv[:, t, :], stats[:, t, :]))
    chain.wait()


def stage_ssm(nc, X, ident, scratch, ins):
    DC, CK = 4, 2
    DR, DS = 16, 16
    RING = 4
    with ExitStack() as ctx:
        sp_ = Space(nc, ctx, "ssm")
        sb, ps, sem = sp_.sb, sp_.ps, sp_.sem
        ctxT = sb("ctxT", [P, B, CK, S])
        w_in = sb("w_in", [P, CK, D])
        w_xp = sb("w_xp", [P, DT, DR + 2 * DS])
        w_dt = sb("w_dt", [DR, D])
        par = sb("par", [P, DT, DC + 3])
        negA = sb("negA", [P, DT, DS])
        acc = sb("acc", [P, DT, S])
        u = sb("u", [P, DT, S])
        tpre = sb("tpre", [P, DT, S])
        delta = sb("delta", [P, DT, S])
        zs = sb("zs", [P, NT, S])
        xdbl = sb("xdbl", [DR + 2 * DS, S])
        BC = sb("BC", [P, RING, 2, S])
        dBu = sb("dBu", [P, 3, S])
        hC = sb("hC", [P, 3, S])
        yo = sb("yo", [P, 2, S])
        stats = sb("stats", [P, NT, 6])
        mv = sb("mv", [P, NT, 2])
        rstd = sb("rstd", [P, NT, 1])
        psY = ps("psY", [P, DT, S])
        psA = ps("psA", [P, 2, S])
        psH = ps("psH", [P, 2, S])

        loaded = sem("loaded")
        prep = sem("prep")
        with nc.Block() as block:
            @block.sync
            def _(sp):
                sp.dma_start(X[:], ins["x"].rearrange("b (t p) d -> p (b t) d", p=P)).then_inc(loaded, 16)
                for b in range(B):
                    sp.dma_start(ctxT[:, b], ins["ctxT"][b].rearrange("(c p) s -> p c s", p=P)).then_inc(loaded, 16)

            @block.scalar
            def _(act):
                act.dma_start(w_in[:], ins["in_proj_wT"].rearrange("(c p) e -> p c e", p=P)).then_inc(loaded, 16)
                act.dma_start(w_xp[:], ins["x_proj_wT"].rearrange("(c p) k -> p c k", p=P)).then_inc(loaded, 16)
                act.dma_start(w_dt[:], ins["dt_proj_wT"]).then_inc(loaded, 16)
                act.dma_start(par[:], ins["channels"].rearrange("(c p) k -> p c k", p=P)).then_inc(loaded, 16)
                act.dma_start(negA[:], ins["A_log"].rearrange("(c p) n -> p c n", p=P)).then_inc(loaded, 16)
                act.wait_ge(loaded, 16 * 10)
                nc.scalar.activation(negA[:], negA[:], ACT.Exp).then_inc(prep, 1)

            @block.vector
            def _(dve):
                dve.wait_ge(prep, 1)
                nc.vector.tensor_scalar(negA[:], negA[:], -1.0, None, ALU.mult).then_inc(prep, 1)
                dve.wait_ge(loaded, 16 * 10)

        sp_.clear()
        inproj, u_done, xdbl_ps, xdbl_sb, dtp = (sem(n) for n in ("inproj", "u_done", "xdbl_ps", "xdbl_sb", "dtp"))
        conv_done, t_done, e_done, l_done, r_done, z_done = (sem(n) for n in ("conv_done", "t_done", "e_done", "l_done", "r_done", "z_done"))
        mv_done, du_done, bc_out, dA_done, dBu_done, hC_done = (sem(n) for n in ("mv_done", "du_done", "bc_out", "dA_done", "dBu_done", "hC_done"))
        bc_in = [sem(f"bc_in{i}") for i in range(RING)]
        h_done, summed, y_done, turned, own, own_act = (sem(n) for n in ("h_done", "summed", "y_done", "turned", "own", "own_act"))
        zcol = sem("zcol")
        UNITS = DS * DT
        X4 = X[:].rearrange("p (b t) d -> p b t d", t=NT)
        with nc.Fori(0, B) as b:
            with nc.Block() as block:
                @block.sync
                def _(sp):
                    sp.wait_ge(xdbl_sb, 1)
                    sp.dma_start(scratch[b], xdbl[DR:, :]).then_inc(bc_out, 16)
                    sp.wait_ge(bc_out, 16)
                    for n in range(DS):
                        if n >= RING:
                            sp.wait_ge(hC_done, DT * (n - RING + 1))
                        sp.dma_start(BC[:, n % RING], bcast_rows(scratch[b], n)).then_inc(bc_in[n % RING], 16)

                @block.tensor
                def _(pe):
                    for e in range(DT):
                        for c in range(CK):
                            mm = nc.tensor.matmul(psY[:, e, :], w_in[:, c, e * P:(e + 1) * P], ctxT[:, b, c, :],
                                                  start=(c == 0), stop=(c == CK - 1))
                        mm.then_inc(inproj, 1)
                    for e in range(DT):
                        pe.wait_ge(u_done, e + 1)
                        mm = nc.tensor.matmul(psA[0:DR + 2 * DS, 0, :], w_xp[:, e, :], u[:, e, :],
                                              start=(e == 0), stop=(e == DT - 1))
                    mm.then_inc(xdbl_ps, 1)
                    pe.wait_ge(xdbl_sb, 1)
                    for e in range(DT):
                        nc.tensor.matmul(psY[:, e, :], w_dt[:, e * P:(e + 1) * P], xdbl[0:DR, :],
                                         start=True, stop=True).then_inc(dtp, 1)
                    pe.wait_ge(t_done, DT)
                    for i in range(UNITS):
                        n, e = divmod(i, DT)
                        pe.wait_ge(hC_done, i + 1)
                        nc.tensor.matmul(psY[:, e, :], ident[:], hC[:, i % 3, :],
                                         start=(n == 0), stop=(n == DS - 1)).then_inc(summed, 1)
                    for e in range(DT):
                        pe.wait_ge(y_done, e + 1)
                        if e >= 2:
                            pe.wait_ge(r_done, 1 + e - 1)
                        for t in range(NT):
                            mm = nc.tensor.transpose(psA[:, e % 2, t * P:(t + 1) * P], yo[:, e % 2, t * P:(t + 1) * P], ident[:])
                        mm.then_inc(turned, 1)

                @block.scalar
                def _(act):
                    for e in range(DT):
                        act.wait_ge(conv_done, e + 1)
                        nc.scalar.activation(u[:, e, :], acc[:, e, :], ACT.Silu, bias=par[:, e, DC:DC + 1]).then_inc(u_done, 1)
                    act.wait_ge(mv_done, 1)
                    nc.scalar.activation(rstd[:], mv[:, :, 1:2], ACT.Sqrt).then_inc(own_act, 1)
                    act.wait_ge(xdbl_ps, 1)
                    nc.scalar.activation(xdbl[:], psA[0:DR + 2 * DS, 0, :], ACT.Copy).then_inc(xdbl_sb, 1)
                    act.wait_ge(z_done, 1)
                    nc.scalar.activation(zs[:], zs[:], ACT.Silu).then_inc(z_done, 1)
                    act.wait_ge(t_done, DT + 1)
                    nc.scalar.activation(acc[:], acc[:], ACT.Exp, scale=-1.0).then_inc(e_done, 1)
                    act.wait_ge(e_done, 1)
                    nc.scalar.activation(acc[:], acc[:], ACT.Ln, bias=1.0).then_inc(l_done, 1)
                    act.wait_ge(zcol, 1)
                    act.wait_ge(r_done, 1)
                    for i in range(UNITS):
                        n, e = divmod(i, DT)
                        if i >= 2:
                            act.wait_ge(h_done, i - 1)
                        nc.scalar.activation(psA[:, i % 2, 1:S], delta[:, e, 1:S], ACT.Exp,
                                             scale=negA[:, e, n:n + 1]).then_inc(dA_done, 1)

                @block.gpsimd
                def _(pool):
                    pool.wait_ge(du_done, 1)
                    for i in range(UNITS):
                        n, e = divmod(i, DT)
                        if e == 0:
                            pool.wait_ge(bc_in[n % RING], 16 * (n // RING + 1))
                        if i >= 3:
                            pool.wait_ge(h_done, i - 2)
                        nc.gpsimd.tensor_tensor(dBu[:, i % 3, :], tpre[:, e, :], BC[:, n % RING, 0, :], ALU.mult).then_inc(dBu_done, 1)

                @block.vector
                def _(dve):
                    chain = Tally(dve, own)
                    layernorm_stats(nc, dve, chain, [X4[:, b, t, :] for t in range(NT)], stats, mv)
                    nc.vector.tensor_scalar(mv[:, :, 1:2], mv[:, :, 1:2], LN_EPS, None, ALU.add).then_inc(mv_done, 1)
                    for e in range(DT):
                        dve.wait_ge(inproj, e + 1)
                        chain.link(nc.vector.tensor_scalar(acc[:, e, :], psY[:, e, :], par[:, e, DC - 1:DC], None, ALU.mult))
                        for k in range(1, DC):
                            ins_ = nc.vector.scalar_tensor_tensor(out=acc[:, e, k:], in0=psY[:, e, :S - k], scalar=par[:, e, DC - 1 - k:DC - k],
                                                                  in1=acc[:, e, k:], op0=ALU.mult, op1=ALU.add)
                            if k < DC - 1:
                                chain.link(ins_)
                        ins_.then_inc(conv_done, 1)
                    dve.wait_ge(own_act, 1)
                    chain.link(nc.vector.reciprocal(rstd[:], rstd[:]))
                    for t in range(NT):
                        ins_ = nc.vector.tensor_scalar(zs[:, t, :], X4[:, b, t, :], mv[:, t, 0:1], rstd[:, t, :], ALU.subtract, ALU.mult)
                        if t < NT - 1:
                            chain.mark(ins_)
                    ins_.then_inc(z_done, 1)
                    chain.wait()
                    for e in range(DT):
                        dve.wait_ge(dtp, e + 1)
                        nc.vector.tensor_scalar(tpre[:, e, :], psY[:, e, :], par[:, e, DC + 1:DC + 2], None, ALU.add).then_inc(t_done, 1)
                    dve.wait_ge(t_done, DT)
                    dve.wait_ge(u_done, DT)
                    nc.vector.scalar_tensor_tensor(out=acc[:], in0=tpre[:], scalar=-1.0, in1=tpre[:], op0=ALU.mult, op1=ALU.max).then_inc(t_done, 1)
                    dve.wait_ge(xdbl_sb, 1)
                    nc.vector.memset(psA[:, :, 0:1], 0.0).then_inc(zcol, 1)
                    dve.wait_ge(l_done, 1)
                    nc.vector.scalar_tensor_tensor(out=delta[:], in0=tpre[:], scalar=0.0, in1=acc[:], op0=ALU.max, op1=ALU.add).then_inc(r_done, 1)
                    dve.wait_ge(r_done, 1)
                    nc.vector.tensor_tensor(tpre[:], delta[:], u[:], ALU.mult).then_inc(du_done, 1)
                    dve.wait_ge(zcol, 1)

                    def project_states(i):
                        n, e = divmod(i, DT)
                        dve.wait_ge(h_done, i + 1)
                        if i >= 3:
                            dve.wait_ge(summed, i - 2)
                        nc.vector.tensor_tensor(hC[:, i % 3, :], psH[:, i % 2, :], BC[:, n % RING, 1, :], ALU.mult).then_inc(hC_done, 1)

                    for i in range(UNITS):
                        n, e = divmod(i, DT)
                        dve.wait_ge(dA_done, i + 1)
                        dve.wait_ge(dBu_done, i + 1)
                        if e == 0:
                            dve.wait_ge(bc_in[n % RING], 16 * (n // RING + 1))
                        if i >= 2:
                            dve.wait_ge(hC_done, i - 1)
                        nc.vector.tensor_tensor_scan(psH[:, i % 2, :], psA[:, i % 2, :], dBu[:, i % 3, :], 0.0, ALU.mult, ALU.add).then_inc(h_done, 1)
                        if i >= 1:
                            project_states(i - 1)
                    project_states(UNITS - 1)
                    dve.wait_ge(z_done, 2)
                    for e in range(DT):
                        dve.wait_ge(summed, UNITS - DT + e + 1)
                        if e >= 2:
                            dve.wait_ge(turned, e - 1)
                        chain.link(nc.vector.scalar_tensor_tensor(out=yo[:, e % 2, :], in0=u[:, e, :], scalar=par[:, e, DC + 2:DC + 3],
                                                                  in1=psY[:, e, :], op0=ALU.mult, op1=ALU.add))
                        nc.vector.tensor_tensor(yo[:, e % 2, :], yo[:, e % 2, :], zs[:, e, :], ALU.mult).then_inc(y_done, 1)
                        dve.wait_ge(turned, e + 1)
                        xe = X4[:, b, :, e * P:(e + 1) * P]
                        nc.vector.tensor_tensor(xe, xe, psA[:, e % 2, :].rearrange("p (t e) -> p t e", e=P), ALU.add).then_inc(r_done, 1)
            sp_.clear()


def bcast_rows(rows, n):
    return rows.rearrange("(w n) s -> n w s", w=2)[n].partition_broadcast(P)


def make_identity(nc, tiles, sems):
    with nc.Block() as block:
        @block.gpsimd
        def _(pool):
            for tile, s in zip(tiles, sems):
                nc.gpsimd.memset(tile[:], 0.0).then_inc(s, 1)
                pool.wait_ge(s, 1)
                nc.gpsimd.affine_select(out=tile[:], in_=tile[:], compare_op=ALU.not_equal, fill=1.0, base=0,
                                        pattern=[[-1, P]], channel_multiplier=1).then_inc(s, 1)
                pool.wait_ge(s, 2)


def stage_experts(nc, X, ident, ident16, scratch, ins):
    E = 32
    STEPS = TILES + E - 1
    ROW = D + 2
    rows, results = scratch
    with ExitStack() as ctx:
        sp_ = Space(nc, ctx, "moe")
        sb, ps, sem = sp_.sb, sp_.ps, sp_.sem
        XN = sb("XN", [P, TILES, ROW])
        router = sb("router", [P, DT, E])
        tern32 = sb("tern32", [P, DT * D])
        tern = sb("tern", [P, DT * D], F16)
        negs = sb("negs", [P, DT * D], F16)
        scale = sb("scale", [P, D])
        iota_i = sb("iota_i", [P, 64], I32)
        iota = sb("iota", [P, 64])
        tile_end = sb("tile_end", [P, TILES])
        before = sb("before", [P, P], F16)
        ones = sb("ones", [P, P], F16)
        ones32 = sb("ones32", [P, E])
        OH = sb("OH", [P, TILES, E], F16)
        CUM = sb("CUM", [P, TILES + 1, E], F16)
        POS = sb("POS", [P, TILES], U32)
        Ef = sb("Ef", [P, STEPS])
        EI = sb("EI", [P, STEPS], I32)
        TI = sb("TI", [P, STEPS], I32)

        with ExitStack() as ctx2:
            r_ = Space(nc, ctx2, "route")
            xb = r_.sb("xb", [P, NT, D])
            xT = r_.sb("xT", [P, 2, DT * P])
            lg = r_.sb("lg", [P, NT, E])
            ex = r_.sb("ex", [P, NT, E])
            m8 = r_.sb("m8", [P, NT, 8])
            negm = r_.sb("negm", [P, NT])
            i8 = r_.sb("i8", [P, NT, 8], U32)
            idx = r_.sb("idx", [P, NT, 1])
            den = r_.sb("den", [P, NT, 1])
            stats = r_.sb("stats", [P, NT, 6])
            mv = r_.sb("mv", [P, NT, 2])
            rstd = r_.sb("rstd", [P, NT, 1])
            psT = r_.ps("psT", [P, 2, DT * P])
            psL = r_.ps("psL", [P, NT, E])
            loaded, consts, tern_own = r_.sem("loaded"), r_.sem("consts"), r_.sem("tern_own")
            with nc.Block() as block:
                @block.sync
                def _(sp):
                    sp.dma_start(router[:], ins["routerT"].rearrange("(c p) e -> p c e", p=P)).then_inc(loaded, 16)
                    sp.dma_start(scale[:], ins["out_scale"].partition_broadcast(P)).then_inc(loaded, 16)
                    sp.dma_start(tern32[:].rearrange("p (c o) -> p c o", c=DT),
                                 ins["ternaryT"].rearrange("(c p) o -> p c o", p=P)).then_inc(loaded, 16)

                @block.gpsimd
                def _(pool):
                    nc.gpsimd.iota(iota_i[:], [[1, 64]], base=0, channel_multiplier=0).then_inc(consts, 1)
                    nc.gpsimd.memset(ones[:], 1.0).then_inc(consts, 1)
                    nc.gpsimd.memset(ones32[:], 1.0).then_inc(consts, 1)
                    pool.wait_ge(consts, 3)
                    nc.gpsimd.tensor_copy(iota[:], iota_i[:]).then_inc(consts, 1)
                    nc.gpsimd.affine_select(out=before[:], in_=ones[:], compare_op=ALU.is_ge, fill=0.0, base=-1,
                                            pattern=[[1, P]], channel_multiplier=-1).then_inc(consts, 1)

                @block.vector
                def _(dve):
                    dve.wait_ge(consts, 5)
                    nc.vector.tensor_scalar(tile_end[:], iota[:, 0:TILES], 1.0, float(P), ALU.add, ALU.mult).then_inc(tern_own, 1)
                    dve.wait_ge(loaded, 48)
                    nc.vector.tensor_scalar(tern[:], tern32[:], 0.25, None, ALU.is_gt).then_inc(tern_own, 1)
                    nc.vector.tensor_scalar(negs[:], tern32[:], -0.25, None, ALU.is_lt).then_inc(tern_own, 1)
                    dve.wait_ge(tern_own, 3)
                    nc.vector.tensor_tensor(tern[:], tern[:], negs[:], ALU.subtract).then_inc(tern_own, 1)
            r_.clear()
            mv_done, rooted, xn_done, kept, turned, xT_done, logits = (r_.sem(n) for n in ("mv_done", "rooted", "xn_done", "kept", "turned", "xT_done", "logits"))
            top_done, summed, own = r_.sem("top_done"), r_.sem("summed"), r_.sem("own")
            X4 = X[:].rearrange("p (b t) d -> p b t d", t=NT)
            XN4 = XN[:].rearrange("p (b t) d -> p b t d", t=NT)
            OH4 = OH[:].rearrange("p (b t) e -> p b t e", t=NT)
            with nc.Fori(0, B) as b:
                with nc.Block() as block:
                    @block.vector
                    def _(dve):
                        chain = Tally(dve, own)
                        layernorm_stats(nc, dve, chain, [X4[:, b, t, :] for t in range(NT)], stats, mv)
                        nc.vector.tensor_scalar(mv[:, :, 1:2], mv[:, :, 1:2], LN_EPS, None, ALU.add).then_inc(mv_done, 1)
                        dve.wait_ge(rooted, 1)
                        chain.link(nc.vector.reciprocal(rstd[:], rstd[:]))
                        for t in range(NT):
                            nc.vector.tensor_scalar(xb[:, t, :], X4[:, b, t, :], mv[:, t, 0:1], rstd[:, t, :], ALU.subtract, ALU.mult).then_inc(xn_done, 1)
                        dve.wait_ge(logits, NT)
                        chain.link(nc.vector.tensor_copy(lg[:], psL[:]))
                        for t in range(NT):
                            chain.mark(nc.vector.max(m8[:, t, :], lg[:, t, :]))
                        chain.wait()
                        nc.vector.tensor_scalar(negm[:], m8[:, :, 0], -1.0, None, ALU.mult).then_inc(top_done, 1)
                        for t in range(NT):
                            chain.mark(nc.vector.max_index(i8[:, t, :], m8[:, t, :], lg[:, t, :]))
                        chain.wait()
                        chain.link(nc.vector.tensor_copy(idx[:], i8[:, :, 0:1]))
                        chain.mark(nc.vector.tensor_copy(XN4[:, b, :, D:D + 1], idx[:]))
                        for t in range(NT):
                            chain.mark(nc.vector.tensor_scalar(OH4[:, b, t, :], iota[:, 0:E], idx[:, t, :], None, ALU.is_equal))
                        dve.wait_ge(summed, NT)
                        chain.mark(nc.vector.reciprocal(XN4[:, b, :, D + 1:D + 2], den[:]))

                    @block.scalar
                    def _(act):
                        act.wait_ge(mv_done, 1)
                        nc.scalar.activation(rstd[:], mv[:, :, 1:2], ACT.Sqrt).then_inc(rooted, 1)
                        for t in range(NT):
                            act.wait_ge(turned, t + 1)
                            if t >= 2:
                                act.wait_ge(logits, t - 1)
                            nc.scalar.activation(xT[:, t % 2, :], psT[:, t % 2, :], ACT.Copy).then_inc(xT_done, 1)
                        act.wait_ge(top_done, 1)
                        for t in range(NT):
                            nc.scalar.activation(ex[:, t, :], lg[:, t, :], ACT.Exp, bias=negm[:, t:t + 1],
                                                 accum_out=den[:, t, :]).then_inc(summed, 1)

                    @block.gpsimd
                    def _(pool):
                        for t in range(NT):
                            pool.wait_ge(xn_done, t + 1)
                            nc.gpsimd.tensor_copy(XN4[:, b, t, 0:D], xb[:, t, :]).then_inc(kept, 1)

                    @block.tensor
                    def _(pe):
                        for t in range(NT + 1):
                            if t < NT:
                                pe.wait_ge(xn_done, t + 1)
                                if t >= 2:
                                    pe.wait_ge(xT_done, t - 1)
                                for c in range(DT):
                                    mm = nc.tensor.transpose(psT[:, t % 2, c * P:(c + 1) * P], xb[:, t, c * P:(c + 1) * P], ident[:])
                                mm.then_inc(turned, 1)
                            if t >= 1:
                                pe.wait_ge(xT_done, t)
                                for c in range(DT):
                                    mm = nc.tensor.matmul(psL[:, t - 1, :], xT[:, (t - 1) % 2, c * P:(c + 1) * P], router[:, c, :],
                                                          start=(c == 0), stop=(c == DT - 1))
                                mm.then_inc(logits, 1)
                r_.clear()

        XH = sb("XH", [P, 2, 2, D], F16)
        XST = sb("XST", [P, TILES, 2 * DT, P], F16)
        CMP = sb("CMP", [P, STEPS, E])
        incl = sb("incl", [P, E])
        excl = sb("excl", [P, E])
        rk = sb("rk", [P, E])
        place = sb("place", [P, TILES, E])
        posf = sb("posf", [P, TILES])
        GO = sb("GO", [P, TILES * E])
        oh2 = sb("oh2", [P, TILES, E])
        with ExitStack() as ctx2:
            s_ = Space(nc, ctx2, "sort")
            psR = s_.ps("psR", [P, TILES, E])
            psC = s_.ps("psC", [P, E])
            psX = s_.ps("psX", [P, 2, 2 * DT, P], F16)
            cum, ranked, own, pos_done, sent, back, hi_done, lo_done, turned, evac = (
                s_.sem(n) for n in ("cum", "ranked", "own", "pos_done", "sent", "back", "hi_done", "lo_done", "turned", "evac"))
            rowsT = rows.rearrange("(t p) d -> p t d", p=P)
            with nc.Block() as block:
                @block.vector
                def _(dve):
                    chain = Tally(dve, own)
                    nc.vector.memset(CUM[:, 0, :], 0.0).then_inc(cum, 1)
                    for t in range(TILES):
                        dve.wait_ge(cum, t + 1)
                        nc.vector.tensor_tensor(CUM[:, t + 1, :], CUM[:, t, :], OH[:, t, :], ALU.add).then_inc(cum, 1)
                    dve.wait_ge(ranked, 1)
                    chain.link(nc.vector.tensor_tensor_scan(incl[:], ones32[:], psC[:], 0.0, ALU.mult, ALU.add))
                    chain.link(nc.vector.tensor_tensor(excl[:], incl[:], psC[:], ALU.subtract))
                    chain.link(nc.vector.tensor_tensor(place[:], psR[:], excl[:].unsqueeze(1).broadcast_to([P, TILES, E]), ALU.add))
                    chain.link(nc.vector.tensor_tensor(place[:], place[:], OH[:], ALU.mult))
                    chain.link(nc.vector.tensor_reduce(posf[:], place[:], AX.X, ALU.add))
                    nc.vector.tensor_copy(POS[:], posf[:]).then_inc(pos_done, 1)
                    ends = CMP[:].rearrange("p k e -> p (k e)")[:, 0:E * TILES].rearrange("p (e t) -> p e t", t=TILES)
                    chain.link(nc.vector.tensor_tensor(ends, incl[:].unsqueeze(2).broadcast_to([P, E, TILES]),
                                                       tile_end[:].unsqueeze(1).broadcast_to([P, E, TILES]), ALU.is_gt))
                    chain.link(nc.vector.tensor_reduce(rk[:], ends, AX.X, ALU.add))
                    chain.link(nc.vector.tensor_tensor(rk[:], rk[:], iota[:, 0:E], ALU.add))
                    chain.link(nc.vector.tensor_tensor(CMP[:], rk[:].unsqueeze(1).broadcast_to([P, STEPS, E]),
                                                       iota[:, 0:STEPS].unsqueeze(2).broadcast_to([P, STEPS, E]), ALU.is_lt))
                    chain.link(nc.vector.tensor_reduce(Ef[:], CMP[:], AX.X, ALU.add))
                    chain.mark(nc.vector.tensor_copy(EI[:], Ef[:]))
                    chain.mark(nc.vector.tensor_tensor(TI[:], iota[:, 0:STEPS], Ef[:], ALU.subtract))
                    for t in range(TILES):
                        dve.wait_ge(hi_done, t + 1)
                        nc.vector.tensor_tensor(XH[:, t % 2, 1, :], XN[:, t, 0:D], XH[:, t % 2, 0, :], ALU.subtract).then_inc(lo_done, 1)
                    chain.link(nc.vector.tensor_tensor(oh2[:], iota[:, 0:E].unsqueeze(1).broadcast_to([P, TILES, E]),
                                                       XN[:, :, D:D + 1].broadcast_to([P, TILES, E]), ALU.is_equal))
                    chain.mark(nc.vector.tensor_tensor(GO[:].rearrange("p (t e) -> p t e", e=E), oh2[:],
                                                       XN[:, :, D + 1:D + 2].broadcast_to([P, TILES, E]), ALU.mult))

                @block.tensor
                def _(pe):
                    pe.wait_ge(cum, TILES + 1)
                    for t in range(TILES):
                        nc.tensor.matmul(psR[:, t, :], before[:], OH[:, t, :], start=True, stop=False)
                        nc.tensor.matmul(psR[:, t, :], ones[:], CUM[:, t, :], start=False, stop=True)
                    nc.tensor.matmul(psC[:], ones[:], CUM[:, TILES, :], start=True, stop=True).then_inc(ranked, 1)
                    for t in range(TILES):
                        pe.wait_ge(lo_done, t + 1)
                        if t >= 2:
                            pe.wait_ge(evac, t - 1)
                        for h in range(2):
                            for c in range(DT):
                                mm = nc.tensor.transpose(psX[:, t % 2, h * DT + c, :], XH[:, t % 2, h, c * P:(c + 1) * P], ident16[:])
                        mm.then_inc(turned, 1)

                @block.gpsimd
                def _(pool):
                    pool.wait_ge(pos_done, 1)
                    for t in range(TILES):
                        pool.indirect_dma_start(out=rows, out_offset=bass.IndirectOffsetOnAxis(ap=POS[:, t:t + 1], axis=0),
                                                in_=XN[:, t, :], in_offset=None).then_inc(sent, 16)

                @block.sync
                def _(sp):
                    sp.wait_ge(sent, 16 * TILES)
                    for g in range(4):
                        sp.dma_start(XN[:, 4 * g:4 * g + 4, :], rowsT[:, 4 * g:4 * g + 4, :]).then_inc(back, 16)

                @block.scalar
                def _(act):
                    for t in range(TILES + 1):
                        if t < TILES:
                            if t == 0:
                                act.wait_ge(back, 16 * 4)
                            if t >= 2:
                                act.wait_ge(turned, t - 1)
                            nc.scalar.activation(XH[:, t % 2, 0, :], XN[:, t, 0:D], ACT.Copy).then_inc(hi_done, 1)
                        if t >= 1:
                            act.wait_ge(turned, t)
                            nc.scalar.activation(XST[:, t - 1], psX[:, (t - 1) % 2], ACT.Copy).then_inc(evac, 1)
            s_.clear()

        YS = sb("YS", [P, TILES, D])
        with ExitStack() as ctx2:
            w_ = Space(nc, ctx2, "walk")
            mask = [w_.sb(f"mask{i}", [P, DT * D]) for i in range(2)]
            W = [w_.sb(f"W{i}", [P, DT, D], F16) for i in range(2)]
            g = w_.sb("g", [P, 1])
            psO = w_.ps("psO", [P, 2, D])
            mask_in = [w_.sem(f"mask_in{i}") for i in range(2)]
            zeroed, W_done, mm_done, g_done, acc_done = (w_.sem(n) for n in ("zeroed", "W_done", "mm_done", "g_done", "acc_done"))
            masks = ins["masksT"].rearrange("e (c p) o -> e p c o", p=P)
            PAIRS = (STEPS - 3) // 2
            with nc.Block() as block:
                @block.sync
                def _(sp):
                    def load_mask(k, j, first=False):
                        e = sp.value_load(EI[0:1, bass.ds(k, 1)], min_val=0, max_val=E - 1)
                        if not first:
                            sp.wait_ge(W_done, k - 1)
                        sp.dma_start(mask[j][:].rearrange("p (c o) -> p c o", c=DT), masks[e]).then_inc(mask_in[j], 16)

                    load_mask(0, 0, True)
                    load_mask(1, 1, True)
                    with sp.Fori(0, PAIRS) as i:
                        for j in range(2):
                            load_mask(i * 2 + (2 + j), j)
                    load_mask(STEPS - 1, 0)

                @block.vector
                def _(dve):
                    def build(n, j):
                        dve.wait_ge(mask_in[j], n * 16)
                        nc.vector.tensor_tensor(W[j][:].rearrange("p c o -> p (c o)"), mask[j][:], tern[:], ALU.mult).then_inc(W_done, 1)

                    def accumulate(k, j):
                        e = dve.value_load(EI[0:1, bass.ds(k, 1)], min_val=0, max_val=E - 1)
                        t = dve.value_load(TI[0:1, bass.ds(k, 1)], min_val=0, max_val=TILES - 1)
                        at = dve.snap(t * E + e, max_val=TILES * E - 1)
                        nc.vector.tensor_copy(g[:], GO[:, bass.ds(at, 1)]).then_inc(g_done, 1)
                        dve.wait_ge(g_done, k + 1)
                        dve.wait_ge(mm_done, k + 1)
                        y = YS[:, t, :]
                        nc.vector.scalar_tensor_tensor(out=y, in0=psO[:, j, :], scalar=g[:], in1=y, op0=ALU.mult, op1=ALU.add).then_inc(acc_done, 1)

                    nc.vector.memset(YS[:], 0.0).then_inc(zeroed, 1)
                    dve.wait_ge(zeroed, 1)
                    build(1, 0)
                    build(1, 1)
                    accumulate(0, 0)
                    with dve.Fori(0, PAIRS) as i:
                        for j in range(2):
                            dve.wait_ge(acc_done, i * 2 + (1 + j))
                            build(i + 2, j)
                            accumulate(i * 2 + (1 + j), 1 - j)
                    dve.wait_ge(acc_done, STEPS - 2)
                    build(STEPS // 2 + 1, 0)
                    accumulate(STEPS - 2, 1)
                    dve.wait_ge(acc_done, STEPS - 1)
                    accumulate(STEPS - 1, 0)

                @block.tensor
                def _(pe):
                    def product(k, j, first=False):
                        t = pe.value_load(TI[0:1, bass.ds(k, 1)], min_val=0, max_val=TILES - 1)
                        pe.wait_ge(W_done, k + 1)
                        if not first:
                            pe.wait_ge(acc_done, k - 1)
                        for q in range(2 * DT):
                            mm = nc.tensor.matmul(psO[:, j, :], XST[:, t, q, :], W[j][:, q % DT, :], start=(q == 0), stop=(q == 2 * DT - 1))
                        mm.then_inc(mm_done, 1)

                    product(0, 0, True)
                    product(1, 1, True)
                    with pe.Fori(0, PAIRS) as i:
                        for j in range(2):
                            product(i * 2 + (2 + j), j)
                    product(STEPS - 1, 0)
            w_.clear()

        with ExitStack() as ctx2:
            u_ = Space(nc, ctx2, "unsort")
            scaled, sent, got, added = (u_.sem(n) for n in ("scaled", "sent", "got", "added"))
            GR = 4
            resT = results.rearrange("(t p) d -> p t d", p=P)
            with nc.Block() as block:
                @block.vector
                def _(dve):
                    for q in range(TILES // GR):
                        y = YS[:, GR * q:GR * q + GR, :]
                        nc.vector.tensor_tensor(y, y, scale[:].unsqueeze(1).broadcast_to([P, GR, D]), ALU.mult).then_inc(scaled, 1)
                    for t in range(TILES):
                        dve.wait_ge(got, 16 * TILES)
                        nc.vector.tensor_tensor(X[:, t, :], X[:, t, :], XN[:, t, 0:D], ALU.add).then_inc(added, 1)

                @block.sync
                def _(sp):
                    for q in range(TILES // GR):
                        sp.wait_ge(scaled, q + 1)
                        sp.dma_start(resT[:, GR * q:GR * q + GR, :], YS[:, GR * q:GR * q + GR, :]).then_inc(sent, 16)

                @block.gpsimd
                def _(pool):
                    pool.wait_ge(sent, 16 * (TILES // GR))
                    for t in range(TILES):
                        pool.indirect_dma_start(out=XN[:, t, 0:D], out_offset=None, in_=results,
                                                in_offset=bass.IndirectOffsetOnAxis(ap=POS[:, t:t + 1], axis=0)).then_inc(got, 16)
            u_.clear()


def stage_attention(nc, X, ident, ident16, ins):
    H, HD = 32, 16
    CK = 2
    AXES, HALF = 2, HD // 4
    FQ = AXES * HALF
    HW = 4 * HD
    G, NG = 4, H // 4
    SCALE = HD ** -0.5
    PI = math.pi
    with ExitStack() as ctx:
        a_ = Space(nc, ctx, "att")
        sb = a_.sb
        Wq = sb("Wq", [P, DT, D])
        Wkv = sb("Wkv", [P, CK, 2 * D])
        Wout = sb("Wout", [P, DT, D])
        bout = sb("bout", [P, D])
        freq = sb("freq", [P, FQ])
        ctxT = sb("ctxT", [P, CK, S])
        xb = sb("xb", [P, NT, D])
        xT = sb("xT", [P, DT, S])
        pos = sb("pos", [P, NT, AXES])
        QS = [sb("QS", [P, H, P], F16), sb("KS", [P, H, P], F16)]
        rot = sb("rot", [P, D])
        t_cos = sb("t_cos", [P, D])
        t_sin = sb("t_sin", [P, D])
        V = sb("V", [P, NT, H, 32])
        QT = sb("QT", [P, H, S], F16)
        KT = sb("KT", [P, H, S], F16)
        with ExitStack() as ctx2:
            c_ = Space(nc, ctx2, "attc")
            loaded, consts, own = c_.sem("loaded"), c_.sem("consts"), c_.sem("own")
            with nc.Block() as block:
                @block.sync
                def _(sp):
                    sp.dma_start(Wq[:], ins["Wq"].rearrange("(c p) n -> p c n", p=P)).then_inc(loaded, 16)
                    sp.dma_start(Wkv[:], ins["Wkv"].rearrange("(c p) n -> p c n", p=P)).then_inc(loaded, 16)
                    sp.dma_start(Wout[:], ins["Wout"].rearrange("(c p) n -> p c n", p=P)).then_inc(loaded, 16)
                    sp.dma_start(bout[:], ins["bout"].partition_broadcast(P)).then_inc(loaded, 16)
                    sp.wait_ge(loaded, 64)

                @block.gpsimd
                def _(pool):
                    nc.gpsimd.memset(V[:], 0.0).then_inc(consts, 1)
                    pool.wait_ge(consts, 1)
                    nc.gpsimd.memset(V[:, :, :, HD:HD + 1], 1.0).then_inc(consts, 1)

                @block.vector
                def _(dve):
                    chain = Tally(dve, own)
                    for j in range(HALF):
                        chain.mark(nc.vector.memset(freq[:].rearrange("p (a f) -> p a f", f=HALF)[:, :, j:j + 1], 10000.0 ** (-j / HALF)))
                    chain.mark(nc.vector.memset(QS[0][:, :, HW:], 0.0))
                    chain.link(nc.vector.memset(QS[1][:, :, HW:], 0.0))
                    chain.mark(nc.vector.memset(QS[1][:, :, HW:HW + 2], 1.0))
            c_.clear()
        X4 = X[:].rearrange("p (b t) d -> p b t d", t=NT)
        posT = ins["pos"].rearrange("b (t p) a -> b p t a", p=P)

        with nc.Fori(0, B) as b:
            with ExitStack() as ctx2:
                p_ = Space(nc, ctx2, "qkv")
                stats = p_.sb("stats", [P, NT, 6])
                mv = p_.sb("mv", [P, NT, 2])
                rstd = p_.sb("rstd", [P, NT, 1])
                ang = p_.sb("ang", [P, 2, NT, FQ])
                turns = p_.sb("turns", [P, 2, NT, FQ], I32)
                turns_f = p_.sb("turns_f", [P, 2, NT, FQ])
                table = p_.sb("table", [P, 2, 2, NT, FQ])
                psX = p_.ps("psX", [P, 2, DT * P])
                psQ = p_.ps("psQ", [P, 3, D])
                psP = p_.ps("psP", [P, 3, 8, P], F16)
                ctx_in, pos_in, mv_done, rooted, xn_done, turned, xT_done = (
                    p_.sem(n) for n in ("ctx_in", "pos_in", "mv_done", "rooted", "xn_done", "turned", "xT_done"))
                proj, ang_done, sin_done, rot_done, hi_done, lo_done, v_done, parts, evac_a, evac_v, own = (
                    p_.sem(n) for n in ("proj", "ang_done", "sin_done", "rot_done", "hi_done", "lo_done", "v_done", "parts", "evac_a", "evac_v", "own"))
                dst = (QT, KT)
                hi_of = (lambda s: s[:, :, 0:2 * HD].rearrange("p h (r d) -> p h r d", r=2),
                         lambda s: s[:, :, 0:HW].rearrange("p h (r w d) -> p h r w d", r=2, w=2)[:, :, :, 0, :])
                lo_of = (lambda s: s[:, :, 2 * HD:HW].rearrange("p h (r d) -> p h r d", r=2),
                         lambda s: s[:, :, 0:HW].rearrange("p h (r w d) -> p h r w d", r=2, w=2)[:, :, :, 1, :])
                with nc.Block() as block:
                    @block.sync
                    def _(sp):
                        sp.dma_start(ctxT[:], ins["ctxT"][b].rearrange("(c p) s -> p c s", p=P)).then_inc(ctx_in, 16)
                        sp.dma_start(pos[:], posT[b]).then_inc(pos_in, 16)

                    @block.tensor
                    def _(pe):
                        def project(t):
                            rows = slice(t * P, (t + 1) * P)
                            if t >= 1:
                                pe.wait_ge(rot_done, 2 * t - 1)
                            for c in range(DT):
                                mm = nc.tensor.matmul(psQ[:, 0, :], xT[:, c, rows], Wq[:, c, :], start=(c == 0), stop=(c == DT - 1))
                            mm.then_inc(proj, 1)
                            if t >= 1:
                                pe.wait_ge(rot_done, 2 * t)
                            for c in range(CK):
                                mm = nc.tensor.matmul(psQ[:, 1, :], ctxT[:, c, rows], Wkv[:, c, 0:D], start=(c == 0), stop=(c == CK - 1))
                            mm.then_inc(proj, 1)
                            if t >= 1:
                                pe.wait_ge(v_done, t)
                            for c in range(CK):
                                mm = nc.tensor.matmul(psQ[:, 2, :], ctxT[:, c, rows], Wkv[:, c, D:], start=(c == 0), stop=(c == CK - 1))
                            mm.then_inc(proj, 1)

                        def turn_parts(t):
                            for s in range(2):
                                pe.wait_ge(hi_done, 2 * t + s + 1)
                                pe.wait_ge(lo_done, 2 * t + s + 1)
                                for q in range(4):
                                    i = (2 * t + s) * 4 + q
                                    if i >= 3:
                                        j = i - 3
                                        pe.wait_ge(evac_v if j % 2 else evac_a, j // 2 + 1)
                                    for h in range(8):
                                        mm = nc.tensor.transpose(psP[:, i % 3, h, :], QS[s][:, 8 * q + h, :], ident16[:])
                                    mm.then_inc(parts, 1)

                        for t in range(NT):
                            pe.wait_ge(xn_done, t + 1)
                            if t >= 2:
                                pe.wait_ge(xT_done, t - 1)
                            for c in range(DT):
                                mm = nc.tensor.transpose(psX[:, t % 2, c * P:(c + 1) * P], xb[:, t, c * P:(c + 1) * P], ident[:])
                            mm.then_inc(turned, 1)
                        pe.wait_ge(ctx_in, 16)
                        for t in range(NT + 1):
                            if t < NT:
                                pe.wait_ge(xT_done, t + 1)
                                project(t)
                            if t >= 1:
                                turn_parts(t - 1)

                    @block.scalar
                    def _(act):
                        act.wait_ge(mv_done, 1)
                        nc.scalar.activation(rstd[:], mv[:, :, 1:2], ACT.Sqrt).then_inc(rooted, 1)
                        act.wait_ge(ang_done, 1)
                        nc.scalar.activation(table[:, 1], ang[:], ACT.Sin).then_inc(sin_done, 1)
                        for t in range(NT):
                            act.wait_ge(turned, t + 1)
                            nc.scalar.activation(xT[:, :, t * P:(t + 1) * P], psX[:, t % 2, :].rearrange("p (c k) -> p c k", c=DT),
                                                 ACT.Copy).then_inc(xT_done, 1)
                        for t in range(NT + 1):
                            for s in range(2):
                                if t >= 1:
                                    for q in (0, 2):
                                        i = (2 * (t - 1) + s) * 4 + q
                                        act.wait_ge(parts, i + 1)
                                        nc.scalar.activation(dst[s][:, 8 * q:8 * q + 8, (t - 1) * P:t * P], psP[:, i % 3], ACT.Copy).then_inc(evac_a, 1)
                                if t < NT:
                                    act.wait_ge(rot_done, 2 * t + s + 1)
                                    if t >= 1:
                                        act.wait_ge(parts, (2 * (t - 1) + s + 1) * 4)
                                    nc.scalar.activation(hi_of[s](QS[s]), rot[:].rearrange("p (h d) -> p h d", h=H).unsqueeze(2).broadcast_to([P, H, 2, HD]),
                                                         ACT.Copy).then_inc(hi_done, 1)
                            if t < NT:
                                act.wait_ge(proj, 3 * t + 3)
                                nc.scalar.activation(V[:, t, :, 0:HD], psQ[:, 2, :].rearrange("p (h d) -> p h d", h=H), ACT.Copy).then_inc(v_done, 1)

                    @block.gpsimd
                    def _(pool):
                        for t in range(NT):
                            for s in range(2):
                                pool.wait_ge(hi_done, 2 * t + s + 1)
                                nc.gpsimd.tensor_tensor(lo_of[s](QS[s]), rot[:].rearrange("p (h d) -> p h d", h=H).unsqueeze(2).broadcast_to([P, H, 2, HD]),
                                                        hi_of[s](QS[s]), ALU.subtract).then_inc(lo_done, 1)

                    @block.vector
                    def _(dve):
                        chain = Tally(dve, own)
                        layernorm_stats(nc, dve, chain, [X4[:, b, t, :] for t in range(NT)], stats, mv)
                        nc.vector.tensor_scalar(mv[:, :, 1:2], mv[:, :, 1:2], LN_EPS, None, ALU.add).then_inc(mv_done, 1)
                        dve.wait_ge(pos_in, 16)
                        chain.link(nc.vector.tensor_tensor(ang[:, 1].rearrange("p t (a f) -> p t a f", f=HALF),
                                                           pos[:].unsqueeze(3).broadcast_to([P, NT, AXES, HALF]),
                                                           freq[:].rearrange("p (a f) -> p a f", f=HALF).unsqueeze(1).broadcast_to([P, NT, AXES, HALF]), ALU.mult))
                        chain.link(nc.vector.tensor_scalar(ang[:, 0], ang[:, 1], PI / 2, None, ALU.add))
                        chain.link(nc.vector.tensor_scalar(turns[:], ang[:], 1 / (2 * PI), None, ALU.mult))
                        chain.link(nc.vector.tensor_copy(turns_f[:], turns[:]))
                        nc.vector.scalar_tensor_tensor(out=ang[:], in0=turns_f[:], scalar=-2 * PI, in1=ang[:], op0=ALU.mult, op1=ALU.add).then_inc(ang_done, 1)
                        dve.wait_ge(rooted, 1)
                        chain.link(nc.vector.reciprocal(rstd[:], rstd[:]))
                        for t in range(NT):
                            nc.vector.tensor_scalar(xb[:, t, :], X4[:, b, t, :], mv[:, t, 0:1], rstd[:, t, :], ALU.subtract, ALU.mult).then_inc(xn_done, 1)
                        dve.wait_ge(sin_done, 1)
                        chain.link(nc.vector.tensor_scalar(table[:, 0], table[:, 1], SCALE, None, ALU.mult))
                        for t in range(NT + 1):
                            for s in range(2):
                                if t < NT:
                                    dve.wait_ge(proj, 3 * t + s + 1)
                                    src = psQ[:, s, :].rearrange("p (h a w) -> p h a w", h=H, w=2)
                                    cos, sin = (table[:, s, w, t, :].unsqueeze(1).unsqueeze(3).broadcast_to([P, H, FQ, 2]) for w in range(2))
                                    chain.mark(nc.vector.tensor_tensor(t_cos[:].rearrange("p (h a w) -> p h a w", h=H, w=2), src, cos, ALU.mult))
                                    chain.link(nc.vector.tensor_tensor(t_sin[:].rearrange("p (h a w) -> p h a w", h=H, w=2), src, sin, ALU.mult))
                                    if 2 * t + s >= 1:
                                        dve.wait_ge(lo_done, 2 * t + s)
                                    c2, s2, r2 = (x[:].rearrange("p (a w) -> p a w", w=2) for x in (t_cos, t_sin, rot))
                                    chain.link(nc.vector.tensor_tensor(r2[:, :, 0], c2[:, :, 0], s2[:, :, 1], ALU.subtract))
                                    nc.vector.tensor_tensor(r2[:, :, 1], s2[:, :, 0], c2[:, :, 1], ALU.add).then_inc(rot_done, 1)
                                    dve.wait_ge(rot_done, 2 * t + s + 1)
                                if t >= 1:
                                    for q in (1, 3):
                                        i = (2 * (t - 1) + s) * 4 + q
                                        dve.wait_ge(parts, i + 1)
                                        nc.vector.tensor_copy(dst[s][:, 8 * q:8 * q + 8, (t - 1) * P:t * P], psP[:, i % 3]).then_inc(evac_v, 1)
                p_.clear()

            with ExitStack() as ctx2:
                s_ = Space(nc, ctx2, "soft")
                NP_ = 4
                Pr = s_.sb("Pr", [P, NP_, 2, S])
                mx = s_.sb("mx", [P, 3, NT, G])
                nm = s_.sb("nm", [P, 3, NT, 2 * G], F16)
                nmT = s_.sb("nmT", [2 * G, 3, S], F16)
                OT = s_.sb("OT", [P, S])
                rec = s_.sb("rec", [P, NT, G])
                psT = s_.ps("psT", [P, 2, 2, S])
                psS = s_.ps("psS", [P, 2, S])
                psO = s_.ps("psO", [P, S])
                psM = s_.ps("psM", [P, S])
                scored, maxed, nm_done, nm_turned, nmT_done, st_done, exp_done, av_done, ot_done, o_turned, o_done, own = (
                    s_.sem(n) for n in ("scored", "maxed", "nm_done", "nm_turned", "nmT_done", "st_done", "exp_done", "av_done", "ot_done", "o_turned", "o_done", "own"))
                rows_in = [s_.sem(f"rows_in{i}") for i in range(3)]
                LAG = 2
                with nc.Block() as block:
                    @block.tensor
                    def _(pe):
                        def score(g, j, qt):
                            i = (g * G + j) * NT + qt
                            if i >= 2:
                                pe.wait_ge(maxed, i - 1)
                            nc.tensor.matmul(psS[:, i % 2, :], QT[:, g * G + j, qt * P:(qt + 1) * P], KT[:, g * G + j, :],
                                             start=True, stop=True).then_inc(scored, 1)

                        def turn_maxima(g):
                            pe.wait_ge(nm_done, g + 1)
                            if g >= LAG + 1:
                                pe.wait_ge(o_done, g - LAG)
                            elif g >= 1:
                                pe.wait_ge(nmT_done, g)
                            v = psM[:, 0:S // 2].bitcast(F16)
                            for qt in range(NT):
                                mm = nc.tensor.transpose(v[0:2 * G, qt * P:(qt + 1) * P], nm[:, g % 3, qt, :], ident16[:])
                            mm.then_inc(nm_turned, 1)

                        def key_scores(g, kt, pair):
                            i = (g * NT + kt) * 2 + pair
                            if kt == 0 and pair == 0:
                                pe.wait_ge(rows_in[g % 3], 32 * (g // 3 + 1))
                            if i >= 2:
                                pe.wait_ge(exp_done, i - 1)
                            for w in range(2):
                                h = g * G + 2 * pair + w
                                mm = nc.tensor.matmul(psT[:, i % 2, w, :], KT[:, h, kt * P:(kt + 1) * P], QT[:, h, :], start=True, stop=True)
                            mm.then_inc(st_done, 1)

                        def values(g, kt):
                            i = (g * NT + kt) * 2
                            pe.wait_ge(exp_done, i + 2)
                            if kt == 0 and g >= 1:
                                pe.wait_ge(ot_done, g)
                            for j in range(G):
                                mm = nc.tensor.matmul(psO[32 * j:32 * j + 32, :], V[:, kt, g * G + j, :], Pr[:, (i + j // 2) % NP_, j % 2, :],
                                                      start=(kt == 0), stop=(kt == NT - 1))
                            mm.then_inc(av_done, 1)

                        def turn_results(g):
                            pe.wait_ge(ot_done, g + 1)
                            if g + LAG < NG:
                                pe.wait_ge(nmT_done, g + LAG + 1)
                            else:
                                pe.wait_ge(o_done, g)
                            for qt in range(NT):
                                mm = nc.tensor.transpose(psM[:, qt * P:(qt + 1) * P], OT[:, qt * P:(qt + 1) * P], ident[:])
                            mm.then_inc(o_turned, 1)

                        for g in range(-LAG, NG + 1):
                            ahead, here = g + LAG < NG, 0 <= g < NG
                            for kt in range(NT):
                                if ahead:
                                    score(g + LAG, kt, 0)
                                if here:
                                    key_scores(g, kt, 0)
                                if ahead:
                                    score(g + LAG, kt, 1)
                                if here:
                                    key_scores(g, kt, 1)
                                if ahead:
                                    score(g + LAG, kt, 2)
                                if here and kt >= 1:
                                    values(g, kt - 1)
                                elif g >= 1 and kt == 0:
                                    values(g - 1, NT - 1)
                                if ahead:
                                    score(g + LAG, kt, 3)
                                if kt == 0 and 0 <= g + LAG - 1 < NG:
                                    turn_maxima(g + LAG - 1)
                                if kt == 1 and g >= 1:
                                    turn_results(g - 1)

                    @block.vector
                    def _(dve):
                        chain = Tally(dve, own)

                        def keep_results(g):
                            dve.wait_ge(av_done, NT * (g + 1))
                            if g >= 1:
                                dve.wait_ge(o_turned, g)
                            nc.vector.tensor_copy(OT[:], psO[:]).then_inc(ot_done, 1)

                        def normalise(g):
                            dve.wait_ge(o_turned, g + 1)
                            o = psM[:].rearrange("p (q h d) -> p q h d", q=NT, h=G)
                            chain.link(nc.vector.reciprocal(rec[:], o[:, :, :, HD]))
                            nc.vector.tensor_tensor(xb[:].rearrange("p q (h d) -> p q h d", d=HD)[:, :, G * g:G * g + G, :], o[:, :, :, 0:HD],
                                                    rec[:].unsqueeze(3).broadcast_to([P, NT, G, HD]), ALU.mult).then_inc(o_done, 1)

                        for g in range(-LAG, NG + 1):
                            m = g + LAG
                            for n in range(G * NT):
                                if m < NG:
                                    i = m * G * NT + n
                                    j, qt = i // NT % G, i % NT
                                    dve.wait_ge(scored, i + 1)
                                    nc.vector.tensor_reduce(mx[:, m % 3, qt, j:j + 1], psS[:, i % 2, :], AX.X, ALU.max).then_inc(maxed, 1)
                                if g >= 1 and n == 4:
                                    keep_results(g - 1)
                                if g >= 1 and n == 9:
                                    normalise(g - 1)
                            if m < NG:
                                dve.wait_ge(maxed, (m + 1) * G * NT)
                                if m >= 3:
                                    dve.wait_ge(nm_turned, m - 2)
                                chain.link(nc.vector.tensor_scalar(nm[:, m % 3, :, 0:G], mx[:, m % 3], -1.0, None, ALU.mult))
                                nc.vector.scalar_tensor_tensor(out=nm[:, m % 3, :, G:], in0=mx[:, m % 3], scalar=-1.0, in1=nm[:, m % 3, :, 0:G],
                                                               op0=ALU.mult, op1=ALU.subtract).then_inc(nm_done, 1)

                    @block.scalar
                    def _(act):
                        def send_maxima(g):
                            act.wait_ge(nm_turned, g + 1)
                            if g >= 3:
                                act.wait_ge(rows_in[g % 3], 32 * (g // 3))
                            nc.scalar.activation(nmT[:, g % 3, :], psM[:, 0:S // 2].bitcast(F16)[0:2 * G, :], ACT.Copy).then_inc(nmT_done, 1)

                        for g in range(-LAG, NG):
                            for n in range(2 * NT):
                                if g >= 0:
                                    i = g * NT * 2 + n
                                    act.wait_ge(st_done, i + 1)
                                    if i >= NP_:
                                        act.wait_ge(av_done, (i - NP_) // 2 + 1)
                                    nc.scalar.activation(Pr[:, i % NP_], psT[:, i % 2], ACT.Exp).then_inc(exp_done, 1)
                                if n == 2 and 0 <= g + LAG - 1 < NG:
                                    send_maxima(g + LAG - 1)

                    @block.sync
                    def _(sp):
                        for g in range(NG):
                            sp.wait_ge(nmT_done, g + 1)
                            for w in range(2):
                                sp.dma_start(QT[HW + w:HW + w + 1, G * g:G * g + G, :], nmT[G * w:G * w + G, g % 3, :]).then_inc(rows_in[g % 3], 16)
                s_.clear()

            with ExitStack() as ctx2:
                o_ = Space(nc, ctx2, "wout")
                psX = o_.ps("psX", [P, 2, DT * P])
                psY = o_.ps("psY", [P, 2, D])
                turned, xT_done, proj, biased, added = (o_.sem(n) for n in ("turned", "xT_done", "proj", "biased", "added"))
                with nc.Block() as block:
                    @block.tensor
                    def _(pe):
                        for t in range(NT + 1):
                            if t < NT:
                                if t >= 2:
                                    pe.wait_ge(xT_done, t - 1)
                                for c in range(DT):
                                    mm = nc.tensor.transpose(psX[:, t % 2, c * P:(c + 1) * P], xb[:, t, c * P:(c + 1) * P], ident[:])
                                mm.then_inc(turned, 1)
                            if t >= 1:
                                pe.wait_ge(xT_done, t)
                                if t >= 3:
                                    pe.wait_ge(added, t - 2)
                                for c in range(DT):
                                    mm = nc.tensor.matmul(psY[:, (t - 1) % 2, :], xT[:, c, (t - 1) * P:t * P], Wout[:, c, :], start=(c == 0), stop=(c == DT - 1))
                                mm.then_inc(proj, 1)

                    @block.scalar
                    def _(act):
                        for t in range(NT):
                            act.wait_ge(turned, t + 1)
                            nc.scalar.activation(xT[:, :, t * P:(t + 1) * P], psX[:, t % 2, :].rearrange("p (c k) -> p c k", c=DT),
                                                 ACT.Copy).then_inc(xT_done, 1)

                    @block.gpsimd
                    def _(pool):
                        for t in range(NT):
                            nc.gpsimd.tensor_tensor(X4[:, b, t, :], X4[:, b, t, :], bout[:], ALU.add).then_inc(biased, 1)

                    @block.vector
                    def _(dve):
                        for t in range(NT):
                            dve.wait_ge(biased, t + 1)
                            dve.wait_ge(proj, t + 1)
                            nc.vector.tensor_tensor(X4[:, b, t, :], X4[:, b, t, :], psY[:, t % 2, :], ALU.add).then_inc(added, 1)
                o_.clear()


def stage_mlp(nc, X, ident, ins):
    JT = 11
    INNER = JT * P
    GU = 2 * INNER
    PER = 8
    EPS = 1e-6
    with ExitStack() as ctx:
        m_ = Space(nc, ctx, "mlp")
        sb = m_.sb
        Vgu = sb("Vgu", [P, DT, GU], F16)
        Wd = sb("Wd", [P, JT, D])
        s_gu16 = sb("s_gu16", [P, 2 * JT, DT], F16)
        s_gu = sb("s_gu", [P, 2 * JT, DT])
        with ExitStack() as ctx2:
            d_ = Space(nc, ctx2, "deq")
            words = d_.sb("words", [P, DT, GU], I32)
            shift = d_.sb("shift", [P, 1], I32)
            t1 = [d_.sb(f"t1{i}", [P, GU], I32) for i in range(2)]
            t2 = d_.sb("t2", [P, GU], I32)
            s_d = d_.sb("s_d", [P, JT * D], F16)
            consts, own, vals, freed = d_.sem("consts"), d_.sem("own"), d_.sem("vals"), d_.sem("freed")
            chunk_in = [d_.sem(f"chunk_in{i}") for i in range(DT)]
            down_in, scales_in = d_.sem("down_in"), d_.sem("scales_in")
            with nc.Block() as block:
                @block.sync
                def _(sp):
                    for g in range(DT):
                        for k in range(PER):
                            sp.dma_start(words[k:P:PER, g, :], ins["gate_upT"][g * 16:(g + 1) * 16, :]).then_inc(chunk_in[g], 16)

                @block.scalar
                def _(act):
                    for k in range(PER):
                        act.dma_start(Wd[k:P:PER].bitcast(I32), ins["downT"].rearrange("(g j) o -> j g o", j=P // PER)).then_inc(down_in, 16)
                    act.dma_start(s_d[:], ins["down_scales"].rearrange("g o -> (g o)").partition_broadcast(P)).then_inc(down_in, 16)
                    act.dma_start(s_gu16[:], ins["gate_up_scalesT"].rearrange("(j p) g -> p j g", p=P)).then_inc(scales_in, 16)
                    for g in range(DT):
                        act.wait_ge(vals, g + 1)
                        half = t1[g % 2][:].bitcast(F16).rearrange("p (o w) -> p o w", w=2)[:, :, 0]
                        nc.scalar.activation(Vgu[:, g, :], half, ACT.Copy, scale=2.0 ** 14).then_inc(freed, 1)

                @block.gpsimd
                def _(pool):
                    nc.gpsimd.iota(shift[:], [[0, 1]], base=0, channel_multiplier=4).then_inc(consts, 1)

                @block.vector
                def _(dve):
                    chain = Tally(dve, own)
                    dve.wait_ge(consts, 1)
                    chain.link(nc.vector.tensor_scalar(shift[:], shift[:], 4 * PER - 1, None, ALU.bitwise_and))

                    def codes(w, t, signal=None):
                        chain.mark(nc.vector.tensor_scalar(t[:], w, shift[:], 7, ALU.logical_shift_right, ALU.bitwise_and))
                        chain.link(nc.vector.tensor_scalar(t2[:], w, shift[:], 8, ALU.logical_shift_right, ALU.bitwise_and))
                        chain.link(nc.vector.scalar_tensor_tensor(out=t[:], in0=t2[:], scalar=3, in1=t[:], op0=ALU.logical_shift_left, op1=ALU.bitwise_or))
                        last = nc.vector.tensor_scalar(t[:], t[:], 9, None, ALU.logical_shift_left)
                        if signal is None:
                            chain.link(last)
                        else:
                            last.then_inc(signal, 1)

                    for g in range(DT):
                        dve.wait_ge(chunk_in[g], 16 * PER)
                        if g >= 2:
                            dve.wait_ge(freed, g - 1)
                        codes(words[:, g, :], t1[g % 2], vals)
                    dve.wait_ge(scales_in, 16)
                    chain.mark(nc.vector.tensor_copy(s_gu[:], s_gu16[:]))
                    dve.wait_ge(down_in, 16 * (PER + 1))
                    dve.wait_ge(freed, DT)
                    flat_d = Wd[:].rearrange("p j o -> p (j o)")
                    for g in range(JT * D // GU):
                        w, s, t = flat_d[:, g * GU:(g + 1) * GU], s_d[:, g * GU:(g + 1) * GU], t1[g % 2]
                        codes(w.bitcast(I32), t)
                        half = t[:].bitcast(F16).rearrange("p (o w) -> p o w", w=2)[:, :, 0]
                        chain.link(nc.vector.scalar_tensor_tensor(out=w, in0=half, scalar=2.0 ** 14, in1=s, op0=ALU.mult, op1=ALU.mult))
            d_.clear()

        xb = sb("xb", [P, NT, D])
        xh = sb("xh", [P, DT, S], F16)
        xl = sb("xl", [P, DT, S], F16)
        first = sb("first", [P, 2, S])
        third = sb("third", [P, 2, S])
        both = sb("both", [P, 2, S])
        sg = sb("sg", [P, 2, S])
        hT = sb("hT", [P, 3, S])
        sq = sb("sq", [P, D])
        ss = sb("ss", [P, NT])
        stats = sb("stats", [P, NT, 6])
        mv = sb("mv", [P, NT, 2])
        rstd = sb("rstd", [P, NT, 1])
        psQ = m_.ps("psQ", [P, DT, S])
        psD = m_.ps("psD", [P, NT, D])
        X4 = X[:].rearrange("p (b t) d -> p b t d", t=NT)
        mv_done, rooted, xn_done, turned, xh_done, xl_done, grp, ev_a, ev_v, summed, silu_done, h_done, down = (
            m_.sem(n) for n in ("mv_done", "rooted", "xn_done", "turned", "xh_done", "xl_done", "grp", "ev_a", "ev_v", "summed",
                                "silu_done", "h_done", "down"))
        final, squared, ms_done, root2, added, own = (m_.sem(n) for n in ("final", "squared", "ms_done", "root2", "added", "own"))
        with nc.Fori(0, B) as b:
            with nc.Block() as block:
                @block.vector
                def _(dve):
                    chain = Tally(dve, own)
                    layernorm_stats(nc, dve, chain, [X4[:, b, t, :] for t in range(NT)], stats, mv)
                    nc.vector.tensor_scalar(mv[:, :, 1:2], mv[:, :, 1:2], LN_EPS, None, ALU.add).then_inc(mv_done, 1)
                    dve.wait_ge(rooted, 1)
                    chain.link(nc.vector.reciprocal(rstd[:], rstd[:]))
                    for t in range(NT):
                        nc.vector.tensor_scalar(xb[:, t, :], X4[:, b, t, :], mv[:, t, 0:1], rstd[:, t, :], ALU.subtract, ALU.mult).then_inc(xn_done, 1)
                    for t in range(NT):
                        dve.wait_ge(xh_done, t + 1)
                        cols = slice(t * P, (t + 1) * P)
                        nc.vector.tensor_tensor(xl[:, :, cols], psD[:, t % 2, :].rearrange("p (c k) -> p c k", c=DT), xh[:, :, cols],
                                                ALU.subtract).then_inc(xl_done, 1)

                    def gated(j):
                        dve.wait_ge(silu_done, j + 1)
                        dve.wait_ge(summed, 2 * j + 2)
                        if j >= 3:
                            dve.wait_ge(down, j - 2)
                        nc.vector.tensor_tensor(hT[:, j % 3, :], sg[:, j % 2, :], both[:, 1, :], ALU.mult).then_inc(h_done, 1)

                    for u in range(2 * JT):
                        j, w = divmod(u, 2)
                        row = w * JT + j
                        for n, g in enumerate((1, 3)):
                            dve.wait_ge(grp, DT * u + g + 1)
                            if n == 0:
                                dve.wait_ge(ev_a, 2 * u + 1)
                            else:
                                dve.wait_ge(ev_v, 2 * u + 1)
                            nc.vector.scalar_tensor_tensor(out=first[:, w, :], in0=psQ[:, g, :], scalar=s_gu[:, row, g:g + 1], in1=first[:, w, :],
                                                           op0=ALU.mult, op1=ALU.add).then_inc(ev_v, 1)
                        if w == 0 and j >= 1:
                            gated(j - 1)
                    gated(JT - 1)
                    for t in range(NT):
                        dve.wait_ge(squared, t + 1)
                        nc.vector.tensor_scalar(ss[:, t:t + 1], ss[:, t:t + 1], 1.0 / D, EPS, ALU.mult, ALU.add).then_inc(ms_done, 1)
                    for t in range(NT):
                        dve.wait_ge(root2, t + 1)
                        chain.link(nc.vector.reciprocal(ss[:, t:t + 1], ss[:, t:t + 1]))
                        nc.vector.scalar_tensor_tensor(out=X4[:, b, t, :], in0=psD[:, t, :], scalar=ss[:, t:t + 1], in1=X4[:, b, t, :],
                                                       op0=ALU.mult, op1=ALU.add).then_inc(added, 1)

                @block.scalar
                def _(act):
                    act.wait_ge(mv_done, 1)
                    nc.scalar.activation(rstd[:], mv[:, :, 1:2], ACT.Sqrt).then_inc(rooted, 1)
                    for t in range(NT):
                        act.wait_ge(turned, t + 1)
                        nc.scalar.activation(xh[:, :, t * P:(t + 1) * P], psD[:, t % 2, :].rearrange("p (c k) -> p c k", c=DT), ACT.Copy).then_inc(xh_done, 1)
                    for u in range(2 * JT):
                        j, w = divmod(u, 2)
                        row = w * JT + j
                        for g, dst in ((0, first), (2, third)):
                            act.wait_ge(grp, DT * u + g + 1)
                            if g == 0 and u >= 2:
                                act.wait_ge(summed, u - 1)
                            nc.scalar.activation(dst[:, w, :], psQ[:, g, :], ACT.Copy, scale=s_gu[:, row, g:g + 1]).then_inc(ev_a, 1)
                        if w == 1:
                            act.wait_ge(summed, 2 * j + 1)
                            if j >= 2:
                                act.wait_ge(h_done, j - 1)
                            nc.scalar.activation(sg[:, j % 2, :], both[:, 0, :], ACT.Silu).then_inc(silu_done, 1)
                    for t in range(NT):
                        act.wait_ge(final, t + 1)
                        if t >= 1:
                            act.wait_ge(squared, t)
                        nc.scalar.activation(sq[:], psD[:, t, :], ACT.Square, accum_out=ss[:, t:t + 1]).then_inc(squared, 1)
                    for t in range(NT):
                        act.wait_ge(ms_done, t + 1)
                        nc.scalar.activation(ss[:, t:t + 1], ss[:, t:t + 1], ACT.Sqrt).then_inc(root2, 1)

                @block.gpsimd
                def _(pool):
                    for u in range(2 * JT):
                        j, w = divmod(u, 2)
                        pool.wait_ge(ev_a, 2 * u + 2)
                        pool.wait_ge(ev_v, 2 * u + 2)
                        if j >= 1:
                            pool.wait_ge(h_done if w else silu_done, j)
                        nc.gpsimd.tensor_tensor(both[:, w, :], first[:, w, :], third[:, w, :], ALU.add).then_inc(summed, 1)

                @block.tensor
                def _(pe):
                    for t in range(NT):
                        pe.wait_ge(xn_done, t + 1)
                        if t >= 2:
                            pe.wait_ge(xl_done, t - 1)
                        for c in range(DT):
                            mm = nc.tensor.transpose(psD[:, t % 2, c * P:(c + 1) * P], xb[:, t, c * P:(c + 1) * P], ident[:])
                        mm.then_inc(turned, 1)
                    pe.wait_ge(xl_done, NT)
                    for j in range(JT + 1):
                        for w in range(2 if j < JT else 0):
                            u = 2 * j + w
                            cols = slice(w * INNER + j * P, w * INNER + (j + 1) * P)
                            for g in range(DT):
                                if u >= 1:
                                    pe.wait_ge(ev_v if g % 2 else ev_a, 2 * (u - 1) + g // 2 + 1)
                                nc.tensor.matmul(psQ[:, g, :], Vgu[:, g, cols], xh[:, g, :], start=True, stop=False)
                                nc.tensor.matmul(psQ[:, g, :], Vgu[:, g, cols], xl[:, g, :], start=False, stop=True).then_inc(grp, 1)
                        if j >= 1:
                            i = j - 1
                            pe.wait_ge(h_done, i + 1)
                            for t in range(NT):
                                mm = nc.tensor.matmul(psD[:, t, :], hT[:, i % 3, t * P:(t + 1) * P], Wd[:, i, :], start=(i == 0), stop=(i == JT - 1))
                                if i == JT - 1:
                                    mm.then_inc(final, 1)
                            if i < JT - 1:
                                mm.then_inc(down, 1)
            m_.clear()


LAYOUT = {
    "x": ("x", None),
    "ctxT": ("ctx_1024", (0, 2, 1)),
    "pos": ("fside_BxSx2_0", None),
    "in_proj_wT": ("L0_xattn_in_proj_w", (1, 0)),
    "x_proj_wT": ("L0_xattn_x_proj_w", (1, 0)),
    "dt_proj_wT": ("L0_xattn_dt_proj_w", (1, 0)),
    "A_log": ("L0_xattn_A_log", None),
    "ternaryT": ("L0_ffn_weight", (1, 0)),
    "out_scale": ("L0_ffn_scale", None),
    "masksT": ("L0_ffn_expert_masks", (0, 2, 1)),
    "routerT": ("L0_ffn_router_w", (1, 0)),
    "Wq": ("L1_xattn_Wq", None),
    "Wkv": ("L1_xattn_Wkv", None),
    "Wout": ("L1_xattn_Wout", None),
    "bout": ("L1_xattn_bout", None),
    "gate_upT": ("L1_ffn_gate_up_packed", (1, 0)),
    "gate_up_scalesT": ("L1_ffn_gate_up_scales", (1, 0)),
    "downT": ("L1_ffn_down_packed", (1, 0)),
    "down_scales": ("L1_ffn_down_scales", None),
}


CHANNELS = ("L0_xattn_conv_w", "L0_xattn_conv_b", "L0_xattn_dt_proj_b", "L0_xattn_D")


def layouts(inputs):
    import numpy as np

    arrays = {}
    for name, (source, axes) in LAYOUT.items():
        a = np.asarray(inputs[source])
        arrays[name] = np.ascontiguousarray(a if axes is None else a.transpose(axes))
    columns = [np.asarray(inputs[c]) for c in CHANNELS]
    arrays["channels"] = np.concatenate([c if c.ndim == 2 else c[:, None] for c in columns], axis=1)
    return arrays


def program(nc, ins, out):
    with ExitStack() as ctx:
        X = ctx.enter_context(nc.sbuf_tensor("X", [P, TILES, D], F32))
        ident = ctx.enter_context(nc.sbuf_tensor("ident", [P, P], F32))
        ident16 = ctx.enter_context(nc.sbuf_tensor("ident16", [P, P], F16))
        id_done = [ctx.enter_context(nc.semaphore(f"id_done{i}")) for i in range(2)]
        stored = ctx.enter_context(nc.semaphore("stored"))
        bc_rows = nc.dram_tensor("bc_rows", (B, 32, S), F32).ap()
        sorted_rows = nc.dram_tensor("sorted_rows", (B * S, D + 2), F32).ap()
        sorted_results = nc.dram_tensor("sorted_results", (B * S, D), F32).ap()
        make_identity(nc, (ident, ident16), id_done)
        stage_ssm(nc, X, ident, bc_rows, ins)
        stage_experts(nc, X, ident, ident16, (sorted_rows, sorted_results), ins)
        stage_attention(nc, X, ident, ident16, ins)
        stage_mlp(nc, X, ident, ins)
        with nc.Block() as block:
            @block.sync
            def _(sp):
                sp.dma_start(out.rearrange("b (t p) d -> p (b t) d", p=P), X[:]).then_inc(stored, 16)
                sp.wait_ge(stored, 16)


def kernel(**inputs):
    import numpy as np
    import concourse.bacc as bacc
    from concourse.bass_utils import run_bass_kernel_spmd

    nc = bacc.Bacc("TRN2", target_bir_lowering=False, num_devices=1)
    arrays = {f"in_{name}": a for name, a in layouts(inputs).items()}
    ins = {name[3:]: nc.dram_tensor(name, a.shape, mybir.dt.from_np(a.dtype), kind="ExternalInput").ap() for name, a in arrays.items()}
    out = nc.dram_tensor("out_x", (B, S, D), F32, kind="ExternalOutput").ap()
    program(nc, ins, out)
    return run_bass_kernel_spmd(nc, [arrays], core_ids=[0]).results[0]["out_x"]
```

```python
import math
from contextlib import ExitStack

import concourse.bass as bass
from concourse import mybir

F32 = mybir.dt.float32
F16 = mybir.dt.float16
I32 = mybir.dt.int32
U32 = mybir.dt.uint32
ALU = mybir.AluOpType
ACT = mybir.ActivationFunctionType
AX = mybir.AxisListType

P = 128
B, S, D = 4, 512, 512
NT = S // P
TILES = B * NT
DT = D // P
LN_EPS = 1e-5


class Tally:

    def __init__(self, eng, sem):
        self.eng, self.sem, self.n = eng, sem, 0

    def mark(self, ins):
        ins.then_inc(self.sem, 1)
        self.n += 1
        return self.n

    def wait(self, n=None):
        self.eng.wait_ge(self.sem, self.n if n is None else n)

    def link(self, ins):
        self.mark(ins)
        self.wait()


class Space:

    def __init__(self, nc, ctx, tag):
        self.nc, self.ctx, self.tag, self.sems = nc, ctx, tag, []

    def sb(self, name, shape, dt=F32):
        return self.ctx.enter_context(self.nc.sbuf_tensor(f"{self.tag}_{name}", shape, dt))

    def ps(self, name, shape, dt=F32):
        return self.ctx.enter_context(self.nc.psum_tensor(f"{self.tag}_{name}", shape, dt))

    def sem(self, name):
        s = self.ctx.enter_context(self.nc.semaphore(f"{self.tag}_{name}"))
        self.sems.append(s)
        return s

    def clear(self):
        for s in self.sems:
            self.nc.sync.sem_clear(s)
        self.nc.all_engine_barrier()


def layernorm_stats(nc, dve, chain, x_tiles, stats, mv):
    for t, x in enumerate(x_tiles):
        chain.mark(nc.vector.bn_stats(stats[:, t, :], x))
    chain.wait()
    for t in range(len(x_tiles)):
        chain.mark(nc.vector.bn_aggr(mv[:, t, :], stats[:, t, :]))
    chain.wait()


def stage_ssm(nc, X, ident, scratch, ins):
    DC, CK = 4, 2
    DR, DS = 16, 16
    RING = 4
    EARLY = 2
    R = 3
    W = 2
    PASSES = DS * DT // W
    with ExitStack() as ctx:
        sp_ = Space(nc, ctx, "ssm")
        sb, ps, sem = sp_.sb, sp_.ps, sp_.sem
        ctxT = sb("ctxT", [P, B, CK, S])
        w_in = sb("w_in", [P, CK, D])
        w_xp = sb("w_xp", [P, DT, DR + 2 * DS])
        w_dt = sb("w_dt", [DR, D])
        par = sb("par", [P, DT, DC + 3])
        negA = sb("negA", [P, DT, DS])
        skip = sb("skip", [P, DT, P])
        acc = sb("acc", [P, DT, S])
        u = sb("u", [P, 2, DT, S])
        du = sb("du", [P, 2, DT, S])
        delta = sb("delta", [P, 2, DT, S])
        zs = sb("zs", [P, 2, NT, S])
        xdbl = sb("xdbl", [DR + 2 * DS, S])
        BC = sb("BC", [P, RING, 2, S])
        dA = sb("dA", [P, R, W, S])
        dBu = sb("dBu", [P, R, W, S])
        h = sb("h", [P, R, W, S])
        hC = sb("hC", [P, R, W, S])
        yo = sb("yo", [P, 2, S])
        stats = sb("stats", [P, NT, 6])
        mv = sb("mv", [P, NT, 2])
        rstd = sb("rstd", [P, NT, 1])
        shift = sb("shift", [P, NT, 1])
        psY = ps("psY", [P, DT, S])
        psI = ps("psI", [P, DT, S])
        X4 = X[:].rearrange("p (b t) d -> p b t d", t=NT)

        ctx0_in, ctx_in, x0_in, x_in, w_loaded, w_used, A_done = (sem(n) for n in (
            "ctx0_in", "ctx_in", "x0_in", "x_in", "w_loaded", "w_used", "A_done"))
        inproj, u_done, xdbl_ps, xdbl_sb, dtp, tap0, tapped, conv_done = (sem(n) for n in (
            "inproj", "u_done", "xdbl_ps", "xdbl_sb", "dtp", "tap0", "tapped", "conv_done"))
        abs_done, relu_done, e_done, l_done, delta_done, du_done, z_done = (sem(n) for n in (
            "abs_done", "relu_done", "e_done", "l_done", "delta_done", "du_done", "z_done"))
        mv_done, rooted, ln_done, bc_out, dA_done, dBu_done, hC_done = (sem(n) for n in (
            "mv_done", "rooted", "ln_done", "bc_out", "dA_done", "dBu_done", "hC_done"))
        h_done, summed, y_done, turned, own, added = (sem(n) for n in (
            "h_done", "summed", "y_done", "turned", "own", "added"))
        bc_in = [sem(f"bc_in{i}") for i in range(RING)]
        bc_next = sem("bc_next")

        def loads_of(n):
            return n // RING + (0 if n % RING < EARLY else 1)

        def run(b, scan, nb, prep, first=False):
            cur, nxt = (b % 2 if scan else 0), (nb % 2 if prep else 0)
            with nc.Block() as block:
                @block.sync
                def _(sp):
                    if first:
                        sp.dma_start(ctxT[:, 0], ins["ctxT"][0].rearrange("(c p) s -> p c s", p=P)).then_inc(ctx0_in, 16)
                        sp.dma_start(X[:, 0:NT, :], ins["x"][0].rearrange("(t p) d -> p t d", p=P)).then_inc(x0_in, 16)
                        for i in range(1, B):
                            sp.dma_start(ctxT[:, i], ins["ctxT"][i].rearrange("(c p) s -> p c s", p=P)).then_inc(ctx_in, 16)
                            sp.dma_start(X[:, i * NT:(i + 1) * NT, :], ins["x"][i].rearrange("(t p) d -> p t d", p=P)).then_inc(x_in, 16)
                    if scan:
                        for n in range(EARLY, DS):
                            if n >= RING:
                                sp.wait_ge(hC_done, DT // W * (n - RING + 1))
                            sp.dma_start(BC[:, n % RING], bcast_rows(scratch[b], n)).then_inc(bc_in[n % RING], 16)
                            if prep and n == DS // 2:
                                sp.wait_ge(xdbl_sb, 1)
                                sp.dma_start(scratch[nb], xdbl[DR:, :]).then_inc(bc_out, 16)
                    elif prep:
                        sp.wait_ge(xdbl_sb, 1)
                        sp.dma_start(scratch[nb], xdbl[DR:, :]).then_inc(bc_out, 16)
                    if prep:
                        sp.wait_ge(bc_out, 16)
                        for n in range(EARLY):
                            if scan:
                                sp.wait_ge(hC_done, DT // W * (DS - RING + n + 1))
                            sp.dma_start(BC[:, n], bcast_rows(scratch[nb], n)).then_inc(bc_next, 16)
                        sp.wait_ge(bc_next, 16 * EARLY)
                    if first:
                        sp.wait_ge(ctx_in, 16 * (B - 1))
                        sp.wait_ge(x_in, 16 * (B - 1))

                @block.tensor
                def _(pe):
                    if first:
                        pe.wait_ge(ctx0_in, 16)
                        pe.wait_ge(w_loaded, 16 * 5)
                    if prep:
                        for e in range(DT):
                            for c in range(CK):
                                mm = nc.tensor.matmul(psI[:, e, :], w_in[:, c, e * P:(e + 1) * P], ctxT[:, nb, c, :],
                                                      start=(c == 0), stop=(c == CK - 1))
                            mm.then_inc(inproj, 1)
                    if scan:
                        for e in range(DT):
                            nc.tensor.matmul(psY[:, e, :], skip[:, e, :], u[:, cur, e, :], start=True, stop=False)
                    for j in range(PASSES):
                        if prep and j == 8:
                            pe.wait_ge(u_done, DT)
                            for e in range(DT):
                                mm = nc.tensor.matmul(psI[0:DR + 2 * DS, 0, :], w_xp[:, e, :], u[:, nxt, e, :],
                                                      start=(e == 0), stop=(e == DT - 1))
                            mm.then_inc(xdbl_ps, 1)
                        if prep and j == 12:
                            pe.wait_ge(xdbl_sb, 1)
                            for e in range(DT):
                                nc.tensor.matmul(psI[:, e, :], w_dt[:, e * P:(e + 1) * P], xdbl[0:DR, :],
                                                 start=True, stop=True).then_inc(dtp, 1)
                        if scan:
                            n, half = divmod(j, DT // W)
                            pe.wait_ge(hC_done, j + 1)
                            for w in range(W):
                                mm = nc.tensor.matmul(psY[:, half * W + w, :], ident[:], hC[:, j % R, w, :],
                                                      start=False, stop=(n == DS - 1))
                            mm.then_inc(summed, 1)
                    if scan:
                        if prep:
                            pe.wait_ge(relu_done, DT)
                        for e in range(DT):
                            pe.wait_ge(y_done, e + 1)
                            for t in range(NT):
                                mm = nc.tensor.transpose(psI[:, e, t * P:(t + 1) * P], yo[:, e % 2, t * P:(t + 1) * P], ident[:])
                            mm.then_inc(turned, 1)

                @block.scalar
                def _(act):
                    if first:
                        act.dma_start(w_in[:], ins["in_proj_wT"].rearrange("(c p) e -> p c e", p=P)).then_inc(w_loaded, 16)
                        act.dma_start(par[:], ins["channels"].rearrange("(c p) k -> p c k", p=P)).then_inc(w_loaded, 16)
                        act.dma_start(w_xp[:], ins["x_proj_wT"].rearrange("(c p) k -> p c k", p=P)).then_inc(w_loaded, 16)
                        act.dma_start(w_dt[:], ins["dt_proj_wT"]).then_inc(w_loaded, 16)
                        act.dma_start(negA[:], ins["A_log"].rearrange("(c p) n -> p c n", p=P)).then_inc(w_loaded, 16)
                        act.wait_ge(w_loaded, 16 * 5)
                        nc.scalar.activation(negA[:], negA[:], ACT.Exp).then_inc(A_done, 1)
                    for j in range(PASSES):
                        if scan:
                            n, half = divmod(j, DT // W)
                            if j >= R:
                                act.wait_ge(h_done, j - R + 1)
                            for w in range(W):
                                e = half * W + w
                                nc.scalar.activation(dA[:, j % R, w, 1:S], delta[:, cur, e, 1:S], ACT.Exp,
                                                     scale=negA[:, e, n:n + 1]).then_inc(dA_done, 1)
                        if prep and j == 4:
                            for e in range(DT):
                                act.wait_ge(inproj, e + 1)
                                nc.scalar.activation(acc[:, e, :], psI[:, e, :], ACT.Identity, scale=par[:, e, DC - 1:DC],
                                                     bias=par[:, e, DC:DC + 1]).then_inc(tap0, 1)
                        if prep and j == 3:
                            act.wait_ge(mv_done, 1)
                            nc.scalar.activation(rstd[:], mv[:, :, 1:2], ACT.Sqrt).then_inc(rooted, 1)
                        if prep and j == 9:
                            for e in range(DT):
                                act.wait_ge(conv_done, e + 1)
                                nc.scalar.activation(u[:, nxt, e, :], acc[:, e, :], ACT.Silu).then_inc(u_done, 1)
                            act.wait_ge(ln_done, 1)
                            for t in range(NT):
                                nc.scalar.activation(zs[:, nxt, t, :], X4[:, nb, t, :], ACT.Silu, scale=rstd[:, t, :],
                                                     bias=shift[:, t, :]).then_inc(z_done, 1)
                        if prep and j == 13:
                            act.wait_ge(xdbl_ps, 1)
                            nc.scalar.activation(xdbl[:], psI[0:DR + 2 * DS, 0, :], ACT.Copy).then_inc(xdbl_sb, 1)
                        if prep and j == 17:
                            for e in range(DT):
                                act.wait_ge(dtp, e + 1)
                                nc.scalar.activation(acc[:, e, :], psI[:, e, :], ACT.Abs, bias=par[:, e, DC + 1:DC + 2]).then_inc(abs_done, 1)
                                nc.scalar.activation(delta[:, nxt, e, :], psI[:, e, :], ACT.Relu, bias=par[:, e, DC + 1:DC + 2]).then_inc(relu_done, 1)
                        if prep and j == 19:
                            act.wait_ge(abs_done, DT)
                            nc.scalar.activation(acc[:], acc[:], ACT.Exp, scale=-1.0).then_inc(e_done, 1)
                        if prep and j == 21:
                            act.wait_ge(e_done, 1)
                            nc.scalar.activation(acc[:], acc[:], ACT.Ln, bias=1.0).then_inc(l_done, 1)

                @block.gpsimd
                def _(pool):
                    if first:
                        nc.gpsimd.memset(dA[:, :, :, 0:1], 0.0).then_inc(w_used, 1)
                    for j in range(PASSES):
                        if scan:
                            n, half = divmod(j, DT // W)
                            if half == 0 and n >= EARLY:
                                pool.wait_ge(bc_in[n % RING], 16 * loads_of(n))
                            if j >= R:
                                pool.wait_ge(h_done, j - R + 1)
                            nc.gpsimd.tensor_tensor(dBu[:, j % R], du[:, cur, half * W:(half + 1) * W, :],
                                                    BC[:, n % RING, 0, :].unsqueeze(1).broadcast_to([P, W, S]), ALU.mult).then_inc(dBu_done, 1)

                @block.vector
                def _(dve):
                    if first:
                        dve.wait_ge(A_done, 1)
                        nc.vector.tensor_scalar(negA[:], negA[:], -1.0, None, ALU.mult).then_inc(A_done, 1)
                        for e in range(DT):
                            nc.vector.tensor_scalar(skip[:, e, :], ident[:], par[:, e, DC + 2:DC + 3], None, ALU.mult).then_inc(w_used, 1)
                        dve.wait_ge(x0_in, 16)
                    chain = Tally(dve, own)
                    if prep:
                        layernorm_stats(nc, dve, chain, [X4[:, nb, t, :] for t in range(NT)], stats, mv)
                        nc.vector.tensor_scalar(mv[:, :, 1:2], mv[:, :, 1:2], LN_EPS, None, ALU.add).then_inc(mv_done, 1)

                    def project_states(j):
                        n, half = divmod(j, DT // W)
                        dve.wait_ge(h_done, j + 1)
                        if j >= R:
                            dve.wait_ge(summed, j - R + 1)
                        nc.vector.tensor_tensor(hC[:, j % R], h[:, j % R],
                                                BC[:, n % RING, 1, :].unsqueeze(1).broadcast_to([P, W, S]), ALU.mult).then_inc(hC_done, 1)

                    for j in range(PASSES):
                        if scan:
                            n, half = divmod(j, DT // W)
                            dve.wait_ge(dA_done, W * (j + 1))
                            dve.wait_ge(dBu_done, j + 1)
                            if half == 0 and n >= EARLY:
                                dve.wait_ge(bc_in[n % RING], 16 * loads_of(n))
                            if j >= R:
                                dve.wait_ge(hC_done, j - R + 1)
                            nc.vector.tensor_tensor_scan(h[:, j % R].rearrange("p w s -> p (w s)"), dA[:, j % R].rearrange("p w s -> p (w s)"),
                                                         dBu[:, j % R].rearrange("p w s -> p (w s)"), 0.0, ALU.mult, ALU.add).then_inc(h_done, 1)
                            if j >= 1:
                                project_states(j - 1)
                        if prep and 3 <= j < 3 + DC - 1:
                            k = j - 2
                            for e in range(DT):
                                if k == 1:
                                    dve.wait_ge(tap0, e + 1)
                                else:
                                    dve.wait_ge(tapped, (k - 2) * DT + e + 1)
                                nc.vector.scalar_tensor_tensor(out=acc[:, e, k:], in0=psI[:, e, :S - k], scalar=par[:, e, DC - 1 - k:DC - k],
                                                               in1=acc[:, e, k:], op0=ALU.mult, op1=ALU.add).then_inc(conv_done if k == DC - 1 else tapped, 1)
                        if prep and j == 5:
                            dve.wait_ge(rooted, 1)
                            chain.link(nc.vector.reciprocal(rstd[:], rstd[:]))
                            nc.vector.scalar_tensor_tensor(out=shift[:], in0=mv[:, :, 0:1], scalar=-1.0, in1=rstd[:], op0=ALU.mult, op1=ALU.mult).then_inc(ln_done, 1)
                        if prep and j == 22:
                            dve.wait_ge(l_done, 1)
                            dve.wait_ge(relu_done, DT)
                            nc.vector.tensor_tensor(delta[:, nxt], delta[:, nxt], acc[:], ALU.add).then_inc(delta_done, 1)
                        if prep and j == 23:
                            dve.wait_ge(delta_done, 1)
                            dve.wait_ge(u_done, DT)
                            nc.vector.tensor_tensor(du[:, nxt], delta[:, nxt], u[:, nxt], ALU.mult).then_inc(du_done, 1)
                    if scan:
                        project_states(PASSES - 1)

                        def add_results(e):
                            dve.wait_ge(turned, e + 1)
                            xe = X4[:, b, :, e * P:(e + 1) * P]
                            nc.vector.tensor_tensor(xe, xe, psI[:, e, :].rearrange("p (t e) -> p t e", e=P), ALU.add).then_inc(added, 1)

                        for e in range(DT):
                            dve.wait_ge(summed, PASSES - DT // W + e // W + 1)
                            if e >= 2:
                                dve.wait_ge(turned, e - 1)
                            nc.vector.tensor_tensor(yo[:, e % 2, :], psY[:, e, :], zs[:, cur, e, :], ALU.mult).then_inc(y_done, 1)
                            if e >= 2:
                                add_results(e - 2)
                        add_results(DT - 2)
                        add_results(DT - 1)
            sp_.clear()

        run(None, False, 0, True, first=True)
        with nc.Fori(0, B - 1) as b:
            run(b, True, b + 1, True)
        run(B - 1, True, None, False)


def bcast_rows(rows, n):
    return rows.rearrange("(w n) s -> n w s", w=2)[n].partition_broadcast(P)


def make_identity(nc, tiles, sems):
    with nc.Block() as block:
        @block.gpsimd
        def _(pool):
            for tile, s in zip(tiles, sems):
                nc.gpsimd.memset(tile[:], 0.0).then_inc(s, 1)
                pool.wait_ge(s, 1)
                nc.gpsimd.affine_select(out=tile[:], in_=tile[:], compare_op=ALU.not_equal, fill=1.0, base=0,
                                        pattern=[[-1, P]], channel_multiplier=1).then_inc(s, 1)
                pool.wait_ge(s, 2)


def stage_experts(nc, X, ident, ident16, scratch, ins):
    E = 32
    STEPS = TILES + E - 1
    ROW = D + 2
    rows, results = scratch
    with ExitStack() as ctx:
        sp_ = Space(nc, ctx, "moe")
        sb, ps, sem = sp_.sb, sp_.ps, sp_.sem
        XN = sb("XN", [P, TILES, ROW])
        router = sb("router", [P, DT, E])
        tern = sb("tern", [P, DT * D], F16)
        scale = sb("scale", [P, D])
        iota_i = sb("iota_i", [P, 64], I32)
        iota = sb("iota", [P, 64])
        tile_end = sb("tile_end", [P, TILES])
        before = sb("before", [P, P], F16)
        ones = sb("ones", [P, P], F16)
        ones32 = sb("ones32", [P, E])
        OH = sb("OH", [P, TILES, E], F16)
        CUM = sb("CUM", [P, TILES + 1, E], F16)
        POS = sb("POS", [P, TILES], U32)
        Ef = sb("Ef", [P, STEPS])
        EI = sb("EI", [P, STEPS], I32)
        TI = sb("TI", [P, STEPS], I32)
        SI = sb("SI", [P, STEPS], I32)
        AI = sb("AI", [P, STEPS], I32)
        SLOTS = 4

        with ExitStack() as ctx2:
            r_ = Space(nc, ctx2, "route")
            tern32 = r_.sb("tern32", [P, DT * D])
            negs = r_.sb("negs", [P, DT * D], F16)
            xT = r_.sb("xT", [P, 2, DT * P])
            lg = r_.sb("lg", [P, TILES, E])
            ex = r_.sb("ex", [P, TILES, E])
            m8 = r_.sb("m8", [P, TILES, 8])
            negm = r_.sb("negm", [P, TILES])
            i8 = r_.sb("i8", [P, TILES, 8], U32)
            idx = r_.sb("idx", [P, TILES, 1])
            den = r_.sb("den", [P, TILES, 1])
            stats = r_.sb("stats", [P, TILES, 6])
            mv = r_.sb("mv", [P, TILES, 2])
            rstd = r_.sb("rstd", [P, TILES, 1])
            psT = r_.ps("psT", [P, 2, DT * P])
            psL = r_.ps("psL", [P, TILES, E])
            loaded, consts, tern_own, mv_done, rooted = (r_.sem(n) for n in ("loaded", "consts", "tern_own", "mv_done", "rooted"))
            stat_own = r_.sem("stat_own")
            with nc.Block() as block:
                @block.sync
                def _(sp):
                    sp.dma_start(router[:], ins["routerT"].rearrange("(c p) e -> p c e", p=P)).then_inc(loaded, 16)
                    sp.dma_start(scale[:], ins["out_scale"].partition_broadcast(P)).then_inc(loaded, 16)
                    sp.dma_start(tern32[:].rearrange("p (c o) -> p c o", c=DT),
                                 ins["ternaryT"].rearrange("(c p) o -> p c o", p=P)).then_inc(loaded, 16)

                @block.gpsimd
                def _(pool):
                    nc.gpsimd.iota(iota_i[:], [[1, 64]], base=0, channel_multiplier=0).then_inc(consts, 1)
                    nc.gpsimd.memset(ones[:], 1.0).then_inc(consts, 1)
                    nc.gpsimd.memset(ones32[:], 1.0).then_inc(consts, 1)
                    pool.wait_ge(consts, 3)
                    nc.gpsimd.tensor_copy(iota[:], iota_i[:]).then_inc(consts, 1)
                    nc.gpsimd.affine_select(out=before[:], in_=ones[:], compare_op=ALU.is_ge, fill=0.0, base=-1,
                                            pattern=[[1, P]], channel_multiplier=-1).then_inc(consts, 1)

                @block.scalar
                def _(act):
                    act.wait_ge(mv_done, 1)
                    nc.scalar.activation(rstd[:], mv[:, :, 1:2], ACT.Sqrt).then_inc(rooted, 1)

                @block.vector
                def _(dve):
                    chain = Tally(dve, stat_own)
                    layernorm_stats(nc, dve, chain, [X[:, t, :] for t in range(TILES)], stats, mv)
                    nc.vector.tensor_scalar(mv[:, :, 1:2], mv[:, :, 1:2], LN_EPS, None, ALU.add).then_inc(mv_done, 1)
                    dve.wait_ge(consts, 5)
                    nc.vector.tensor_scalar(tile_end[:], iota[:, 0:TILES], 1.0, float(P), ALU.add, ALU.mult).then_inc(tern_own, 1)
                    dve.wait_ge(loaded, 48)
                    nc.vector.tensor_scalar(tern[:], tern32[:], 0.25, None, ALU.is_gt).then_inc(tern_own, 1)
                    nc.vector.tensor_scalar(negs[:], tern32[:], -0.25, None, ALU.is_lt).then_inc(tern_own, 1)
                    dve.wait_ge(tern_own, 3)
                    nc.vector.tensor_tensor(tern[:], tern[:], negs[:], ALU.subtract).then_inc(tern_own, 1)
                    dve.wait_ge(rooted, 1)
                    nc.vector.reciprocal(rstd[:], rstd[:]).then_inc(tern_own, 1)
            r_.clear()
            xn_done, turned, xT_done, logits = (r_.sem(n) for n in ("xn_done", "turned", "xT_done", "logits"))
            top_done, summed, own = r_.sem("top_done"), r_.sem("summed"), r_.sem("own")
            with nc.Block() as block:
                @block.vector
                def _(dve):
                    chain = Tally(dve, own)
                    for t in range(TILES):
                        nc.vector.tensor_scalar(XN[:, t, 0:D], X[:, t, :], mv[:, t, 0:1], rstd[:, t, :], ALU.subtract, ALU.mult).then_inc(xn_done, 1)
                    dve.wait_ge(logits, TILES)
                    chain.link(nc.vector.tensor_copy(lg[:], psL[:]))
                    for t in range(TILES):
                        chain.mark(nc.vector.max(m8[:, t, :], lg[:, t, :]))
                    chain.wait()
                    nc.vector.tensor_scalar(negm[:], m8[:, :, 0], -1.0, None, ALU.mult).then_inc(top_done, 1)
                    for t in range(TILES):
                        chain.mark(nc.vector.max_index(i8[:, t, :], m8[:, t, :], lg[:, t, :]))
                    chain.wait()
                    chain.link(nc.vector.tensor_copy(idx[:], i8[:, :, 0:1]))
                    chain.mark(nc.vector.tensor_copy(XN[:, :, D:D + 1], idx[:]))
                    for t in range(TILES):
                        chain.mark(nc.vector.tensor_scalar(OH[:, t, :], iota[:, 0:E], idx[:, t, :], None, ALU.is_equal))
                    dve.wait_ge(summed, TILES)
                    chain.mark(nc.vector.reciprocal(XN[:, :, D + 1:D + 2], den[:]))

                @block.scalar
                def _(act):
                    for t in range(TILES):
                        act.wait_ge(turned, t + 1)
                        if t >= 2:
                            act.wait_ge(logits, t - 1)
                        nc.scalar.activation(xT[:, t % 2, :], psT[:, t % 2, :], ACT.Copy).then_inc(xT_done, 1)
                    act.wait_ge(top_done, 1)
                    for t in range(TILES):
                        nc.scalar.activation(ex[:, t, :], lg[:, t, :], ACT.Exp, bias=negm[:, t:t + 1],
                                             accum_out=den[:, t, :]).then_inc(summed, 1)

                @block.tensor
                def _(pe):
                    for t in range(TILES + 1):
                        if t < TILES:
                            pe.wait_ge(xn_done, t + 1)
                            if t >= 2:
                                pe.wait_ge(xT_done, t - 1)
                            for c in range(DT):
                                mm = nc.tensor.transpose(psT[:, t % 2, c * P:(c + 1) * P], XN[:, t, c * P:(c + 1) * P], ident[:])
                            mm.then_inc(turned, 1)
                        if t >= 1:
                            pe.wait_ge(xT_done, t)
                            for c in range(DT):
                                mm = nc.tensor.matmul(psL[:, t - 1, :], xT[:, (t - 1) % 2, c * P:(c + 1) * P], router[:, c, :],
                                                      start=(c == 0), stop=(c == DT - 1))
                            mm.then_inc(logits, 1)
            r_.clear()

        YS = sb("YS", [P, TILES, D])
        XH = sb("XH", [P, 2, 2, D], F16)
        XST = sb("XST", [P, TILES, 2 * DT, P], F16)
        CMP = sb("CMP", [P, STEPS, E])
        incl = sb("incl", [P, E])
        excl = sb("excl", [P, E])
        rk = sb("rk", [P, E])
        place = sb("place", [P, TILES, E])
        posf = sb("posf", [P, TILES])
        GO = sb("GO", [P, TILES * E])
        oh2 = sb("oh2", [P, TILES, E])
        with ExitStack() as ctx2:
            s_ = Space(nc, ctx2, "sort")
            Af = s_.sb("Af", [P, STEPS])
            psR = s_.ps("psR", [P, TILES, E])
            psC = s_.ps("psC", [P, E])
            psX = s_.ps("psX", [P, 2, 2 * DT, P], F16)
            cum, ranked, own, pos_done, sent, hi_done, lo_done, turned, evac = (
                s_.sem(n) for n in ("cum", "ranked", "own", "pos_done", "sent", "hi_done", "lo_done", "turned", "evac"))
            back = [s_.sem(f"back{i}") for i in range(4)]
            zeroed, lo_odd = s_.sem("zeroed"), s_.sem("lo_odd")
            rowsT = rows.rearrange("(t p) d -> p t d", p=P)
            with nc.Block() as block:
                @block.vector
                def _(dve):
                    chain = Tally(dve, own)
                    nc.vector.memset(CUM[:, 0, :], 0.0).then_inc(cum, 1)
                    for t in range(TILES):
                        dve.wait_ge(cum, t + 1)
                        nc.vector.tensor_tensor(CUM[:, t + 1, :], CUM[:, t, :], OH[:, t, :], ALU.add).then_inc(cum, 1)
                    dve.wait_ge(ranked, 1)
                    chain.link(nc.vector.tensor_tensor_scan(incl[:], ones32[:], psC[:], 0.0, ALU.mult, ALU.add))
                    chain.link(nc.vector.tensor_tensor(excl[:], incl[:], psC[:], ALU.subtract))
                    chain.link(nc.vector.tensor_tensor(place[:], psR[:], excl[:].unsqueeze(1).broadcast_to([P, TILES, E]), ALU.add))
                    chain.link(nc.vector.tensor_tensor(place[:], place[:], OH[:], ALU.mult))
                    chain.link(nc.vector.tensor_reduce(posf[:], place[:], AX.X, ALU.add))
                    nc.vector.tensor_copy(POS[:], posf[:]).then_inc(pos_done, 1)
                    ends = CMP[:].rearrange("p k e -> p (k e)")[:, 0:E * TILES].rearrange("p (e t) -> p e t", t=TILES)
                    chain.link(nc.vector.tensor_tensor(ends, incl[:].unsqueeze(2).broadcast_to([P, E, TILES]),
                                                       tile_end[:].unsqueeze(1).broadcast_to([P, E, TILES]), ALU.is_gt))
                    chain.link(nc.vector.tensor_reduce(rk[:], ends, AX.X, ALU.add))
                    chain.link(nc.vector.tensor_tensor(rk[:], rk[:], iota[:, 0:E], ALU.add))
                    chain.link(nc.vector.tensor_tensor(CMP[:], rk[:].unsqueeze(1).broadcast_to([P, STEPS, E]),
                                                       iota[:, 0:STEPS].unsqueeze(2).broadcast_to([P, STEPS, E]), ALU.is_lt))
                    chain.link(nc.vector.tensor_reduce(Ef[:], CMP[:], AX.X, ALU.add))
                    chain.mark(nc.vector.tensor_copy(EI[:], Ef[:]))
                    chain.mark(nc.vector.tensor_tensor(TI[:], iota[:, 0:STEPS], Ef[:], ALU.subtract))
                    chain.link(nc.vector.tensor_scalar(Af[:], iota[:, 0:STEPS], float(E), None, ALU.mult))
                    chain.mark(nc.vector.scalar_tensor_tensor(out=AI[:], in0=Ef[:], scalar=1.0 - E, in1=Af[:], op0=ALU.mult, op1=ALU.add))
                    chain.mark(nc.vector.tensor_scalar(SI[:], EI[:], SLOTS - 1, None, ALU.bitwise_and))
                    for t in range(TILES):
                        if t % 4 == 0:
                            dve.wait_ge(back[t // 4], 16)
                        if t >= 2:
                            dve.wait_ge(turned, t - 1)
                        nc.vector.tensor_copy(XH[:, t % 2, 0, :], XN[:, t, 0:D]).then_inc(hi_done, 1)
                        if t % 2 == 0:
                            dve.wait_ge(hi_done, t + 1)
                            nc.vector.tensor_tensor(XH[:, 0, 1, :], XN[:, t, 0:D], XH[:, 0, 0, :], ALU.subtract).then_inc(lo_done, 1)
                    for g in range(4):
                        dve.wait_ge(back[g], 16)
                    chain.link(nc.vector.tensor_tensor(oh2[:], iota[:, 0:E].unsqueeze(1).broadcast_to([P, TILES, E]),
                                                       XN[:, :, D:D + 1].broadcast_to([P, TILES, E]), ALU.is_equal))
                    chain.mark(nc.vector.tensor_tensor(GO[:].rearrange("p (t e) -> p t e", e=E), oh2[:],
                                                       XN[:, :, D + 1:D + 2].broadcast_to([P, TILES, E]), ALU.mult))

                @block.tensor
                def _(pe):
                    pe.wait_ge(cum, TILES + 1)
                    for t in range(TILES):
                        nc.tensor.matmul(psR[:, t, :], before[:], OH[:, t, :], start=True, stop=False)
                        nc.tensor.matmul(psR[:, t, :], ones[:], CUM[:, t, :], start=False, stop=True)
                    nc.tensor.matmul(psC[:], ones[:], CUM[:, TILES, :], start=True, stop=True).then_inc(ranked, 1)
                    for t in range(TILES):
                        pe.wait_ge(lo_odd if t % 2 else lo_done, t // 2 + 1)
                        if t >= 2:
                            pe.wait_ge(evac, t - 1)
                        for h in range(2):
                            for c in range(DT):
                                mm = nc.tensor.transpose(psX[:, t % 2, h * DT + c, :], XH[:, t % 2, h, c * P:(c + 1) * P], ident16[:])
                        mm.then_inc(turned, 1)

                @block.gpsimd
                def _(pool):
                    nc.gpsimd.memset(YS[:], 0.0).then_inc(zeroed, 1)
                    pool.wait_ge(pos_done, 1)
                    for t in range(TILES):
                        pool.indirect_dma_start(out=rows, out_offset=bass.IndirectOffsetOnAxis(ap=POS[:, t:t + 1], axis=0),
                                                in_=XN[:, t, :], in_offset=None).then_inc(sent, 16)
                    for t in range(1, TILES, 2):
                        pool.wait_ge(hi_done, t + 1)
                        nc.gpsimd.tensor_tensor(XH[:, 1, 1, :], XN[:, t, 0:D], XH[:, 1, 0, :], ALU.subtract).then_inc(lo_odd, 1)

                @block.sync
                def _(sp):
                    sp.wait_ge(sent, 16 * TILES)
                    for g in range(4):
                        sp.dma_start(XN[:, 4 * g:4 * g + 4, :], rowsT[:, 4 * g:4 * g + 4, :]).then_inc(back[g], 16)

                @block.scalar
                def _(act):
                    for t in range(TILES):
                        act.wait_ge(turned, t + 1)
                        nc.scalar.activation(XST[:, t], psX[:, t % 2], ACT.Copy).then_inc(evac, 1)
            s_.clear()

        with ExitStack() as ctx2:
            w_ = Space(nc, ctx2, "walk")
            CUT = DT * D * 5 // 8
            mask = w_.sb("mask", [P, SLOTS, DT * D])
            W = [w_.sb(f"W{i}", [P, DT * D], F16) for i in range(SLOTS)]
            g = w_.sb("g", [P, 2])
            psO = w_.ps("psO", [P, SLOTS, D])
            mask_in = [w_.sem(f"mask_in{i}") for i in range(SLOTS)]
            W_done, W_last, mm_done, g_done, acc_done = (w_.sem(n) for n in ("W_done", "W_last", "mm_done", "g_done", "acc_done"))
            masks = ins["masksT"].rearrange("e (c p) o -> e p c o", p=P)
            HEAD = SLOTS
            TURNS = (STEPS - HEAD) // SLOTS
            TAIL = HEAD + TURNS * SLOTS
            with nc.Block() as block:
                @block.sync
                def _(sp):
                    def load_mask(k, j, first=False):
                        e = sp.value_load(EI[0:1, bass.ds(k, 1)], min_val=0, max_val=E - 1)
                        to = mask[:, e % SLOTS].rearrange("p (c o) -> p c o", c=DT)
                        if first:
                            sp.dma_start(to, masks[e]).then_inc(mask_in[j], 16)
                            return
                        before_e = sp.value_load(EI[0:1, bass.ds(k - 1, 1)], min_val=0, max_val=E - 1)
                        sp.dma_start(to, masks[e], cond=e - before_e, cond_hint=True).then_inc(mask_in[j], 16)

                    for k in range(HEAD):
                        load_mask(k, k, k == 0)
                    with sp.Fori(0, TURNS) as i:
                        for j in range(SLOTS):
                            sp.wait_ge(W_done, i * SLOTS + (j + 1))
                            sp.wait_ge(W_last, i * SLOTS + (j + 1))
                            load_mask(i * SLOTS + (HEAD + j), j)
                    for k in range(TAIL, STEPS):
                        sp.wait_ge(W_done, k - SLOTS + 1)
                        sp.wait_ge(W_last, k - SLOTS + 1)
                        load_mask(k, k % SLOTS)

                @block.gpsimd
                def _(pool):
                    def build_last(k, j, n, first=False):
                        slot = pool.value_load(SI[0:1, bass.ds(k, 1)], min_val=0, max_val=SLOTS - 1)
                        pool.wait_ge(mask_in[j], n * 16)
                        if not first:
                            pool.wait_ge(mm_done, k - SLOTS + 1)
                        nc.gpsimd.tensor_tensor(W[j % SLOTS][:, CUT:], mask[:, slot, CUT:], tern[:, CUT:], ALU.mult).then_inc(W_last, 1)

                    for k in range(HEAD):
                        build_last(k, k, 1, True)
                    with pool.Fori(0, TURNS) as i:
                        for j in range(SLOTS):
                            build_last(i * SLOTS + (HEAD + j), j, i + 2)
                    for k in range(TAIL, STEPS):
                        build_last(k, k % SLOTS, k // SLOTS + 1)

                @block.vector
                def _(dve):
                    def build(k, j, n, back=True):
                        slot = dve.value_load(SI[0:1, bass.ds(k, 1)], min_val=0, max_val=SLOTS - 1)
                        if back:
                            t, y = gates(k - 2, j)
                        dve.wait_ge(mask_in[j], n * 16)
                        if not (isinstance(k, int) and k < SLOTS):
                            dve.wait_ge(mm_done, k - SLOTS + 1)
                        nc.vector.tensor_tensor(W[j % SLOTS][:, 0:CUT], mask[:, slot, 0:CUT], tern[:, 0:CUT], ALU.mult).then_inc(W_done, 1)
                        if back:
                            accumulate(k - 2, j, y)

                    def gates(k, j):
                        t = dve.value_load(TI[0:1, bass.ds(k, 1)], min_val=0, max_val=TILES - 1)
                        at = dve.value_load(AI[0:1, bass.ds(k, 1)], min_val=0, max_val=TILES * E - 1)
                        nc.vector.tensor_copy(g[:, j % 2:j % 2 + 1], GO[:, bass.ds(at, 1)]).then_inc(g_done, 1)
                        return t, YS[:, t, :]

                    def accumulate(k, j, y):
                        dve.wait_ge(g_done, k + 1)
                        dve.wait_ge(mm_done, k + 1)
                        if not (isinstance(k, int) and k == 0):
                            dve.wait_ge(acc_done, k)
                        nc.vector.scalar_tensor_tensor(out=y, in0=psO[:, (j - 2) % SLOTS, :], scalar=g[:, j % 2:j % 2 + 1], in1=y,
                                                       op0=ALU.mult, op1=ALU.add).then_inc(acc_done, 1)

                    for k in range(HEAD):
                        build(k, k, 1, k >= 2)
                    with dve.Fori(0, TURNS) as i:
                        for j in range(SLOTS):
                            build(i * SLOTS + (HEAD + j), j, i + 2)
                    for k in range(TAIL, STEPS):
                        build(k, k % SLOTS, k // SLOTS + 1)
                    for k in range(STEPS - 2, STEPS):
                        t, y = gates(k, k + 2)
                        accumulate(k, k + 2, y)

                @block.tensor
                def _(pe):
                    def product(k, j, first=False):
                        t = pe.value_load(TI[0:1, bass.ds(k, 1)], min_val=0, max_val=TILES - 1)
                        pe.wait_ge(W_done, k + 1)
                        pe.wait_ge(W_last, k + 1)
                        if not first:
                            pe.wait_ge(acc_done, k - SLOTS + 1)
                        for q in range(2 * DT):
                            mm = nc.tensor.matmul(psO[:, j, :], XST[:, t, q, :], W[j][:, q % DT * D:(q % DT + 1) * D], start=(q == 0), stop=(q == 2 * DT - 1))
                        mm.then_inc(mm_done, 1)

                    for k in range(HEAD):
                        product(k, k, True)
                    with pe.Fori(0, TURNS) as i:
                        for j in range(SLOTS):
                            product(i * SLOTS + (HEAD + j), j)
                    for k in range(TAIL, STEPS):
                        product(k, k % SLOTS)
            w_.clear()

        with ExitStack() as ctx2:
            u_ = Space(nc, ctx2, "unsort")
            scaled, sent, added = (u_.sem(n) for n in ("scaled", "sent", "added"))
            GR = 4
            got = [u_.sem(f"got{i}") for i in range(TILES // GR)]
            resT = results.rearrange("(t p) d -> p t d", p=P)
            with nc.Block() as block:
                @block.vector
                def _(dve):
                    for q in range(TILES // GR):
                        y = YS[:, GR * q:GR * q + GR, :]
                        nc.vector.tensor_tensor(y, y, scale[:].unsqueeze(1).broadcast_to([P, GR, D]), ALU.mult).then_inc(scaled, 1)
                    for t in range(TILES):
                        dve.wait_ge(got[t // GR], 16 * GR)
                        nc.vector.tensor_tensor(X[:, t, :], X[:, t, :], XN[:, t, 0:D], ALU.add).then_inc(added, 1)

                @block.sync
                def _(sp):
                    for q in range(TILES // GR):
                        sp.wait_ge(scaled, q + 1)
                        sp.dma_start(resT[:, GR * q:GR * q + GR, :], YS[:, GR * q:GR * q + GR, :]).then_inc(sent, 16)

                @block.gpsimd
                def _(pool):
                    pool.wait_ge(sent, 16 * (TILES // GR))
                    for t in range(TILES):
                        pool.indirect_dma_start(out=XN[:, t, 0:D], out_offset=None, in_=results,
                                                in_offset=bass.IndirectOffsetOnAxis(ap=POS[:, t:t + 1], axis=0)).then_inc(got[t // GR], 16)
            u_.clear()


def stage_attention(nc, X, ident, ident16, ins):
    H, HD = 32, 16
    CK = 2
    AXES, HALF = 2, HD // 4
    FQ = AXES * HALF
    HW = 4 * HD
    G, NG = 4, H // 4
    SCALE = HD ** -0.5
    PI = math.pi
    with ExitStack() as ctx:
        a_ = Space(nc, ctx, "att")
        sb = a_.sb
        Wq = sb("Wq", [P, DT, D])
        Wkv = sb("Wkv", [P, CK, 2 * D])
        Wout = sb("Wout", [P, DT, D])
        bout = sb("bout", [P, D])
        freq = sb("freq", [P, FQ])
        ctxT = sb("ctxT", [P, CK, S])
        heads = sb("heads", [P, NT, D])
        xT = sb("xT", [P, DT, S])
        mv = sb("mv", [P, TILES, 2])
        rstd = sb("rstd", [P, TILES, 1])
        table = sb("table", [P, 2, 2, TILES, FQ])
        QS = [sb("QS", [P, H, P], F16), sb("KS", [P, H, P], F16)]
        rot = sb("rot", [P, D])
        t_cos = sb("t_cos", [P, D])
        t_sin = sb("t_sin", [P, D])
        V = sb("V", [P, NT, H, 32])
        QT = sb("QT", [P, H, S], F16)
        KT = sb("KT", [P, H, S], F16)
        with ExitStack() as ctx2:
            c_ = Space(nc, ctx2, "attc")
            stats = c_.sb("stats", [P, TILES, 6])
            pos = c_.sb("pos", [P, TILES, AXES])
            ang = c_.sb("ang", [P, 2, TILES, FQ])
            turns = c_.sb("turns", [P, 2, TILES, FQ], I32)
            turns_f = c_.sb("turns_f", [P, 2, TILES, FQ])
            pos_in, loaded, consts, own, mv_done, rooted, ang_done, sin_done = (c_.sem(n) for n in (
                "pos_in", "loaded", "consts", "own", "mv_done", "rooted", "ang_done", "sin_done"))
            with nc.Block() as block:
                @block.sync
                def _(sp):
                    sp.dma_start(pos[:], ins["pos"].rearrange("b (t p) a -> p (b t) a", p=P)).then_inc(pos_in, 16)
                    sp.dma_start(Wq[:], ins["Wq"].rearrange("(c p) n -> p c n", p=P)).then_inc(loaded, 16)
                    sp.dma_start(Wkv[:], ins["Wkv"].rearrange("(c p) n -> p c n", p=P)).then_inc(loaded, 16)
                    sp.dma_start(Wout[:], ins["Wout"].rearrange("(c p) n -> p c n", p=P)).then_inc(loaded, 16)
                    sp.dma_start(bout[:], ins["bout"].partition_broadcast(P)).then_inc(loaded, 16)
                    sp.wait_ge(loaded, 64)

                @block.gpsimd
                def _(pool):
                    nc.gpsimd.memset(V[:], 0.0).then_inc(consts, 1)
                    pool.wait_ge(consts, 1)
                    nc.gpsimd.memset(V[:, :, :, HD:HD + 1], 1.0).then_inc(consts, 1)

                @block.scalar
                def _(act):
                    act.wait_ge(ang_done, 1)
                    nc.scalar.activation(table[:, 1], ang[:], ACT.Sin).then_inc(sin_done, 1)
                    act.wait_ge(mv_done, 1)
                    nc.scalar.activation(rstd[:], mv[:, :, 1:2], ACT.Sqrt).then_inc(rooted, 1)

                @block.vector
                def _(dve):
                    chain = Tally(dve, own)
                    for j in range(HALF):
                        chain.mark(nc.vector.memset(freq[:].rearrange("p (a f) -> p a f", f=HALF)[:, :, j:j + 1], 10000.0 ** (-j / HALF)))
                    chain.mark(nc.vector.memset(QS[0][:, :, HW:], 0.0))
                    chain.link(nc.vector.memset(QS[1][:, :, HW:], 0.0))
                    chain.mark(nc.vector.memset(QS[1][:, :, HW:HW + 2], 1.0))
                    dve.wait_ge(pos_in, 16)
                    chain.link(nc.vector.tensor_tensor(ang[:, 1].rearrange("p t (a f) -> p t a f", f=HALF),
                                                       pos[:].unsqueeze(3).broadcast_to([P, TILES, AXES, HALF]),
                                                       freq[:].rearrange("p (a f) -> p a f", f=HALF).unsqueeze(1).broadcast_to([P, TILES, AXES, HALF]), ALU.mult))
                    chain.link(nc.vector.tensor_scalar(ang[:, 0], ang[:, 1], PI / 2, None, ALU.add))
                    chain.link(nc.vector.tensor_scalar(turns[:], ang[:], 1 / (2 * PI), None, ALU.mult))
                    chain.link(nc.vector.tensor_copy(turns_f[:], turns[:]))
                    nc.vector.scalar_tensor_tensor(out=ang[:], in0=turns_f[:], scalar=-2 * PI, in1=ang[:], op0=ALU.mult, op1=ALU.add).then_inc(ang_done, 1)
                    layernorm_stats(nc, dve, chain, [X[:, t, :] for t in range(TILES)], stats, mv)
                    nc.vector.tensor_scalar(mv[:, :, 1:2], mv[:, :, 1:2], LN_EPS, None, ALU.add).then_inc(mv_done, 1)
                    dve.wait_ge(sin_done, 1)
                    chain.mark(nc.vector.tensor_scalar(table[:, 0], table[:, 1], SCALE, None, ALU.mult))
                    dve.wait_ge(rooted, 1)
                    chain.mark(nc.vector.reciprocal(rstd[:], rstd[:]))
            c_.clear()
        X4 = X[:].rearrange("p (b t) d -> p b t d", t=NT)
        mv4 = mv[:].rearrange("p (b t) k -> p b t k", t=NT)
        rstd4 = rstd[:].rearrange("p (b t) k -> p b t k", t=NT)
        table4 = table[:].rearrange("p s w (b t) f -> p s w b t f", t=NT)

        def project_in(b, run):
            with ExitStack() as ctx2:
                p_ = Space(nc, ctx2, f"qkv_{run}")
                xn = p_.sb("xn", [P, NT, D])
                psX = p_.ps("psX", [P, 2, DT * P])
                psQ = p_.ps("psQ", [P, 3, D])
                psP = p_.ps("psP", [P, 3, 8, P], F16)
                ctx_in, xn_done, turned, xT_done = (p_.sem(n) for n in ("ctx_in", "xn_done", "turned", "xT_done"))
                proj, rot_done, hi_done, lo_done, v_done, parts, evac_a, evac_v, own = (
                    p_.sem(n) for n in ("proj", "rot_done", "hi_done", "lo_done", "v_done", "parts", "evac_a", "evac_v", "own"))
                dst = (QT, KT)
                hi_of = (lambda s: s[:, :, 0:2 * HD].rearrange("p h (r d) -> p h r d", r=2),
                         lambda s: s[:, :, 0:HW].rearrange("p h (r w d) -> p h r w d", r=2, w=2)[:, :, :, 0, :])
                lo_of = (lambda s: s[:, :, 2 * HD:HW].rearrange("p h (r d) -> p h r d", r=2),
                         lambda s: s[:, :, 0:HW].rearrange("p h (r w d) -> p h r w d", r=2, w=2)[:, :, :, 1, :])
                with nc.Block() as block:
                    @block.sync
                    def _(sp):
                        sp.dma_start(ctxT[:], ins["ctxT"][b].rearrange("(c p) s -> p c s", p=P)).then_inc(ctx_in, 16)

                    @block.tensor
                    def _(pe):
                        def project(t):
                            rows = slice(t * P, (t + 1) * P)
                            if t >= 1:
                                pe.wait_ge(rot_done, 2 * t - 1)
                            for c in range(DT):
                                mm = nc.tensor.matmul(psQ[:, 0, :], xT[:, c, rows], Wq[:, c, :], start=(c == 0), stop=(c == DT - 1))
                            mm.then_inc(proj, 1)
                            if t >= 1:
                                pe.wait_ge(rot_done, 2 * t)
                            for c in range(CK):
                                mm = nc.tensor.matmul(psQ[:, 1, :], ctxT[:, c, rows], Wkv[:, c, 0:D], start=(c == 0), stop=(c == CK - 1))
                            mm.then_inc(proj, 1)
                            if t >= 1:
                                pe.wait_ge(v_done, t)
                            for c in range(CK):
                                mm = nc.tensor.matmul(psQ[:, 2, :], ctxT[:, c, rows], Wkv[:, c, D:], start=(c == 0), stop=(c == CK - 1))
                            mm.then_inc(proj, 1)

                        def turn_parts(t):
                            for s in range(2):
                                pe.wait_ge(hi_done, 2 * t + s + 1)
                                pe.wait_ge(lo_done, 2 * t + s + 1)
                                for q in range(4):
                                    i = (2 * t + s) * 4 + q
                                    if i >= 3:
                                        j = i - 3
                                        pe.wait_ge(evac_v if j % 2 else evac_a, j // 2 + 1)
                                    for h in range(8):
                                        mm = nc.tensor.transpose(psP[:, i % 3, h, :], QS[s][:, 8 * q + h, :], ident16[:])
                                    mm.then_inc(parts, 1)

                        for t in range(NT):
                            pe.wait_ge(xn_done, t + 1)
                            if t >= 2:
                                pe.wait_ge(xT_done, t - 1)
                            for c in range(DT):
                                mm = nc.tensor.transpose(psX[:, t % 2, c * P:(c + 1) * P], xn[:, t, c * P:(c + 1) * P], ident[:])
                            mm.then_inc(turned, 1)
                        pe.wait_ge(ctx_in, 16)
                        for t in range(NT + 1):
                            if t < NT:
                                pe.wait_ge(xT_done, t + 1)
                                project(t)
                            if t >= 1:
                                turn_parts(t - 1)

                    @block.scalar
                    def _(act):
                        for t in range(NT):
                            act.wait_ge(turned, t + 1)
                            nc.scalar.activation(xT[:, :, t * P:(t + 1) * P], psX[:, t % 2, :].rearrange("p (c k) -> p c k", c=DT),
                                                 ACT.Copy).then_inc(xT_done, 1)
                        for t in range(NT + 1):
                            for s in range(2):
                                if t >= 1:
                                    for q in (0, 2):
                                        i = (2 * (t - 1) + s) * 4 + q
                                        act.wait_ge(parts, i + 1)
                                        nc.scalar.activation(dst[s][:, 8 * q:8 * q + 8, (t - 1) * P:t * P], psP[:, i % 3], ACT.Copy).then_inc(evac_a, 1)
                                if t < NT:
                                    act.wait_ge(rot_done, 2 * t + s + 1)
                                    if t >= 1:
                                        act.wait_ge(parts, (2 * (t - 1) + s + 1) * 4)
                                    nc.scalar.activation(hi_of[s](QS[s]), rot[:].rearrange("p (h d) -> p h d", h=H).unsqueeze(2).broadcast_to([P, H, 2, HD]),
                                                         ACT.Copy).then_inc(hi_done, 1)
                            if t < NT:
                                act.wait_ge(proj, 3 * t + 3)
                                nc.scalar.activation(V[:, t, :, 0:HD], psQ[:, 2, :].rearrange("p (h d) -> p h d", h=H), ACT.Copy).then_inc(v_done, 1)

                    @block.gpsimd
                    def _(pool):
                        for t in range(NT):
                            for s in range(2):
                                pool.wait_ge(hi_done, 2 * t + s + 1)
                                nc.gpsimd.tensor_tensor(lo_of[s](QS[s]), rot[:].rearrange("p (h d) -> p h d", h=H).unsqueeze(2).broadcast_to([P, H, 2, HD]),
                                                        hi_of[s](QS[s]), ALU.subtract).then_inc(lo_done, 1)

                    @block.vector
                    def _(dve):
                        chain = Tally(dve, own)
                        for t in range(NT):
                            nc.vector.tensor_scalar(xn[:, t, :], X4[:, b, t, :], mv4[:, b, t, 0:1], rstd4[:, b, t, :], ALU.subtract, ALU.mult).then_inc(xn_done, 1)
                        for t in range(NT + 1):
                            for s in range(2):
                                if t < NT:
                                    dve.wait_ge(proj, 3 * t + s + 1)
                                    src = psQ[:, s, :].rearrange("p (h a w) -> p h a w", h=H, w=2)
                                    cos, sin = (table4[:, s, w, b, t, :].unsqueeze(1).unsqueeze(3).broadcast_to([P, H, FQ, 2]) for w in range(2))
                                    chain.mark(nc.vector.tensor_tensor(t_cos[:].rearrange("p (h a w) -> p h a w", h=H, w=2), src, cos, ALU.mult))
                                    chain.link(nc.vector.tensor_tensor(t_sin[:].rearrange("p (h a w) -> p h a w", h=H, w=2), src, sin, ALU.mult))
                                    if 2 * t + s >= 1:
                                        dve.wait_ge(lo_done, 2 * t + s)
                                    c2, s2, r2 = (x[:].rearrange("p (a w) -> p a w", w=2) for x in (t_cos, t_sin, rot))
                                    chain.link(nc.vector.tensor_tensor(r2[:, :, 0], c2[:, :, 0], s2[:, :, 1], ALU.subtract))
                                    nc.vector.tensor_tensor(r2[:, :, 1], s2[:, :, 0], c2[:, :, 1], ALU.add).then_inc(rot_done, 1)
                                    dve.wait_ge(rot_done, 2 * t + s + 1)
                                if t >= 1:
                                    for q in (1, 3):
                                        i = (2 * (t - 1) + s) * 4 + q
                                        dve.wait_ge(parts, i + 1)
                                        nc.vector.tensor_copy(dst[s][:, 8 * q:8 * q + 8, (t - 1) * P:t * P], psP[:, i % 3]).then_inc(evac_v, 1)
                p_.clear()

        def attend(b, ob, run):
            with ExitStack() as ctx2:
                s_ = Space(nc, ctx2, f"soft_{run}")
                NP_ = 4
                Pr = s_.sb("Pr", [P, NP_, 2, S])
                mx = s_.sb("mx", [P, 3, NT, G])
                nm = s_.sb("nm", [P, 3, NT, 2 * G], F16)
                nmT = s_.sb("nmT", [2 * G, 3, S], F16)
                OT = s_.sb("OT", [P, S])
                rec = s_.sb("rec", [P, NT, G])
                psT = s_.ps("psT", [P, 2, 2, S])
                psS = s_.ps("psS", [P, 2, S])
                psO = s_.ps("psO", [P, S])
                psM = s_.ps("psM", [P, S])
                scored, maxed, nm_done, nm_turned, nmT_done, st_done, exp_done, av_done, ot_done, o_turned, o_done, own = (
                    s_.sem(n) for n in ("scored", "maxed", "nm_done", "nm_turned", "nmT_done", "st_done", "exp_done", "av_done", "ot_done", "o_turned", "o_done", "own"))
                rows_in = [s_.sem(f"rows_in{i}") for i in range(3)]
                turned, xT_done, proj, biased, added = (s_.sem(n) for n in ("turned", "xT_done", "proj", "biased", "added"))
                LAG = 2
                CHUNKS = (NT + 1) * DT
                SLOTS = LAG * G * NT
                with nc.Block() as block:
                    @block.tensor
                    def _(pe):
                        def project_out(k):
                            t, c = divmod(k, DT)
                            if t < NT:
                                if c == 0 and t >= 2:
                                    pe.wait_ge(xT_done, t - 1)
                                mm = nc.tensor.transpose(psT[:, 0, t % 2, c * P:(c + 1) * P], heads[:, t, c * P:(c + 1) * P], ident[:])
                                if c == DT - 1:
                                    mm.then_inc(turned, 1)
                            if t >= 1:
                                if c == 0:
                                    pe.wait_ge(xT_done, t)
                                    if t >= 3:
                                        pe.wait_ge(added, t - 2)
                                mm = nc.tensor.matmul(psT[:, 1, (t - 1) % 2, :], xT[:, c, (t - 1) * P:t * P], Wout[:, c, :],
                                                      start=(c == 0), stop=(c == DT - 1))
                                if c == DT - 1:
                                    mm.then_inc(proj, 1)

                        if b is None:
                            for k in range(CHUNKS):
                                project_out(k)
                            return

                        def score(g, j, qt):
                            i = (g * G + j) * NT + qt
                            k = -(-i * CHUNKS // SLOTS)
                            if ob is not None and k < CHUNKS and k * SLOTS // CHUNKS == i:
                                project_out(k)
                            if i >= 2:
                                pe.wait_ge(maxed, i - 1)
                            nc.tensor.matmul(psS[:, i % 2, :], QT[:, g * G + j, qt * P:(qt + 1) * P], KT[:, g * G + j, :],
                                             start=True, stop=True).then_inc(scored, 1)

                        def turn_maxima(g):
                            pe.wait_ge(nm_done, g + 1)
                            if g >= LAG + 1:
                                pe.wait_ge(o_done, g - LAG)
                            elif g >= 1:
                                pe.wait_ge(nmT_done, g)
                            v = psM[:, 0:S // 2].bitcast(F16)
                            for qt in range(NT):
                                mm = nc.tensor.transpose(v[0:2 * G, qt * P:(qt + 1) * P], nm[:, g % 3, qt, :], ident16[:])
                            mm.then_inc(nm_turned, 1)

                        def key_scores(g, kt, pair):
                            i = (g * NT + kt) * 2 + pair
                            if kt == 0 and pair == 0:
                                pe.wait_ge(rows_in[g % 3], 32 * (g // 3 + 1))
                            if ob is not None and i == 0:
                                pe.wait_ge(xT_done, NT)
                            if ob is not None and i == 1:
                                pe.wait_ge(added, NT)
                            if i >= 2:
                                pe.wait_ge(exp_done, i - 1)
                            for w in range(2):
                                h = g * G + 2 * pair + w
                                mm = nc.tensor.matmul(psT[:, i % 2, w, :], KT[:, h, kt * P:(kt + 1) * P], QT[:, h, :], start=True, stop=True)
                            mm.then_inc(st_done, 1)

                        def values(g, kt):
                            i = (g * NT + kt) * 2
                            pe.wait_ge(exp_done, i + 2)
                            if kt == 0 and g >= 1:
                                pe.wait_ge(ot_done, g)
                            for j in range(G):
                                mm = nc.tensor.matmul(psO[32 * j:32 * j + 32, :], V[:, kt, g * G + j, :], Pr[:, (i + j // 2) % NP_, j % 2, :],
                                                      start=(kt == 0), stop=(kt == NT - 1))
                            mm.then_inc(av_done, 1)

                        def turn_results(g):
                            pe.wait_ge(ot_done, g + 1)
                            if g + LAG < NG:
                                pe.wait_ge(nmT_done, g + LAG + 1)
                            else:
                                pe.wait_ge(o_done, g)
                            for qt in range(NT):
                                mm = nc.tensor.transpose(psM[:, qt * P:(qt + 1) * P], OT[:, qt * P:(qt + 1) * P], ident[:])
                            mm.then_inc(o_turned, 1)

                        for g in range(-LAG, NG + 1):
                            ahead, here = g + LAG < NG, 0 <= g < NG
                            for kt in range(NT):
                                if ahead:
                                    score(g + LAG, kt, 0)
                                if here:
                                    key_scores(g, kt, 0)
                                if ahead:
                                    score(g + LAG, kt, 1)
                                if here:
                                    key_scores(g, kt, 1)
                                if ahead:
                                    score(g + LAG, kt, 2)
                                if here and kt >= 1:
                                    values(g, kt - 1)
                                elif g >= 1 and kt == 0:
                                    values(g - 1, NT - 1)
                                if ahead:
                                    score(g + LAG, kt, 3)
                                if kt == 0 and 0 <= g + LAG - 1 < NG:
                                    turn_maxima(g + LAG - 1)
                                if kt == 1 and g >= 1:
                                    turn_results(g - 1)

                    @block.vector
                    def _(dve):
                        chain = Tally(dve, own)

                        def add_projection(t):
                            dve.wait_ge(biased, t + 1)
                            dve.wait_ge(proj, t + 1)
                            nc.vector.tensor_tensor(X4[:, ob, t, :], X4[:, ob, t, :], psT[:, 1, t % 2, :], ALU.add).then_inc(added, 1)

                        if b is None:
                            for t in range(NT):
                                add_projection(t)
                            return

                        def keep_results(g):
                            dve.wait_ge(av_done, NT * (g + 1))
                            if g >= 1:
                                dve.wait_ge(o_turned, g)
                            nc.vector.tensor_copy(OT[:], psO[:]).then_inc(ot_done, 1)

                        def normalise(g):
                            dve.wait_ge(o_turned, g + 1)
                            o = psM[:].rearrange("p (q h d) -> p q h d", q=NT, h=G)
                            chain.link(nc.vector.reciprocal(rec[:], o[:, :, :, HD]))
                            if ob is not None and g == 0:
                                dve.wait_ge(turned, NT)
                            nc.vector.tensor_tensor(heads[:].rearrange("p q (h d) -> p q h d", d=HD)[:, :, G * g:G * g + G, :], o[:, :, :, 0:HD],
                                                    rec[:].unsqueeze(3).broadcast_to([P, NT, G, HD]), ALU.mult).then_inc(o_done, 1)

                        for g in range(-LAG, NG + 1):
                            m = g + LAG
                            for n in range(G * NT):
                                if m < NG:
                                    i = m * G * NT + n
                                    j, qt = i // NT % G, i % NT
                                    dve.wait_ge(scored, i + 1)
                                    nc.vector.tensor_reduce(mx[:, m % 3, qt, j:j + 1], psS[:, i % 2, :], AX.X, ALU.max).then_inc(maxed, 1)
                                if ob is not None:
                                    for t in range(NT):
                                        if m * G * NT + n == min(SLOTS - 1, ((t + 2) * DT - 1) * SLOTS // CHUNKS + 2):
                                            add_projection(t)
                                if g >= 1 and n == 4:
                                    keep_results(g - 1)
                                if g >= 1 and n == 9:
                                    normalise(g - 1)
                            if m < NG:
                                dve.wait_ge(maxed, (m + 1) * G * NT)
                                if m >= 3:
                                    dve.wait_ge(nm_turned, m - 2)
                                chain.link(nc.vector.tensor_scalar(nm[:, m % 3, :, 0:G], mx[:, m % 3], -1.0, None, ALU.mult))
                                nc.vector.scalar_tensor_tensor(out=nm[:, m % 3, :, G:], in0=mx[:, m % 3], scalar=-1.0, in1=nm[:, m % 3, :, 0:G],
                                                               op0=ALU.mult, op1=ALU.subtract).then_inc(nm_done, 1)

                    @block.scalar
                    def _(act):
                        def keep_turned(t):
                            act.wait_ge(turned, t + 1)
                            nc.scalar.activation(xT[:, :, t * P:(t + 1) * P], psT[:, 0, t % 2, :].rearrange("p (c k) -> p c k", c=DT),
                                                 ACT.Copy).then_inc(xT_done, 1)

                        if b is None:
                            for t in range(NT):
                                keep_turned(t)
                            return

                        def send_maxima(g):
                            act.wait_ge(nm_turned, g + 1)
                            if g >= 3:
                                act.wait_ge(rows_in[g % 3], 32 * (g // 3))
                            nc.scalar.activation(nmT[:, g % 3, :], psM[:, 0:S // 2].bitcast(F16)[0:2 * G, :], ACT.Copy).then_inc(nmT_done, 1)

                        for g in range(-LAG, NG):
                            if ob is not None and g < 0:
                                for t in range((g + LAG) * NT // LAG, (g + LAG + 1) * NT // LAG):
                                    keep_turned(t)
                            for n in range(2 * NT):
                                if g >= 0:
                                    i = g * NT * 2 + n
                                    act.wait_ge(st_done, i + 1)
                                    if i >= NP_:
                                        act.wait_ge(av_done, (i - NP_) // 2 + 1)
                                    nc.scalar.activation(Pr[:, i % NP_], psT[:, i % 2], ACT.Exp).then_inc(exp_done, 1)
                                if n == 2 and 0 <= g + LAG - 1 < NG:
                                    send_maxima(g + LAG - 1)

                    @block.gpsimd
                    def _(pool):
                        for t in range(NT if ob is not None else 0):
                            nc.gpsimd.tensor_tensor(X4[:, ob, t, :], X4[:, ob, t, :], bout[:], ALU.add).then_inc(biased, 1)

                    @block.sync
                    def _(sp):
                        for g in range(NG if b is not None else 0):
                            sp.wait_ge(nmT_done, g + 1)
                            for w in range(2):
                                sp.dma_start(QT[HW + w:HW + w + 1, G * g:G * g + G, :], nmT[G * w:G * w + G, g % 3, :]).then_inc(rows_in[g % 3], 16)
                s_.clear()

        project_in(0, "first")
        attend(0, None, "first")
        with nc.Fori(1, B) as b:
            project_in(b, "next")
            attend(b, b - 1, "next")
        attend(None, B - 1, "last")


def stage_mlp(nc, X, ident, ins):
    JT = 11
    INNER = JT * P
    GU = 2 * INNER
    PER = 8
    EPS = 1e-6
    with ExitStack() as ctx:
        m_ = Space(nc, ctx, "mlp")
        sb = m_.sb
        Vgu = sb("Vgu", [P, DT, GU], F16)
        Wd = sb("Wd", [P, JT, D])
        s_gu16 = sb("s_gu16", [P, 2 * JT, DT], F16)
        s_gu = sb("s_gu", [P, 2 * JT, DT])
        shift = sb("shift", [P, 3], I32)
        s_d = sb("s_d", [P, JT, D], F16)
        mv = sb("mv", [P, TILES, 2])
        rstd = sb("rstd", [P, TILES, 1])
        xb = sb("xb", [P, NT, D])
        xh = sb("xh", [P, DT, S], F16)
        xl = sb("xl", [P, DT, S], F16)
        psQ = m_.ps("psQ", [P, DT, S])
        X4 = X[:].rearrange("p (b t) d -> p b t d", t=NT)
        mv4 = mv[:].rearrange("p (b t) k -> p b t k", t=NT)
        rstd4 = rstd[:].rearrange("p (b t) k -> p b t k", t=NT)
        xn_done, turned, xh_done, xl_done = (m_.sem(n) for n in ("xn_done", "turned", "xh_done", "xl_done"))

        def codes(chain, w, t, t2):
            chain.link(nc.vector.tensor_scalar(t, w, shift[:, 1:2], shift[:, 2:3], ALU.logical_shift_left, ALU.logical_shift_right))
            chain.link(nc.vector.tensor_scalar(t2, t, 1 << 12, 3, ALU.bitwise_and, ALU.logical_shift_left))
            return nc.vector.scalar_tensor_tensor(out=t, in0=t, scalar=7 << 9, in1=t2, op0=ALU.bitwise_and, op1=ALU.bitwise_or)

        def normalise(nb):
            for t in range(NT):
                nc.vector.tensor_scalar(xb[:, t, :], X4[:, nb, t, :], mv4[:, nb, t, 0:1], rstd4[:, nb, t, :], ALU.subtract, ALU.mult).then_inc(xn_done, 1)

        def turn(pe):
            for t in range(NT):
                pe.wait_ge(xn_done, t + 1)
                for c in range(DT):
                    mm = nc.tensor.transpose(psQ[:, t, c * P:(c + 1) * P], xb[:, t, c * P:(c + 1) * P], ident[:])
                mm.then_inc(turned, 1)

        def high_parts(act):
            for t in range(NT):
                act.wait_ge(turned, t + 1)
                nc.scalar.activation(xh[:, :, t * P:(t + 1) * P], psQ[:, t, :].rearrange("p (c k) -> p c k", c=DT), ACT.Copy).then_inc(xh_done, 1)

        def low_parts(dve):
            for t in range(NT):
                dve.wait_ge(xh_done, t + 1)
                cols = slice(t * P, (t + 1) * P)
                nc.vector.tensor_tensor(xl[:, :, cols], psQ[:, t, :].rearrange("p (c k) -> p c k", c=DT), xh[:, :, cols],
                                        ALU.subtract).then_inc(xl_done, 1)

        with ExitStack() as ctx2:
            d_ = Space(nc, ctx2, "deq")
            words = d_.sb("words", [P, DT, GU], I32)
            stats = d_.sb("stats", [P, TILES, 6])
            t1 = [d_.sb(f"t1{i}", [P, GU], I32) for i in range(2)]
            t2 = d_.sb("t2", [P, GU], I32)
            consts, own, vals, freed = d_.sem("consts"), d_.sem("own"), d_.sem("vals"), d_.sem("freed")
            chunk_in = [d_.sem(f"chunk_in{i}") for i in range(DT)]
            down_in, scales_in, stat_own, mv_done, rooted = (d_.sem(n) for n in ("down_in", "scales_in", "stat_own", "mv_done", "rooted"))
            with nc.Block() as block:
                @block.sync
                def _(sp):
                    for g in range(DT):
                        for k in range(PER):
                            sp.dma_start(words[k:P:PER, g, :], ins["gate_upT"][g * 16:(g + 1) * 16, :]).then_inc(chunk_in[g], 16)

                @block.scalar
                def _(act):
                    for k in range(PER):
                        act.dma_start(Wd[k:P:PER].bitcast(I32), ins["downT"].rearrange("(g j) o -> j g o", j=P // PER)).then_inc(down_in, 16)
                    act.dma_start(s_d[:].rearrange("p g o -> p (g o)"), ins["down_scales"].rearrange("g o -> (g o)").partition_broadcast(P)).then_inc(down_in, 16)
                    act.dma_start(s_gu16[:], ins["gate_up_scalesT"].rearrange("(j p) g -> p j g", p=P)).then_inc(scales_in, 16)
                    act.wait_ge(mv_done, 1)
                    nc.scalar.activation(rstd[:], mv[:, :, 1:2], ACT.Sqrt).then_inc(rooted, 1)
                    high_parts(act)
                    for g in range(DT):
                        act.wait_ge(vals, g + 1)
                        half = t1[g % 2][:].bitcast(F16).rearrange("p (o w) -> p o w", w=2)[:, :, 0]
                        nc.scalar.activation(Vgu[:, g, :], half, ACT.Copy, scale=2.0 ** 14).then_inc(freed, 1)

                @block.tensor
                def _(pe):
                    turn(pe)

                @block.gpsimd
                def _(pool):
                    nc.gpsimd.iota(shift[:, 0:1], [[0, 1]], base=0, channel_multiplier=4).then_inc(consts, 1)

                @block.vector
                def _(dve):
                    chain = Tally(dve, own)
                    dve.wait_ge(consts, 1)
                    chain.link(nc.vector.tensor_scalar(shift[:, 0:1], shift[:, 0:1], 4 * PER - 1, None, ALU.bitwise_and))
                    chain.mark(nc.vector.tensor_scalar(shift[:, 2:3], shift[:, 0:1], -9, 0, ALU.add, ALU.max))
                    chain.link(nc.vector.tensor_scalar(shift[:, 1:2], shift[:, 0:1], -9, 0, ALU.add, ALU.min))
                    chain.mark(nc.vector.tensor_scalar(shift[:, 1:2], shift[:, 1:2], -1, None, ALU.mult))
                    layernorm_stats(nc, dve, Tally(dve, stat_own), [X[:, t, :] for t in range(TILES)], stats, mv)
                    nc.vector.tensor_scalar(mv[:, :, 1:2], mv[:, :, 1:2], LN_EPS, None, ALU.add).then_inc(mv_done, 1)
                    dve.wait_ge(rooted, 1)
                    chain.link(nc.vector.reciprocal(rstd[:], rstd[:]))
                    normalise(0)
                    low_parts(dve)

                    for g in range(DT):
                        dve.wait_ge(chunk_in[g], 16 * PER)
                        if g >= 2:
                            dve.wait_ge(freed, g - 1)
                        codes(chain, words[:, g, :], t1[g % 2][:], t2[:]).then_inc(vals, 1)
                    dve.wait_ge(scales_in, 16)
                    chain.mark(nc.vector.tensor_copy(s_gu[:], s_gu16[:]))
                    dve.wait_ge(down_in, 16 * (PER + 1))
            d_.clear()
            m_.clear()

        first = sb("first", [P, 2, S])
        third = sb("third", [P, 2, S])
        both = sb("both", [P, 2, S])
        sg = sb("sg", [P, 2, S])
        hT = sb("hT", [P, 3, S])
        sq = sb("sq", [P, D])
        td = [sb(f"td{i}", [P, D], I32) for i in range(2)]
        ss = sb("ss", [P, NT])
        psD = m_.ps("psD", [P, NT, D])
        grp, ev_a, ev_v, summed, silu_done, h_done, down = (
            m_.sem(n) for n in ("grp", "ev_a", "ev_v", "summed",
                                "silu_done", "h_done", "down"))
        wd_done = m_.sem("wd_done")
        squared, ms_done, root2, added, own = (m_.sem(n) for n in ("squared", "ms_done", "root2", "added", "own"))
        def run(b, nb, pb):
            first_batch = b is not None and pb is None
            with nc.Block() as block:
                @block.vector
                def _(dve):
                    chain = Tally(dve, own)
                    def mean_squares():
                        dve.wait_ge(squared, NT)
                        nc.vector.tensor_scalar(ss[:], ss[:], 1.0 / D, EPS, ALU.mult, ALU.add).then_inc(ms_done, 1)

                    def add_results():
                        dve.wait_ge(root2, 1)
                        chain.link(nc.vector.reciprocal(ss[:], ss[:]))
                        for t in range(NT):
                            nc.vector.scalar_tensor_tensor(out=X4[:, pb, t, :], in0=psD[:, t, :], scalar=ss[:, t:t + 1], in1=X4[:, pb, t, :],
                                                           op0=ALU.mult, op1=ALU.add).then_inc(added, 1)

                    if b is None:
                        mean_squares()
                        add_results()
                        return

                    def gated(j):
                        dve.wait_ge(silu_done, j + 1)
                        dve.wait_ge(summed, 2 * j + 2)
                        if j >= 3:
                            dve.wait_ge(down, j - 2)
                        nc.vector.tensor_tensor(hT[:, j % 3, :], sg[:, j % 2, :], both[:, 1, :], ALU.mult).then_inc(h_done, 1)

                    for u in range(2 * JT):
                        if u == JT and nb is not None:
                            normalise(nb)
                        j, w = divmod(u, 2)
                        if first_batch and w == 0:
                            chain.link(codes(chain, Wd[:, j, :].bitcast(I32), td[0][:], td[1][:]))
                            half = td[0][:].bitcast(F16).rearrange("p (o w) -> p o w", w=2)[:, :, 0]
                            nc.vector.scalar_tensor_tensor(out=Wd[:, j, :], in0=half, scalar=2.0 ** 14, in1=s_d[:, j, :],
                                                           op0=ALU.mult, op1=ALU.mult).then_inc(wd_done, 1)
                        row = w * JT + j
                        for n, g in enumerate((1, 3)):
                            dve.wait_ge(grp, DT * u + g + 1)
                            if n == 0:
                                dve.wait_ge(ev_a, 2 * u + 1)
                            else:
                                dve.wait_ge(ev_v, 2 * u + 1)
                            nc.vector.scalar_tensor_tensor(out=first[:, w, :], in0=psQ[:, g, :], scalar=s_gu[:, row, g:g + 1], in1=first[:, w, :],
                                                           op0=ALU.mult, op1=ALU.add).then_inc(ev_v, 1)
                        if pb is not None and u == 1:
                            mean_squares()
                        if pb is not None and u == 2:
                            add_results()
                        if w == 0 and j >= 1:
                            gated(j - 1)
                    gated(JT - 1)
                    if nb is not None:
                        low_parts(dve)

                @block.scalar
                def _(act):
                    def square(t):
                        if t >= 1:
                            act.wait_ge(squared, t)
                        nc.scalar.activation(sq[:], psD[:, t, :], ACT.Square, accum_out=ss[:, t:t + 1]).then_inc(squared, 1)

                    def root():
                        act.wait_ge(ms_done, 1)
                        nc.scalar.activation(ss[:], ss[:], ACT.Sqrt).then_inc(root2, 1)

                    if b is None:
                        for t in range(NT):
                            square(t)
                        root()
                        return

                    for u in range(2 * JT):
                        j, w = divmod(u, 2)
                        row = w * JT + j
                        for g, dst in ((0, first), (2, third)):
                            act.wait_ge(grp, DT * u + g + 1)
                            if g == 0 and u >= 2:
                                act.wait_ge(summed, u - 1)
                            nc.scalar.activation(dst[:, w, :], psQ[:, g, :], ACT.Copy, scale=s_gu[:, row, g:g + 1]).then_inc(ev_a, 1)
                        if pb is not None and u < 2:
                            square(2 * u)
                            square(2 * u + 1)
                        if pb is not None and u == 2:
                            root()
                        if w == 1:
                            act.wait_ge(summed, 2 * j + 1)
                            if j >= 2:
                                act.wait_ge(h_done, j - 1)
                            nc.scalar.activation(sg[:, j % 2, :], both[:, 0, :], ACT.Silu).then_inc(silu_done, 1)
                    if nb is not None:
                        high_parts(act)

                @block.gpsimd
                def _(pool):
                    for u in range(2 * JT if b is not None else 0):
                        j, w = divmod(u, 2)
                        pool.wait_ge(ev_a, 2 * u + 2)
                        pool.wait_ge(ev_v, 2 * u + 2)
                        if j >= 1:
                            pool.wait_ge(h_done if w else silu_done, j)
                        nc.gpsimd.tensor_tensor(both[:, w, :], first[:, w, :], third[:, w, :], ALU.add).then_inc(summed, 1)

                @block.tensor
                def _(pe):
                    for j in range(JT + 1 if b is not None else 0):
                        for w in range(2 if j < JT else 0):
                            u = 2 * j + w
                            cols = slice(w * INNER + j * P, w * INNER + (j + 1) * P)
                            for g in range(DT):
                                if u >= 1:
                                    pe.wait_ge(ev_v if g % 2 else ev_a, 2 * (u - 1) + g // 2 + 1)
                                nc.tensor.matmul(psQ[:, g, :], Vgu[:, g, cols], xh[:, g, :], start=True, stop=False)
                                nc.tensor.matmul(psQ[:, g, :], Vgu[:, g, cols], xl[:, g, :], start=False, stop=True).then_inc(grp, 1)
                        if j == JT and nb is not None:
                            pe.wait_ge(ev_a, 4 * JT)
                            pe.wait_ge(ev_v, 4 * JT)
                            turn(pe)
                        if j >= 1:
                            i = j - 1
                            pe.wait_ge(h_done, i + 1)
                            if first_batch:
                                pe.wait_ge(wd_done, i + 1)
                            if i == 0 and pb is not None:
                                pe.wait_ge(added, NT)
                            for t in range(NT):
                                mm = nc.tensor.matmul(psD[:, t, :], hT[:, i % 3, t * P:(t + 1) * P], Wd[:, i, :], start=(i == 0), stop=(i == JT - 1))
                            if i < JT - 1:
                                mm.then_inc(down, 1)
            m_.clear()

        run(0, 1, None)
        with nc.Fori(1, B - 1) as b:
            run(b, b + 1, b - 1)
        run(B - 1, None, B - 2)
        run(None, None, B - 1)


LAYOUT = {
    "x": ("x", None),
    "ctxT": ("ctx_1024", (0, 2, 1)),
    "pos": ("fside_BxSx2_0", None),
    "in_proj_wT": ("L0_xattn_in_proj_w", (1, 0)),
    "x_proj_wT": ("L0_xattn_x_proj_w", (1, 0)),
    "dt_proj_wT": ("L0_xattn_dt_proj_w", (1, 0)),
    "A_log": ("L0_xattn_A_log", None),
    "ternaryT": ("L0_ffn_weight", (1, 0)),
    "out_scale": ("L0_ffn_scale", None),
    "masksT": ("L0_ffn_expert_masks", (0, 2, 1)),
    "routerT": ("L0_ffn_router_w", (1, 0)),
    "Wq": ("L1_xattn_Wq", None),
    "Wkv": ("L1_xattn_Wkv", None),
    "Wout": ("L1_xattn_Wout", None),
    "bout": ("L1_xattn_bout", None),
    "gate_upT": ("L1_ffn_gate_up_packed", (1, 0)),
    "gate_up_scalesT": ("L1_ffn_gate_up_scales", (1, 0)),
    "downT": ("L1_ffn_down_packed", (1, 0)),
    "down_scales": ("L1_ffn_down_scales", None),
}


CHANNELS = ("L0_xattn_conv_w", "L0_xattn_conv_b", "L0_xattn_dt_proj_b", "L0_xattn_D")


def layouts(inputs):
    import numpy as np

    arrays = {}
    for name, (source, axes) in LAYOUT.items():
        a = np.asarray(inputs[source])
        arrays[name] = np.ascontiguousarray(a if axes is None else a.transpose(axes))
    columns = [np.asarray(inputs[c]) for c in CHANNELS]
    arrays["channels"] = np.concatenate([c if c.ndim == 2 else c[:, None] for c in columns], axis=1)
    return arrays


def program(nc, ins, out):
    with ExitStack() as ctx:
        X = ctx.enter_context(nc.sbuf_tensor("X", [P, TILES, D], F32))
        ident = ctx.enter_context(nc.sbuf_tensor("ident", [P, P], F32))
        ident16 = ctx.enter_context(nc.sbuf_tensor("ident16", [P, P], F16))
        id_done = [ctx.enter_context(nc.semaphore(f"id_done{i}")) for i in range(2)]
        stored = ctx.enter_context(nc.semaphore("stored"))
        bc_rows = nc.dram_tensor("bc_rows", (B, 32, S), F32).ap()
        sorted_rows = nc.dram_tensor("sorted_rows", (B * S, D + 2), F32).ap()
        sorted_results = nc.dram_tensor("sorted_results", (B * S, D), F32).ap()
        make_identity(nc, (ident, ident16), id_done)
        stage_ssm(nc, X, ident, bc_rows, ins)
        stage_experts(nc, X, ident, ident16, (sorted_rows, sorted_results), ins)
        stage_attention(nc, X, ident, ident16, ins)
        stage_mlp(nc, X, ident, ins)
        with nc.Block() as block:
            @block.sync
            def _(sp):
                sp.dma_start(out.rearrange("b (t p) d -> p (b t) d", p=P), X[:]).then_inc(stored, 16)
                sp.wait_ge(stored, 16)


def kernel(**inputs):
    import numpy as np
    import concourse.bacc as bacc
    from concourse.bass_utils import run_bass_kernel_spmd

    nc = bacc.Bacc("TRN2", target_bir_lowering=False, num_devices=1)
    arrays = {f"in_{name}": a for name, a in layouts(inputs).items()}
    ins = {name[3:]: nc.dram_tensor(name, a.shape, mybir.dt.from_np(a.dtype), kind="ExternalInput").ap() for name, a in arrays.items()}
    out = nc.dram_tensor("out_x", (B, S, D), F32, kind="ExternalOutput").ap()
    program(nc, ins, out)
    return run_bass_kernel_spmd(nc, [arrays], core_ids=[0]).results[0]["out_x"]
```
